# Optimizing a Trainium2 kernel written in Bass

```python
import numpy as np
import jax
import jax.numpy as jnp

def _softmax(x, axis=-1):
    return jax.nn.softmax(x, axis=axis)

def _gelu(x):
    return jax.nn.gelu(x, approximate=True)

def _silu(x):
    return jax.nn.silu(x)

def _sigmoid(x):
    return jax.nn.sigmoid(x)

def _layernorm(x, axis=-1, eps=1e-05):
    m = jnp.mean(x, axis=axis, keepdims=True)
    v = jnp.var(x, axis=axis, keepdims=True)
    return (x - m) / jnp.sqrt(v + eps)

def _scatter_add(tgt, idx, src, axis=0):
    return tgt.at[idx].add(src)

def _segment_sum(src, seg, n):
    return jax.ops.segment_sum(src, seg, n)
kernel_name = 'mk_prb_d2_jaxref_r8_a6a3e3'

def setup_inputs(seed: int=0):
    np.random.seed(seed)
    _w = jnp.asarray

    def _L0_attn_setup():
        import jax, jax.numpy as jnp
        import numpy as np
        N_STATE = 64
        SEQ_L = 512
        BATCH, HCH = (16, 64)
        DT_MIN, DT_MAX = (0.001, 0.1)

        def _make_DPLR_HiPPO(N):
            P = np.sqrt(1 + 2 * np.arange(N))
            A = P[:, None] * P[None, :]
            A = np.tril(A) - np.diag(np.arange(N))
            nhippo = -A
            p = 0.5 * np.sqrt(2 * np.arange(1, N + 1) + 1.0)
            q = 2 * p
            S = nhippo + p[:, None] * q[None, :]
            Lambda, V = np.linalg.eig(S)
            Vc = V.conj().T
            p_t = Vc @ p
            q_t = Vc @ q.conj()
            return (Lambda, p_t, q_t, Vc)

        def _ri(z):
            return np.stack([z.real, z.imag], axis=-1).astype(np.float32)

        def _cplx(x_ri):
            return x_ri[..., 0] + 1j * x_ri[..., 1]

        def _s4_kernel(Lambda, p, q, B, Ct, step, L):
            Omega = jnp.exp(-2j * jnp.pi * (jnp.arange(L) / L))
            g = 2.0 / step * ((1.0 - Omega) / (1.0 + Omega))
            c = 2.0 / (1.0 + Omega)
            denom = g[:, None] - Lambda[None, :]
            cauchy = lambda v: (v[None, :] / denom).sum(-1)
            k00 = cauchy(Ct.conj() * B)
            k01 = cauchy(Ct.conj() * p)
            k10 = cauchy(q.conj() * B)
            k11 = cauchy(q.conj() * p)
            at_roots = c * (k00 - k01 * (1.0 / (1.0 + k11)) * k10)
            return jnp.fft.ifft(at_roots, L).real
        key = jax.random.key(seed)
        k_u, k_ct, k_b, k_d, k_ls = jax.random.split(key, 5)
        Lambda, p, q, Vc = _make_DPLR_HiPPO(N_STATE)
        u = jax.random.normal(k_u, (BATCH, HCH, SEQ_L), dtype=jnp.float32)
        Ct_ri = jax.random.normal(k_ct, (1, N_STATE, 2), dtype=jnp.float32) / np.sqrt(N_STATE)
        Bp = jax.random.normal(k_b, (N_STATE, 1), dtype=jnp.float32) / np.sqrt(N_STATE)
        D = jax.random.uniform(k_d, (1,), dtype=jnp.float32)
        log_step = jax.random.uniform(k_ls, (1,), dtype=jnp.float32, minval=np.log(DT_MIN), maxval=np.log(DT_MAX))
        return {'u': u, 'Lambda_ri': jnp.asarray(_ri(Lambda)), 'p_ri': jnp.asarray(_ri(p)), 'q_ri': jnp.asarray(_ri(q)), 'Vc_ri': jnp.asarray(_ri(Vc)), 'Ct_ri': Ct_ri, 'Bp': Bp, 'D': D, 'log_step': log_step}
    _L0_attn_in = _L0_attn_setup()

    def _L0_ffn_setup():
        import jax, jax.numpy as jnp
        import numpy as np
        D_MODEL = 512
        D_FF = 1376
        key = jax.random.key(seed)
        k1, k2, k3, k4 = jax.random.split(key, 4)
        x = jax.random.normal(k1, (2, 256, D_MODEL), dtype=jnp.float32)
        W_gate = jax.random.normal(k2, (D_FF, D_MODEL), dtype=jnp.float32) * D_MODEL ** (-0.5)
        W_up = jax.random.normal(k3, (D_FF, D_MODEL), dtype=jnp.float32) * D_MODEL ** (-0.5)
        W_down = jax.random.normal(k4, (D_MODEL, D_FF), dtype=jnp.float32) * D_FF ** (-0.5)
        return {'x': x, 'W_gate': W_gate, 'W_up': W_up, 'W_down': W_down}
    _L0_ffn_in = _L0_ffn_setup()

    def _L1_attn_setup():
        import jax, jax.numpy as jnp
        import numpy as np
        H = 32
        DN = 128
        DR = 64
        DV = 128
        DQ = DN + DR
        HID = 512
        NEG_INF = -1e+30
        key = jax.random.key(seed)
        k0, k1, k2, k3 = jax.random.split(key, 4)
        B, S = (4, 128)
        hidden_states = jax.random.normal(k0, (B, S, HID), dtype=jnp.float32)
        wq = jax.random.normal(k1, (HID, H * DQ), dtype=jnp.float32) * 0.02
        wkv = jax.random.normal(k2, (HID, H * (DN + DV) + DR), dtype=jnp.float32) * 0.02
        wo = jax.random.normal(k3, (H * DV, HID), dtype=jnp.float32) * 0.02
        return {'hidden_states': hidden_states, 'wq': wq, 'wkv': wkv, 'wo': wo}
    _L1_attn_in = _L1_attn_setup()

    def _L1_ffn_setup():
        import jax, jax.numpy as jnp
        import numpy as np
        B, S, D, O, E, R = (4, 256, 512, 512, 8, 16)
        SCALING = 32.0 / 16.0
        MAX_THRESHOLD = 0.125
        key = jax.random.key(seed)
        ks = jax.random.split(key, 8)
        return {'x': jax.random.normal(ks[0], (B, S, D), jnp.float32), 'W_base': jax.random.normal(ks[1], (O, D), jnp.float32) * (1.0 / np.sqrt(D)), 'b_base': jax.random.normal(ks[2], (O,), jnp.float32) * 0.02, 'W_gate': jax.random.normal(ks[3], (E, D), jnp.float32) * (1.0 / np.sqrt(D)), 'W_thr': jax.random.normal(ks[4], (D,), jnp.float32) * (1.0 / np.sqrt(D)), 'b_thr': jax.random.normal(ks[5], (1,), jnp.float32) * 0.02, 'A_w': jax.random.normal(ks[6], (E, R, D), jnp.float32) * (1.0 / np.sqrt(D)), 'B_w': jax.random.normal(ks[7], (E, O, R), jnp.float32) * (1.0 / np.sqrt(R))}
    _L1_ffn_in = _L1_ffn_setup()
    _d = {'L0_attn_u': _L0_attn_in['u'], 'L0_attn_Lambda_ri': _L0_attn_in['Lambda_ri'], 'L0_attn_p_ri': _L0_attn_in['p_ri'], 'L0_attn_q_ri': _L0_attn_in['q_ri'], 'L0_attn_Vc_ri': _L0_attn_in['Vc_ri'], 'L0_attn_Ct_ri': _L0_attn_in['Ct_ri'], 'L0_attn_Bp': _L0_attn_in['Bp'], 'L0_attn_D': _L0_attn_in['D'], 'L0_attn_log_step': _L0_attn_in['log_step'], 'L0_ffn_W_gate': _L0_ffn_in['W_gate'], 'L0_ffn_W_up': _L0_ffn_in['W_up'], 'L0_ffn_W_down': _L0_ffn_in['W_down'], 'L1_attn_wq': _L1_attn_in['wq'], 'L1_attn_wkv': _L1_attn_in['wkv'], 'L1_attn_wo': _L1_attn_in['wo'], 'L1_ffn_W_base': _L1_ffn_in['W_base'], 'L1_ffn_b_base': _L1_ffn_in['b_base'], 'L1_ffn_W_gate': _L1_ffn_in['W_gate'], 'L1_ffn_W_thr': _L1_ffn_in['W_thr'], 'L1_ffn_b_thr': _L1_ffn_in['b_thr'], 'L1_ffn_A_w': _L1_ffn_in['A_w'], 'L1_ffn_B_w': _L1_ffn_in['B_w']}
    _x0 = _d['L0_attn_u']
    _d['L0_attn_u'] = jax.random.normal(jax.random.fold_in(jax.random.key(seed), 1), (4, 256, 512), dtype=_x0.dtype)
    del _x0
    return _d

def reference(L0_attn_u, L0_attn_Lambda_ri, L0_attn_p_ri, L0_attn_q_ri, L0_attn_Vc_ri, L0_attn_Ct_ri, L0_attn_Bp, L0_attn_D, L0_attn_log_step, L0_ffn_W_gate, L0_ffn_W_up, L0_ffn_W_down, L1_attn_wq, L1_attn_wkv, L1_attn_wo, L1_ffn_W_base, L1_ffn_b_base, L1_ffn_W_gate, L1_ffn_W_thr, L1_ffn_b_thr, L1_ffn_A_w, L1_ffn_B_w):

    def _L0_attn_ref(u, Lambda_ri, p_ri, q_ri, Vc_ri, Ct_ri, Bp, D, log_step):
        import jax, jax.numpy as jnp
        import numpy as np
        N_STATE = 64
        SEQ_L = 512
        BATCH, HCH = (16, 64)
        DT_MIN, DT_MAX = (0.001, 0.1)

        def _make_DPLR_HiPPO(N):
            P = np.sqrt(1 + 2 * np.arange(N))
            A = P[:, None] * P[None, :]
            A = np.tril(A) - np.diag(np.arange(N))
            nhippo = -A
            p = 0.5 * np.sqrt(2 * np.arange(1, N + 1) + 1.0)
            q = 2 * p
            S = nhippo + p[:, None] * q[None, :]
            Lambda, V = np.linalg.eig(S)
            Vc = V.conj().T
            p_t = Vc @ p
            q_t = Vc @ q.conj()
            return (Lambda, p_t, q_t, Vc)

        def _ri(z):
            return np.stack([z.real, z.imag], axis=-1).astype(np.float32)

        def _cplx(x_ri):
            return x_ri[..., 0] + 1j * x_ri[..., 1]

        def _s4_kernel(Lambda, p, q, B, Ct, step, L):
            Omega = jnp.exp(-2j * jnp.pi * (jnp.arange(L) / L))
            g = 2.0 / step * ((1.0 - Omega) / (1.0 + Omega))
            c = 2.0 / (1.0 + Omega)
            denom = g[:, None] - Lambda[None, :]
            cauchy = lambda v: (v[None, :] / denom).sum(-1)
            k00 = cauchy(Ct.conj() * B)
            k01 = cauchy(Ct.conj() * p)
            k10 = cauchy(q.conj() * B)
            k11 = cauchy(q.conj() * p)
            at_roots = c * (k00 - k01 * (1.0 / (1.0 + k11)) * k10)
            return jnp.fft.ifft(at_roots, L).real
        L = u.shape[-1]
        Lambda = _cplx(Lambda_ri)
        p = _cplx(p_ri)
        q = _cplx(q_ri)
        Vc = _cplx(Vc_ri)
        Ct = _cplx(Ct_ri).reshape(-1)
        B = (Vc @ Bp.astype(Vc.dtype)).reshape(-1)
        step = jnp.exp(log_step)[0]
        K = _s4_kernel(Lambda, p, q, B, Ct, step, L).astype(u.dtype)
        n = 2 * L
        y = jnp.fft.irfft(jnp.fft.rfft(u, n=n) * jnp.fft.rfft(K, n=n), n=n)[..., :L]
        return y + D[0] * u

    def _L0_ffn_ref(x, W_gate, W_up, W_down):
        import jax, jax.numpy as jnp
        import numpy as np
        D_MODEL = 512
        D_FF = 1376
        out_shape = x.shape[:-1] + (W_down.shape[0],)
        xf = x.reshape(-1, x.shape[-1])
        up = jnp.einsum('td,fd->tf', xf, W_up)
        gate = jax.nn.silu(jnp.einsum('td,fd->tf', xf, W_gate))
        h = gate * up
        y = jnp.einsum('tf,df->td', h, W_down)
        return y.reshape(out_shape)

    def _L1_attn_ref(hidden_states, wq, wkv, wo):
        import jax, jax.numpy as jnp
        import numpy as np
        H = 32
        DN = 128
        DR = 64
        DV = 128
        DQ = DN + DR
        HID = 512
        NEG_INF = -1e+30
        B, S, D = hidden_states.shape
        q = jnp.einsum('bsd,de->bse', hidden_states, wq).reshape(B, S, H, DQ)
        kv = jnp.einsum('bsd,de->bse', hidden_states, wkv)
        k = kv[..., :H * DN].reshape(B, S, H, DN)
        v = kv[..., H * DN:H * (DN + DV)].reshape(B, S, H, DV)
        scale = DQ ** (-0.5)
        scores = jnp.einsum('bqhd,bkhd->bhqk', q[..., :DN], k) * scale
        causal = jnp.tril(jnp.ones((S, S), dtype=bool))
        scores = jnp.where(causal[None, None], scores, NEG_INF)
        probs = jax.nn.softmax(scores, axis=-1)
        attn = jnp.einsum('bhqk,bkhd->bqhd', probs, v).reshape(B, S, H * DV)
        return jnp.einsum('bse,ed->bsd', attn, wo)

    def _L1_ffn_ref(x, W_base, b_base, W_gate, W_thr, b_thr, A_w, B_w):
        import jax, jax.numpy as jnp
        import numpy as np
        B, S, D, O, E, R = (4, 256, 512, 512, 8, 16)
        SCALING = 32.0 / 16.0
        MAX_THRESHOLD = 0.125
        base = jnp.einsum('bsd,od->bso', x, W_base) + b_base
        xf = x.reshape(-1, D)
        gate = jax.nn.softmax(xf @ W_gate.T, axis=-1)
        thr = jax.nn.sigmoid(xf @ W_thr + b_thr[0]) * MAX_THRESHOLD
        adapted = gate - thr[:, None]
        selected = (adapted >= 0).astype(x.dtype)
        w = adapted * selected
        wsum = jnp.sum(w, axis=-1, keepdims=True)
        wsum = jnp.where(wsum == 0, jnp.ones_like(wsum), wsum)
        w = w / wsum
        h = jnp.einsum('nd,erd->ner', xf, A_w)
        moe = jnp.einsum('ner,ne,eor->no', h, w, B_w) * SCALING
        return base + moe.reshape(base.shape)
    x = L0_attn_u
    xn = _layernorm(x, axis=-1)
    x = x + _L0_attn_ref(xn, L0_attn_Lambda_ri, L0_attn_p_ri, L0_attn_q_ri, L0_attn_Vc_ri, L0_attn_Ct_ri, L0_attn_Bp, L0_attn_D, L0_attn_log_step) + _L0_ffn_ref(xn, L0_ffn_W_gate, L0_ffn_W_up, L0_ffn_W_down)
    xn = _layernorm(x, axis=-1)
    x = x + _L1_attn_ref(xn, L1_attn_wq, L1_attn_wkv, L1_attn_wo) + _L1_ffn_ref(xn, L1_ffn_W_base, L1_ffn_b_base, L1_ffn_W_gate, L1_ffn_W_thr, L1_ffn_b_thr, L1_ffn_A_w, L1_ffn_B_w)
    return x

_drawn_inputs = setup_inputs


def setup_inputs(seed=0):
    import zlib

    import numpy as np

    out = dict(_drawn_inputs(seed))
    spreads = {}
    factors = {'L0_attn_Lambda_ri': 8.0,
     'L0_attn_p_ri': 8.0,
     'L0_attn_q_ri': 8.0,
     'L0_attn_Vc_ri': 8.0,
     'L0_attn_Ct_ri': 8.0,
     'L0_attn_Bp': 8.0,
     'L1_attn_wq': 8.0,
     'L1_ffn_b_base': 6.463}
    for name, (base, spread) in spreads.items():
        noise = np.random.default_rng([zlib.crc32(name.encode()), seed]).standard_normal(out[name].shape)
        drawn = base * np.exp(spread * noise) if base else spread * noise
        out[name] = jnp.asarray(drawn.astype(out[name].dtype))
    for name, factor in factors.items():
        out[name] = (out[name] * factor).astype(out[name].dtype)
    return out
```

```python
from contextlib import ExitStack

import concourse.bass as bass
from concourse import mybir

P = 128
F32 = mybir.dt.float32
F32R = mybir.dt.float32r
ALU = mybir.AluOpType
ACT = mybir.ActivationFunctionType
AX_X = mybir.AxisListType.X

BATCH, SEQ, DM = 4, 256, 512
TOK = BATCH * SEQ
NT = TOK // P
KD = DM // P
HALF = TOK // 2
TH = NT // 2
FF = 1376
NF = (FF + P - 1) // P
NS = 64
HEADS, DH = 32, 128
QK_SCALE = float(192) ** -0.5
GH = 4
NG = HEADS // GH
PAIRS = GH * BATCH
NE, RANK = 8, 16
ER = NE * RANK
WC = DM + ER + NE + 2
CUT = 384
EPS = 1e-5
NEG = -1e30
MAX_THRESHOLD, SCALING = 0.125, 2.0

GROUP = [("Q", 0, 0), ("K", 0, 0), ("V", 0),
         ("S", 0), ("V", 1), ("Q", 0, 1), ("K", 0, 1),
         ("S", 1), ("T", 0), ("V", 2), ("O", 0),
         ("S", 2), ("T", 1), ("V", 3), ("V", 4), ("Q", 1, 0), ("O", 1),
         ("S", 3), ("T", 2), ("V", 5), ("V", 6), ("K", 1, 0), ("O", 2),
         ("S", 4), ("T", 3), ("V", 7), ("Q", 1, 1), ("O", 3),
         ("S", 5), ("T", 4), ("K", 1, 1), ("O", 4)]
for _h in (2, 3):
    _p = 4 * _h - 2
    GROUP += [("S", _p), ("T", _p - 1), ("Q", _h, 0), ("O", _p - 1),
              ("S", _p + 1), ("T", _p), ("K", _h, 0), ("O", _p),
              ("S", _p + 2), ("T", _p + 1), ("Q", _h, 1), ("O", _p + 1),
              ("S", _p + 3), ("T", _p + 2), ("K", _h, 1), ("O", _p + 2)]
GROUP += [("S", 14), ("T", 13), ("O", 13),
          ("S", 15), ("T", 14), ("W", 0), ("O", 14), ("W", 1), ("T", 15), ("W", 2), ("O", 15),
          ("W", 3), ("W", 4), ("W", 5), ("W", 6), ("W", 7)]
UNITS = [s for s in GROUP if s[0] in "QKVW"]
NU = len(UNITS)
GBANKS = 4
SPLITS = [("q", 0), ("k", 0), ("v", 0), ("v", 1), ("v", 2), ("v", 3), ("N", 0), ("q", 1), ("N", 1), ("k", 1),
          ("N", 2), ("o", 0), ("N", 3), ("o", 1), ("N", 4), ("q", 2), ("N", 5), ("k", 2),
          ("N", 6), ("o", 2), ("N", 7), ("o", 3), ("N", 8), ("q", 3), ("N", 9), ("k", 3)]
SPLITS += [("N", p) for p in range(10, PAIRS)]
NQK = 2 * GH
NVO = KD + GH
RING = 2


def matmul3(nc, out, w_hi, w_lo, x_hi, x_lo, first, last):
    nc.tensor.matmul(out, w_hi, x_hi, start=first, stop=False)
    nc.tensor.matmul(out, w_hi, x_lo, start=False, stop=False)
    return nc.tensor.matmul(out, w_lo, x_hi, start=False, stop=last)


def as_f32(ap):
    return ap.bitcast(F32)


def layer0(nc, shared, ins):
    acc, xT_hi, xT_lo, ident, ident_dram, banks = shared
    (x, w_gu, w_down, lam, p_ri, q_ri, ct, vc, bp, d_skip, log_step, om_rows, om_cols, tables,
     w_comb, b_base, b_thr, w_expb) = ins
    G, D = 0, 4

    with ExitStack() as ctx:
        def sb(name, shape, dt=F32):
            return ctx.enter_context(nc.sbuf_tensor(name, shape, dt))

        def sem(name):
            return ctx.enter_context(nc.semaphore(name))

        hT_hi, hT_lo = (sb(f"hT_{s}", [P, NF, HALF], F32R) for s in ("hi", "lo"))
        gu_stage = sb("gu_stage", [P, 2, 2, KD, P])
        gu_hi, gu_lo = (sb(f"gu_{s}", [P, 2, 2, KD, P], F32R) for s in ("hi", "lo"))
        wd_stage = sb("wd_stage", [P, 2, DM])
        wd_hi, wd_lo = (sb(f"wd_{s}", [P, 2, DM], F32R) for s in ("hi", "lo"))
        work = sb("work", [P, 4, DM])
        toep_hi, toep_lo = (sb(f"toep_{s}", [P, P + DM], F32R) for s in ("hi", "lo"))
        tab = sb("tab", [P, 2 * KD * DM])
        cos_t = tab[:, 0:KD * DM].rearrange("p (t l) -> p t l", t=KD)
        sin_t = tab[:, KD * DM:].rearrange("p (t l) -> p t l", t=KD)
        wc_stage = tab[:, 0:KD * WC].rearrange("p (k n) -> p k n", k=KD)
        wb_stage = tab[:, KD * WC:KD * WC + DM]
        wc_hi, wc_lo = (sb(f"wc_{s}", [P, KD, WC], F32R) for s in ("hi", "lo"))
        wb_hi, wb_lo = (sb(f"wb_{s}", [P, DM], F32R) for s in ("hi", "lo"))
        s4 = sb("s4", [P, 8, DM])
        uv = sb("uv", [P, 2, KD, P])
        vcs = sb("vcs", [NS, 2 * NS])
        bps = sb("bps", [NS, NS])
        sm = sb("sm", [NS, 12])
        bb = sb("bb", [NS, 8])
        vv = sb("vv", [NS, 16])
        omc = sb("omc", [P, 2, KD])
        cs = sb("cs", [P, 24, KD])
        A = sb("A", [P, KD, 8])
        dsk = sb("dsk", [P, 2])
        st = sb("st", [P, TH, 6])
        mv = sb("mv", [P, TH, 2])
        ln = sb("ln", [P, 4, TH])
        gt = sb("gt", [P, 10, TH])
        bias = s4[:, 7, :]
        om = s4[0:NS, 0:3, :]
        hg = s4[:, 0:2, :].rearrange("p a b -> p (a b)")[:, 0:TH * (WC - DM)].rearrange("p (t n) -> p t n", t=TH)
        hw = s4[:, 2, :].rearrange("p (t n) -> p t n", t=TH)
        ge = s4[:, 3, 0:TH * NE].rearrange("p (t e) -> p t e", t=TH)
        gw = s4[:, 4, 0:TH * NE].rearrange("p (t e) -> p t e", t=TH)

        x_loaded = [sem(f"x_loaded{i}") for i in range(2)]
        ident_loaded = sem("ident_loaded")
        gu_loaded = [sem(f"gu_loaded{i}") for i in range(2)]
        wd_loaded = [sem(f"wd_loaded{i}") for i in range(2)]
        s4_loaded = sem("s4_loaded")
        tab_loaded = sem("tab_loaded")
        wc_loaded = sem("wc_loaded")
        bias_loaded = sem("bias_loaded")
        gu_hi_done = sem("gu_hi_done")
        gu_ready = sem("gu_ready")
        gu_used = sem("gu_used")
        wait_passed = sem("wait_passed")
        silu_done = sem("silu_done")
        h_done = sem("h_done")
        h_hi_done = sem("h_hi_done")
        h_lo_done = sem("h_lo_done")
        wd_hi_done = sem("wd_hi_done")
        wd_ready = sem("wd_ready")
        wd_used = sem("wd_used")
        var_done = sem("var_done")
        sd_done = sem("sd_done")
        xn_done = sem("xn_done")
        xT_done = sem("xT_done")
        xT_hi_done = sem("xT_hi_done")
        xT_lo_done = sem("xT_lo_done")
        step_done = sem("step_done")
        cauchy_in = sem("cauchy_in")
        cauchy_done = sem("cauchy_done")
        cauchy_read = sem("cauchy_read")
        uv_done = sem("uv_done")
        toep_done = sem("toep_done")
        toep_copied = sem("toep_copied")
        toep_masked = sem("toep_masked")
        toep_ready = sem("toep_ready")
        y_done = sem("y_done")
        x1_done = sem("x1_done")
        comb_hi_done = sem("comb_hi_done")
        comb_ready = sem("comb_ready")
        base_done = sem("base_done")
        hg_done = sem("hg_done")
        base_added = sem("base_added")
        bias_added = sem("bias_added")
        ge_in = sem("ge_in")
        ge_done = sem("ge_done")
        hw_done = sem("hw_done")
        hwT_done = sem("hwT_done")
        hwT_hi_done = sem("hwT_hi_done")
        hwT_lo_done = sem("hwT_lo_done")
        moe_done = sem("moe_done")
        moe_added = sem("moe_added")
        dve_chain = sem("dve_chain")

        def ffn_tiles(eng, half, body, first=0, end=NF // 2 + 1):
            if first < min(end, NF // 2):
                with eng.Fori(first, min(end, NF // 2)) as it:
                    for j in range(2):
                        n = half * NF + j
                        body(it * 2 + j, n % 2, it + n // 2)
            if end > NF // 2:
                n = half * NF + NF - 1
                body(NF - 1, n % 2, n // 2)

        block = ctx.enter_context(nc.Block())

        @block.sync
        def _(sp):
            sp.dma_start(ident[:, :], ident_dram).then_inc(ident_loaded, 16)
            for t in range(NT):
                sp.dma_start(acc[:, t, :], x[t * P:(t + 1) * P, :]).then_inc(x_loaded[t // TH], 16)
            for half in range(2):
                def load_gu(f, i, seen):
                    sp.wait_ge(gu_ready, seen * 2 + i + 1)
                    sp.dma_start(gu_stage[:, i], w_gu[f]).then_inc(gu_loaded[i], 16)
                ffn_tiles(sp, half, load_gu)
                for c in range(NF):
                    n = half * NF + c
                    if n >= 2:
                        sp.wait_ge(wd_ready, n - 1)
                    sp.dma_start(wd_stage[:, n % 2], w_down[c]).then_inc(wd_loaded[n % 2], 16)
            sp.dma_start(bias, b_base.partition_broadcast(P)).then_inc(bias_loaded, 16)
            sp.dma_start(dsk[:, 1:2], b_thr.partition_broadcast(P)).then_inc(bias_loaded, 16)
            sp.wait_ge(toep_done, 1)
            sp.dma_start(wc_stage, w_comb.rearrange("k p n -> p k n")).then_inc(wc_loaded, 16)
            sp.dma_start(wb_stage, w_expb).then_inc(wc_loaded, 16)

        @block.gpsimd
        def _(pool):
            for half in range(2):
                def split_gu(f, i, seen):
                    n = seen * 2 + i
                    pool.wait_ge(gu_loaded[i], seen * 16 + 16)
                    pool.wait_ge(gu_used, n + 1)
                    pool.sem_inc(wait_passed, 1)
                    nc.gpsimd.tensor_scalar(gu_hi[:, i], gu_stage[:, i], 1.0, 1.0, ALU.mult, ALU.mult).then_inc(gu_hi_done, 1)
                    pool.wait_ge(gu_hi_done, n + 1)
                    nc.gpsimd.tensor_tensor(gu_lo[:, i], gu_stage[:, i], as_f32(gu_hi[:, i]),
                                            ALU.subtract).then_inc(gu_ready, 1)
                ffn_tiles(pool, half, split_gu)
                for c in range(NF):
                    n = half * NF + c
                    i = n % 2
                    pool.wait_ge(wd_loaded[i], 16 * (n // 2 + 1))
                    if n >= 2:
                        pool.wait_ge(wd_used, n - 1)
                    nc.gpsimd.tensor_scalar(wd_hi[:, i], wd_stage[:, i], 1.0, 1.0, ALU.mult, ALU.mult).then_inc(wd_hi_done, 1)
                    pool.wait_ge(wd_hi_done, n + 1)
                    nc.gpsimd.tensor_tensor(wd_lo[:, i], wd_stage[:, i], as_f32(wd_hi[:, i]),
                                            ALU.subtract).then_inc(wd_ready, 1)
                    if n == 7:
                        pool.wait_ge(toep_copied, 1)
                        nc.gpsimd.affine_select(out=s4[:, 5, 0:P], in_=s4[:, 5, 0:P], compare_op=ALU.is_ge, fill=0.0,
                                                base=0, pattern=[[1, P]], channel_multiplier=-1).then_inc(toep_masked, 1)
            pool.wait_ge(wc_loaded, 32)
            for k in range(KD):
                nc.gpsimd.tensor_scalar(wc_hi[:, k], wc_stage[:, k], 1.0, 1.0, ALU.mult, ALU.mult).then_inc(comb_hi_done, 1)
                pool.wait_ge(comb_hi_done, k + 1)
                nc.gpsimd.tensor_tensor(wc_lo[:, k], wc_stage[:, k], as_f32(wc_hi[:, k]),
                                        ALU.subtract).then_inc(comb_ready, 1)
            nc.gpsimd.tensor_scalar(wb_hi[:, :], wb_stage, 1.0, 1.0, ALU.mult, ALU.mult).then_inc(comb_hi_done, 1)
            pool.wait_ge(comb_hi_done, KD + 1)
            nc.gpsimd.tensor_tensor(wb_lo[:, :], wb_stage, as_f32(wb_hi[:, :]), ALU.subtract).then_inc(comb_ready, 1)
            pool.wait_ge(bias_loaded, 32)
            for t in range(NT):
                pool.wait_ge(xn_done, NT + t + 1)
                nc.gpsimd.tensor_tensor(acc[:, t, :], acc[:, t, :], bias, ALU.add).then_inc(bias_added, 1)

        @block.scalar
        def _(act):
            for c, a in ((0, lam), (2, p_ri), (4, q_ri), (6, ct)):
                act.dma_start(sm[:, c:c + 2], a).then_inc(s4_loaded, 16)
            act.dma_start(sm[:, 8:9], log_step.partition_broadcast(NS)).then_inc(s4_loaded, 16)
            act.dma_start(vcs[:, :], vc).then_inc(s4_loaded, 16)
            act.dma_start(bps[:, :], bp.partition_broadcast(NS)).then_inc(s4_loaded, 16)
            act.dma_start(om, om_rows.partition_broadcast(NS)).then_inc(s4_loaded, 16)
            act.dma_start(omc[:, :, :], om_cols).then_inc(s4_loaded, 16)
            act.dma_start(dsk[:, 0:1], d_skip.partition_broadcast(P)).then_inc(s4_loaded, 16)
            act.dma_start(tab[:, :], tables).then_inc(tab_loaded, 16)

            def sqrt_var(n):
                act.wait_ge(var_done, n + 1)
                nc.scalar.activation(ln[:, 1, :], ln[:, 0, :], ACT.Sqrt).then_inc(sd_done, 1)

            def xT_evac(n, bank):
                act.wait_ge(xT_done, n + 1)
                t = n % NT
                nc.scalar.activation(xT_hi[:, :, t * P:(t + 1) * P],
                                     banks[:, bank, :].rearrange("p (k n) -> p k n", k=KD),
                                     ACT.Copy).then_inc(xT_hi_done, 1)

            def ffn(half):
                def silu_tile(f, i, seen):
                    n = seen * 2 + i
                    act.wait_ge(gu_used, n + 3)
                    nc.scalar.activation(work[:, i], banks[:, G + 2 * i], ACT.Silu).then_inc(silu_done, 1)
                    act.wait_ge(h_done, n + 3)
                    nc.scalar.activation(hT_hi[:, f], work[:, 2 + i], ACT.Copy).then_inc(h_hi_done, 1)
                ffn_tiles(act, half, silu_tile)

            def hg_copy(half):
                for t in range(TH):
                    n = half * TH + t
                    act.wait_ge(base_done, n + 1)
                    if half:
                        act.wait_ge(hw_done, 1)
                    nc.scalar.activation(hg[:, t, :], banks[:, G + 2 * (n % 2) + 1, DM - CUT:WC - CUT],
                                         ACT.Copy).then_inc(hg_done, 1)

            def gate_exps(half):
                act.wait_ge(ge_in, 2 * half + 2)
                nc.scalar.activation(ge, ge, ACT.Exp).then_inc(ge_done, 1)
                nc.scalar.activation(gt[:, 1, :], gt[:, 0, :], ACT.Exp, scale=-1.0).then_inc(ge_done, 1)

            def hwT_evac(half):
                for t in range(TH):
                    n = half * TH + t
                    act.wait_ge(hwT_done, n + 1)
                    if n >= 2:
                        act.wait_ge(moe_done, n - 1)
                    nc.scalar.activation(wd_hi[:, t % 2, 0:P], banks[:, D + t % 2, 0:P], ACT.Copy).then_inc(hwT_hi_done, 1)

            sqrt_var(0)
            for t in range(TH):
                xT_evac(t, D + t)
            act.wait_ge(s4_loaded, 160)
            nc.scalar.activation(sm[:, 9:10], sm[:, 8:9], ACT.Exp, scale=-1.0).then_inc(step_done, 1)
            ffn(0)
            sqrt_var(1)
            for t in range(TH, NT):
                xT_evac(t, G + t - TH)
            act.wait_ge(toep_ready, 1)
            nc.scalar.activation(toep_hi[:, P:], s4[:, 6, :], ACT.Copy).then_inc(toep_ready, 1)
            ffn(1)
            sqrt_var(2)
            for t in range(TH):
                xT_evac(NT + t, G + t)
            sqrt_var(3)
            hg_copy(0)
            for t in range(TH, NT):
                xT_evac(NT + t, D + t - TH)
            gate_exps(0)
            hg_copy(1)
            hwT_evac(0)
            gate_exps(1)
            hwT_evac(1)

        @block.vector
        def _(dve):
            chained = [0]

            def link(ins):
                chained[0] += 1
                ins.then_inc(dve_chain, 1)
                dve.wait_ge(dve_chain, chained[0])

            dve.sem_inc(h_done, 2)
            dve.sem_inc(gu_ready, 2)
            dve.sem_inc(gu_used, 2)
            nc.vector.memset(as_f32(toep_hi[:, 0:P]), 0.0)
            link(nc.vector.memset(as_f32(toep_lo[:, 0:P]), 0.0))

            def norm(n, half):
                tiles = range(half * TH, half * TH + TH)
                for j, t in enumerate(tiles):
                    ins = nc.vector.bn_stats(st[:, j, :], acc[:, t, :])
                link(ins)
                for j in range(TH):
                    ins = nc.vector.bn_aggr(mv[:, j, :], st[:, j, :])
                link(ins)
                nc.vector.tensor_scalar(ln[:, 0, :], mv[:, :, 1], EPS, None, ALU.add).then_inc(var_done, 1)
                dve.wait_ge(sd_done, n + 1)
                link(nc.vector.reciprocal(ln[:, 2, :], ln[:, 1, :]))
                link(nc.vector.tensor_tensor(ln[:, 3, :], ln[:, 2, :], ln[:, 2, :], ALU.mult))
                link(nc.vector.tensor_tensor(ln[:, 3, :], ln[:, 3, :], ln[:, 0, :], ALU.mult))
                link(nc.vector.tensor_scalar(ln[:, 3, :], ln[:, 3, :], -0.5, 1.5, ALU.mult, ALU.add))
                link(nc.vector.tensor_tensor(ln[:, 2, :], ln[:, 2, :], ln[:, 3, :], ALU.mult))
                for j, t in enumerate(tiles):
                    nc.vector.tensor_scalar(work[:, j], acc[:, t, :], mv[:, j, 0:1], ln[:, 2, j:j + 1],
                                            ALU.subtract, ALU.mult).then_inc(xn_done, 1)

            def xT_evac(n, bank):
                dve.wait_ge(xT_hi_done, n + 1)
                cols = slice((n % NT) * P, (n % NT + 1) * P)
                nc.vector.tensor_tensor(xT_lo[:, :, cols], banks[:, bank, :].rearrange("p (k n) -> p k n", k=KD),
                                        as_f32(xT_hi[:, :, cols]), ALU.subtract).then_inc(xT_lo_done, 1)

            def ffn(half, between):
                def h_tile(f, i, seen):
                    n = seen * 2 + i
                    dve.wait_ge(silu_done, n + 1)
                    nc.vector.tensor_tensor(work[:, 2 + i], banks[:, G + 2 * i + 1], work[:, i],
                                            ALU.mult).then_inc(h_done, 1)
                    dve.wait_ge(h_hi_done, n + 1)
                    nc.vector.tensor_tensor(hT_lo[:, f], work[:, 2 + i], as_f32(hT_hi[:, f]),
                                            ALU.subtract).then_inc(h_lo_done, 1)
                cuts = [0, *sorted(between), NF // 2 + 1]
                for first, end in zip(cuts, cuts[1:]):
                    if first in between:
                        between[first]()
                    ffn_tiles(dve, half, h_tile, first, end)

            one_m, one_p, w_im, dr, di, sq = (s4[0:NS, i, :] for i in range(6))

            def cauchy_d():
                dve.wait_ge(s4_loaded, 160)
                dve.wait_ge(step_done, 1)
                link(nc.vector.tensor_scalar(sm[:, 9:10], sm[:, 9:10], 2.0, None, ALU.mult))
                link(nc.vector.tensor_scalar(sm[:, 11:12], sm[:, 0:1], -1.0, None, ALU.mult))
                nc.vector.tensor_scalar(bb[:, 4:5], sm[:, 1:2], -1.0, None, ALU.mult)
                link(nc.vector.tensor_tensor(sm[:, 10:11], sm[:, 11:12], sm[:, 9:10], ALU.subtract))
                link(nc.vector.tensor_scalar(dr, one_m, sm[:, 9:10], None, ALU.mult))
                link(nc.vector.scalar_tensor_tensor(dr, one_p, sm[:, 11:12], dr, ALU.mult, ALU.add))
                link(nc.vector.scalar_tensor_tensor(dr, w_im, sm[:, 1:2], dr, ALU.mult, ALU.add))
                link(nc.vector.tensor_scalar(di, w_im, sm[:, 10:11], None, ALU.mult))
                link(nc.vector.scalar_tensor_tensor(di, one_p, bb[:, 4:5], di, ALU.mult, ALU.add))

            def cauchy_inverse():
                link(nc.vector.tensor_tensor(sq, dr, dr, ALU.mult))
                link(nc.vector.tensor_tensor(one_m, di, di, ALU.mult))
                link(nc.vector.tensor_tensor(sq, sq, one_m, ALU.add))
                link(nc.vector.reciprocal(sq, sq))
                nc.vector.tensor_tensor(dr, dr, sq, ALU.mult)
                link(nc.vector.scalar_tensor_tensor(di, di, -1.0, sq, ALU.mult, ALU.mult))

            def cauchy_numerators():
                for c in range(2):
                    link(nc.vector.tensor_tensor(sq[:, 0:NS], vcs[:, c * NS:(c + 1) * NS], bps[:, :], ALU.mult))
                    link(nc.vector.tensor_reduce(bb[:, 2 * c:2 * c + 1], sq[:, 0:NS], AX_X, ALU.add))
                nc.vector.tensor_copy(bb[:, 1:2], sm[:, 2:3])
                link(nc.vector.tensor_copy(bb[:, 3:4], sm[:, 3:4]))
                for n, a in enumerate((6, 4)):
                    re, im = sm[:, a:a + 1], sm[:, a + 1:a + 2]
                    link(nc.vector.tensor_scalar(bb[:, 5:7], bb[:, 0:2], re, None, ALU.mult))
                    link(nc.vector.scalar_tensor_tensor(vv[:, 2 * n:2 * n + 2], bb[:, 2:4], im, bb[:, 5:7],
                                                        ALU.mult, ALU.add))
                    link(nc.vector.tensor_scalar(bb[:, 5:7], bb[:, 0:2], im, None, ALU.mult))
                    link(nc.vector.scalar_tensor_tensor(vv[:, 4 + 2 * n:6 + 2 * n], bb[:, 2:4], re, bb[:, 5:7],
                                                        ALU.mult, ALU.subtract))
                nc.vector.tensor_scalar(vv[:, 8:12], vv[:, 4:8], -1.0, None, ALU.mult)
                link(nc.vector.tensor_copy(vv[:, 12:16], vv[:, 0:4]))
                dve.sem_inc(cauchy_in, 1)

            def roots():
                dve.wait_ge(cauchy_done, 1)
                nc.vector.tensor_copy(A[:, :, :], banks[:, D, 0:KD * 8].rearrange("p (t c) -> p t c",
                                                                                   t=KD)).then_inc(cauchy_read, 1)
                dve.wait_ge(cauchy_read, 1)
                wr, wi = omc[:, 0, :], omc[:, 1, :]

                def c(i):
                    return cs[:, i, :]

                def a(i):
                    return A[:, :, i], A[:, :, 4 + i]

                def cmul(o, u, v, t):
                    nc.vector.tensor_tensor(c(t), u[0], v[0], ALU.mult)
                    nc.vector.tensor_tensor(c(t + 1), u[1], v[1], ALU.mult)
                    nc.vector.tensor_tensor(c(t + 2), u[0], v[1], ALU.mult)
                    link(nc.vector.tensor_tensor(c(t + 3), u[1], v[0], ALU.mult))
                    nc.vector.tensor_tensor(c(o), c(t), c(t + 1), ALU.subtract)
                    link(nc.vector.tensor_tensor(c(o + 1), c(t + 2), c(t + 3), ALU.add))
                    return c(o), c(o + 1)

                den = cmul(0, (wr, wi), a(3), 8)
                link(nc.vector.tensor_scalar(c(0), c(0), 1.0, None, ALU.add))
                num = cmul(2, a(1), a(2), 8)
                num = cmul(4, num, (wr, wi), 8)
                nc.vector.tensor_tensor(c(8), den[0], den[0], ALU.mult)
                link(nc.vector.tensor_tensor(c(9), den[1], den[1], ALU.mult))
                link(nc.vector.tensor_tensor(c(8), c(8), c(9), ALU.add))
                link(nc.vector.reciprocal(c(8), c(8)))
                nc.vector.tensor_tensor(c(0), den[0], c(8), ALU.mult)
                link(nc.vector.scalar_tensor_tensor(c(1), den[1], -1.0, c(8), ALU.mult, ALU.mult))
                quo = cmul(6, num, den, 8)
                nc.vector.tensor_tensor(c(8), a(0)[0], quo[0], ALU.subtract)
                link(nc.vector.tensor_tensor(c(9), a(0)[1], quo[1], ALU.subtract))
                link(nc.vector.tensor_scalar(cs[:, 8:10, :], cs[:, 8:10, :], 2.0 / DM, None, ALU.mult))

            def phases():
                dve.wait_ge(tab_loaded, 16)
                for t in range(KD):
                    re, im = cs[:, 8, t:t + 1], cs[:, 9, t:t + 1]
                    nc.vector.tensor_scalar(s4[:, 6, 0:P], cos_t[:, t, 0:P], re, None, ALU.mult)
                    link(nc.vector.tensor_scalar(s4[:, 6, P:2 * P], cos_t[:, t, 0:P], im, None, ALU.mult))
                    nc.vector.scalar_tensor_tensor(uv[:, 0, t], sin_t[:, t, 0:P], im, s4[:, 6, 0:P], ALU.mult, ALU.add)
                    link(nc.vector.scalar_tensor_tensor(uv[:, 1, t], sin_t[:, t, 0:P], re, s4[:, 6, P:2 * P],
                                                        ALU.mult, ALU.subtract))
                dve.sem_inc(uv_done, 1)

            def toeplitz():
                dve.wait_ge(toep_done, 1)
                nc.vector.tensor_copy(s4[:, 5, :], banks[:, G + 1, :]).then_inc(toep_copied, 1)
                dve.wait_ge(toep_masked, 1)
                nc.vector.tensor_copy(s4[:, 6, P:], s4[:, 5, P:])
                nc.vector.scalar_tensor_tensor(s4[:, 6, 0:P], ident[:, :], dsk[:, 0:1], s4[:, 5, 0:P],
                                               ALU.mult, ALU.add).then_inc(toep_ready, 1)
                dve.wait_ge(toep_ready, 2)
                nc.vector.tensor_tensor(toep_lo[:, P:], s4[:, 6, :], as_f32(toep_hi[:, P:]),
                                        ALU.subtract).then_inc(toep_ready, 1)

            def residual(half):
                for t in range(half * TH, half * TH + TH):
                    dve.wait_ge(y_done, t + 1)
                    ins = nc.vector.tensor_tensor(acc[:, t, :], acc[:, t, :], banks[:, D + t % TH, :], ALU.add)
                    ins.then_inc(x1_done, 1)
                dve.wait_ge(x1_done, half * TH + TH)

            def linear_add(n):
                t, bank = n, G + 2 * (n % 2)
                dve.wait_ge(hg_done, n + 1)
                dve.wait_ge(bias_added, n + 1)
                nc.vector.tensor_tensor(acc[:, t, 0:CUT], acc[:, t, 0:CUT], banks[:, bank, 0:CUT], ALU.add)
                nc.vector.tensor_tensor(acc[:, t, CUT:DM], acc[:, t, CUT:DM], banks[:, bank + 1, 0:DM - CUT],
                                        ALU.add).then_inc(base_added, 1)

            def gates(half):
                dve.wait_ge(hg_done, half * TH + TH)
                logits = hg[:, :, ER:ER + NE]

                def wide(i):
                    return gt[:, i, :].unsqueeze(2).broadcast_to([P, TH, NE])
                link(nc.vector.tensor_reduce(gt[:, 2, :], logits, AX_X, ALU.max))
                nc.vector.tensor_tensor(ge, logits, wide(2), ALU.subtract).then_inc(ge_in, 1)
                nc.vector.tensor_scalar(gt[:, 0, :], hg[:, :, ER + NE], dsk[:, 1:2], None, ALU.add).then_inc(ge_in, 1)
                dve.wait_ge(ge_done, 2 * half + 2)
                nc.vector.tensor_reduce(gt[:, 3, :], ge, AX_X, ALU.add)
                link(nc.vector.tensor_scalar(gt[:, 4, :], gt[:, 1, :], 1.0, None, ALU.add))
                nc.vector.reciprocal(gt[:, 5, :], gt[:, 3, :])
                link(nc.vector.reciprocal(gt[:, 6, :], gt[:, 4, :]))
                nc.vector.tensor_tensor(gw, ge, wide(5), ALU.mult)
                link(nc.vector.tensor_scalar(gt[:, 6, :], gt[:, 6, :], MAX_THRESHOLD, None, ALU.mult))
                link(nc.vector.tensor_tensor(gw, gw, wide(6), ALU.subtract))
                link(nc.vector.tensor_scalar(gw, gw, 0.0, None, ALU.max))
                link(nc.vector.tensor_reduce(gt[:, 7, :], gw, AX_X, ALU.add))
                link(nc.vector.tensor_scalar(gt[:, 8, :], gt[:, 7, :], 0.0, None, ALU.is_equal))
                link(nc.vector.tensor_tensor(gt[:, 7, :], gt[:, 7, :], gt[:, 8, :], ALU.add))
                link(nc.vector.reciprocal(gt[:, 9, :], gt[:, 7, :]))
                link(nc.vector.tensor_scalar(gt[:, 9, :], gt[:, 9, :], SCALING, None, ALU.mult))
                link(nc.vector.tensor_tensor(gw, gw, wide(9), ALU.mult))
                if half:
                    dve.wait_ge(hwT_done, TH)
                for t in range(TH):
                    ins = nc.vector.tensor_tensor(hw[:, t, :].rearrange("p (e r) -> p e r", e=NE),
                                                  hg[:, t, 0:ER].rearrange("p (e r) -> p e r", e=NE),
                                                  gw[:, t, :].unsqueeze(2).broadcast_to([P, NE, RANK]), ALU.mult)
                ins.then_inc(hw_done, 1)

            def experts_add(half):
                for t in range(TH):
                    n = half * TH + t
                    dve.wait_ge(hwT_hi_done, n + 1)
                    nc.vector.tensor_tensor(wd_lo[:, t % 2, 0:P], banks[:, D + t % 2, 0:P],
                                            as_f32(wd_hi[:, t % 2, 0:P]), ALU.subtract).then_inc(hwT_lo_done, 1)
                    if t:
                        expert_out(n - 1)
                expert_out(half * TH + TH - 1)

            def expert_out(n):
                dve.wait_ge(moe_done, n + 1)
                nc.vector.tensor_tensor(acc[:, n, :], acc[:, n, :], banks[:, D + 2 + n % 2, :],
                                        ALU.add).then_inc(moe_added, 1)

            dve.wait_ge(x_loaded[0], 16 * TH)
            norm(0, 0)
            for t in range(TH):
                xT_evac(t, D + t)
            ffn(0, {1: cauchy_d, 2: cauchy_inverse, 3: cauchy_numerators, 5: roots})
            phases()
            dve.wait_ge(x_loaded[1], 16 * TH)
            norm(1, 1)
            for t in range(TH, NT):
                xT_evac(t, G + t - TH)
            toeplitz()
            residual(0)
            ffn(1, {})
            norm(2, 0)
            for t in range(TH):
                xT_evac(NT + t, G + t)
            residual(1)
            norm(3, 1)
            for n in range(TH):
                linear_add(n)
            for t in range(TH, NT):
                xT_evac(NT + t, D + t - TH)
            gates(0)
            for n in range(TH, NT):
                linear_add(n)
            experts_add(0)
            gates(1)
            experts_add(1)

        @block.tensor
        def _(pe):
            def transposes(n, bank):
                pe.wait_ge(xn_done, n + 1)
                for k in range(KD):
                    ins = nc.tensor.transpose(banks[:, bank, k * P:(k + 1) * P],
                                              work[:, n % TH, k * P:(k + 1) * P], ident[:, :])
                ins.then_inc(xT_done, 1)

            def gate_up(half):
                def tile(f, i, seen):
                    n = seen * 2 + i
                    pe.wait_ge(gu_ready, n + 3)
                    pe.wait_ge(h_done, n + 1)
                    for m in range(2):
                        for k in range(KD):
                            cols = slice(half * HALF, (half + 1) * HALF)
                            ins = matmul3(nc, banks[:, G + 2 * i + m], gu_hi[:, i, m, k], gu_lo[:, i, m, k],
                                          xT_hi[:, k, cols], xT_lo[:, k, cols], k == 0, k == KD - 1)
                    ins.then_inc(gu_used, 1)
                return tile

            def down(half, chunks):
                for c in chunks:
                    n = half * NF + c
                    pe.wait_ge(wd_ready, n + 1)
                    pe.wait_ge(h_lo_done, n + 1)
                    for t in range(TH):
                        cols = slice(t * P, (t + 1) * P)
                        ins = matmul3(nc, banks[:, D + t], hT_hi[:, c, cols], hT_lo[:, c, cols],
                                      wd_hi[:, n % 2], wd_lo[:, n % 2], c == 0, False)
                    ins.then_inc(wd_used, 1)

            def convolve(half):
                pe.wait_ge(toep_ready, 3)
                for t in range(half * TH, half * TH + TH):
                    cols = slice(t * P, (t + 1) * P)
                    for j in range(KD):
                        lo = min(j * P, DM - 2 * P)
                        src = slice(P + lo - j * P, P + DM - j * P)
                        ins = matmul3(nc, banks[:, D + t % TH, lo:DM], xT_hi[:, j, cols], xT_lo[:, j, cols],
                                      toep_hi[:, src], toep_lo[:, src], False, j == KD - 1)
                    ins.then_inc(y_done, 1)

            def linear(n):
                cols = slice(n * P, (n + 1) * P)
                bank = G + 2 * (n % 2)
                pe.wait_ge(comb_ready, KD)
                pe.wait_ge(xT_lo_done, NT + max(n + 1, TH))
                if n >= 2:
                    pe.wait_ge(base_added, n - 1)
                for b, part in ((bank, slice(0, CUT)), (bank + 1, slice(CUT, WC))):
                    for k in range(KD):
                        ins = matmul3(nc, banks[:, b, 0:part.stop - part.start], xT_hi[:, k, cols], xT_lo[:, k, cols],
                                      wc_hi[:, k, part], wc_lo[:, k, part], k == 0, k == KD - 1)
                ins.then_inc(base_done, 1)

            def experts(half):
                for t in range(TH + 1):
                    n = half * TH + t
                    if t < TH:
                        pe.wait_ge(hw_done, half + 1)
                        if n >= 2:
                            pe.wait_ge(hwT_lo_done, n - 1)
                        nc.tensor.transpose(banks[:, D + t % 2, 0:P], hw[:, t, :], ident[:, :]).then_inc(hwT_done, 1)
                    if t:
                        expert_product(n - 1)

            def expert_product(n):
                i = n % 2
                pe.wait_ge(hwT_lo_done, n + 1)
                pe.wait_ge(comb_ready, KD + 1)
                if n >= 2:
                    pe.wait_ge(moe_added, n - 1)
                matmul3(nc, banks[:, D + 2 + i], wd_hi[:, i, 0:P], wd_lo[:, i, 0:P], wb_hi[:, :], wb_lo[:, :],
                        True, True).then_inc(moe_done, 1)

            pe.wait_ge(ident_loaded, 16)
            for t in range(TH):
                transposes(t, D + t)
            pe.wait_ge(xT_lo_done, TH)
            ffn_tiles(pe, 0, gate_up(0), 0, 4)
            pe.wait_ge(cauchy_in, 1)
            for t in range(KD):
                out = banks[:, D, 8 * t:8 * t + 8]
                nc.tensor.matmul(out, s4[0:NS, 3, t * P:(t + 1) * P], vv[:, 0:8], start=True, stop=False)
                ins = nc.tensor.matmul(out, s4[0:NS, 4, t * P:(t + 1) * P], vv[:, 8:16], start=False, stop=True)
            ins.then_inc(cauchy_done, 1)
            ffn_tiles(pe, 0, gate_up(0), 4, 6)
            pe.wait_ge(cauchy_read, 1)
            down(0, range(0, 4))
            for t in range(TH, NT):
                transposes(t, G + t - TH)
            pe.wait_ge(xT_lo_done, NT)
            pe.wait_ge(uv_done, 1)
            for i, table in enumerate((cos_t, sin_t)):
                for t in range(KD):
                    ins = nc.tensor.matmul(banks[:, G + 1, :], uv[:, i, t], table[:, t, :],
                                           start=i + t == 0, stop=i * KD + t == 2 * KD - 1)
            ins.then_inc(toep_done, 1)
            down(0, range(4, NF))
            convolve(0)
            ffn_tiles(pe, 1, gate_up(1), 0, 6)
            pe.wait_ge(x1_done, TH)
            down(1, range(0, 6))
            for t in range(TH):
                transposes(NT + t, G + t)
            down(1, range(6, NF))
            convolve(1)
            for n in range(TH):
                linear(n)
            pe.wait_ge(x1_done, NT)
            for t in range(TH, NT):
                transposes(NT + t, D + t - TH)
            for n in range(TH, NT):
                linear(n)
            experts(0)
            experts(1)


def attention(nc, shared, ins):
    acc, xT_hi, xT_lo, ident, ident_dram, banks = shared
    w_qk, w_v, w_o, mask_dram, out = ins
    G, S, T, O = 0, 4, 6, 7

    with ExitStack() as ctx:
        def sb(name, shape, dt=F32):
            return ctx.enter_context(nc.sbuf_tensor(name, shape, dt))

        def sem(name):
            return ctx.enter_context(nc.semaphore(name))

        qT_hi, qT_lo, kT_hi, kT_lo = (sb(f"{n}T_{s}", [P, TOK], F32R) for n in "qk" for s in ("hi", "lo"))
        v_hi, v_lo = (sb(f"v_{s}", [P, NT, GH * DH], F32R) for s in ("hi", "lo"))
        oT_hi, oT_lo = (sb(f"oT_{s}", [P, GH, TOK], F32R) for s in ("hi", "lo"))
        wqk_stage = sb("wqk_stage", [P, RING, 2, KD, DH])
        wvo_stage = sb("wvo_stage", [P, RING, DM])
        wqk_hi, wqk_lo = (sb(f"wqk_{s}", [P, RING, 2, KD, DH], F32R) for s in ("hi", "lo"))
        wv_hi, wv_lo = (sb(f"wv_{s}", [P, KD, GH * DH], F32R) for s in ("hi", "lo"))
        wo_hi, wo_lo = (sb(f"wo_{s}", [P, GH, DM], F32R) for s in ("hi", "lo"))
        prob = sb("prob", [P, 2, 3 * P])
        pT_hi, pT_lo = (sb(f"pT_{s}", [P, 2, 4 * P], F32R) for s in ("hi", "lo"))
        mask = sb("mask", [P, 2 * P])
        top = sb("top", [P, 2, 2])
        total = sb("total", [P, 2, 2])
        inv = sb("inv", [P, 2, 2])

        mask_loaded = sem("mask_loaded")
        qk_loaded = [sem(f"qk_loaded{i}") for i in range(RING)]
        vo_loaded = [sem(f"vo_loaded{i}") for i in range(RING)]
        qk_ready = sem("qk_ready")
        vo_ready = sem("vo_ready")
        unit_free = sem("unit_free")
        oT_ready = sem("oT_ready")
        QK0, VO0, FREE0, OT0 = 2 * RING, RING, GBANKS, 1
        split_hi = sem("split_hi")
        unit_done = sem("unit_done")
        unit_hi = sem("unit_hi")
        s_done = sem("s_done")
        s_top = sem("s_top")
        exp_done = sem("exp_done")
        inv_done = sem("inv_done")
        norm_done = sem("norm_done")
        t_done = sem("t_done")
        pT_hi_done = sem("pT_hi_done")
        pT_ready = sem("pT_ready")
        o_done = sem("o_done")
        oT_hi_done = sem("oT_hi_done")
        zeros_done = sem("zeros_done")
        credit_given = sem("credit_given")
        out_done = sem("out_done")
        wait_passed = sem("wait_passed")

        def unit(*step):
            return UNITS.index(step) + 1

        n_split_units = sum(u[0] != "W" for u in UNITS)

        def split_unit(step):
            return [u for u in UNITS if u[0] != "W"].index(step) + 1

        def unit_dest(step):
            if step[0] == "V":
                return v_hi[:, step[1], :], v_lo[:, step[1], :]
            cols = slice(step[2] * HALF, (step[2] + 1) * HALF)
            hi, lo = (qT_hi, qT_lo) if step[0] == "Q" else (kT_hi, kT_lo)
            return hi[:, cols], lo[:, cols]

        def row_tiles(p):
            yield 0, prob[:, p % 2, 0:P], banks[:, S + p % 2, 0:P], mask[:, P:2 * P]
            yield 1, prob[:, p % 2, P:3 * P], banks[:, S + p % 2, 2 * P:4 * P], mask[:, :]

        block = ctx.enter_context(nc.Block())

        @block.sync
        def _(sp):
            sp.dma_start(mask[:, :], mask_dram).then_inc(mask_loaded, 16)
            sp.wait_ge(credit_given, 1)
            with sp.Fori(0, NG) as g:
                for kind, n in SPLITS:
                    if kind == "q":
                        sp.wait_ge(qk_ready, g * NQK + 2 * (n - RING) + 2 + QK0)
                        sp.dma_start(wqk_stage[:, n % RING], w_qk[g * GH + n]).then_inc(qk_loaded[n % RING], 16)
                    elif kind in "vo":
                        j = n + KD * (kind == "o")
                        sp.wait_ge(vo_ready, g * NVO + j - RING + 1 + VO0)
                        src = w_v[g, n] if kind == "v" else w_o[g * GH + n]
                        sp.dma_start(wvo_stage[:, j % RING], src).then_inc(vo_loaded[j % RING], 16)
            for t in range(NT):
                sp.wait_ge(unit_free, (NG - 1) * NU + unit("W", t) + FREE0)
                sp.dma_start(out[t * P:(t + 1) * P, :], acc[:, t, :]).then_inc(out_done, 16)
            sp.wait_ge(out_done, 16 * NT)

        @block.gpsimd
        def _(pool):
            with pool.Fori(0, NG) as g:
                pieces = 0
                for kind, n in SPLITS:
                    if kind == "N":
                        i = n % 2
                        pool.wait_ge(inv_done, g * PAIRS + n + 1)
                        pool.sem_inc(wait_passed, 1)
                        nc.gpsimd.tensor_scalar(prob[:, i, 0:P], prob[:, i, 0:P], inv[:, i, 0:1], 1.0,
                                                ALU.mult, ALU.mult)
                        nc.gpsimd.tensor_scalar(prob[:, i, P:3 * P], prob[:, i, P:3 * P], inv[:, i, 1:2], 1.0,
                                                ALU.mult, ALU.mult).then_inc(norm_done, 1)
                        continue
                    if kind in "qk":
                        i, m = n % RING, "qk".index(kind)
                        pool.wait_ge(qk_loaded[i], g * (16 * GH // RING) + 16 * (n // RING + 1))
                        src, hi, lo, ready = wqk_stage[:, i, m], wqk_hi[:, i, m], wqk_lo[:, i, m], qk_ready
                    else:
                        j = n + KD * (kind == "o")
                        pool.wait_ge(vo_loaded[j % RING], g * (16 * NVO // RING) + 16 * (j // RING + 1))
                        hi, lo = (wv_hi, wv_lo) if kind == "v" else (wo_hi, wo_lo)
                        src, hi, lo, ready = wvo_stage[:, j % RING], hi[:, n], lo[:, n], vo_ready
                    pool.sem_inc(wait_passed, 1)
                    pieces += 1
                    nc.gpsimd.tensor_scalar(hi, src, 1.0, 1.0, ALU.mult, ALU.mult).then_inc(split_hi, 1)
                    pool.wait_ge(split_hi, g * (NQK + NVO) + pieces)
                    nc.gpsimd.tensor_tensor(lo, src, as_f32(hi), ALU.subtract).then_inc(ready, 1)

        @block.scalar
        def _(act):
            act.wait_ge(zeros_done, 1)

            def exps(g, p):
                act.wait_ge(s_top, g * PAIRS + p + 1)
                for r, pr, _, _ in row_tiles(p):
                    ins = nc.scalar.activation(pr, pr, ACT.Exp, bias=top[:, p % 2, r:r + 1], scale=-1.0,
                                               accum_out=total[:, p % 2, r:r + 1])
                ins.then_inc(exp_done, 1)

            with act.Fori(0, NG) as g:
                for step in GROUP:
                    if step == ("S", 0):
                        exps(g, 0)
                    elif step[0] in "QKV":
                        act.wait_ge(unit_done, g * NU + unit(*step))
                        nc.scalar.activation(unit_dest(step)[0], banks[:, G + (unit(*step) - 1) % GBANKS],
                                             ACT.Copy).then_inc(unit_hi, 1)
                    elif step[0] == "T":
                        p = step[1]
                        act.wait_ge(t_done, g * PAIRS + p + 1)
                        nc.scalar.activation(pT_hi[:, p % 2, P:], banks[:, T, 0:3 * P], ACT.Copy).then_inc(pT_hi_done, 1)
                        if p + 1 < PAIRS:
                            exps(g, p + 1)
                    elif step[0] == "O" and step[1] % 2:
                        h, half = step[1] // BATCH, step[1] % BATCH // 2
                        act.wait_ge(o_done, g * PAIRS + step[1] + 1)
                        nc.scalar.activation(oT_hi[:, h, half * HALF:(half + 1) * HALF], banks[:, O],
                                             ACT.Copy).then_inc(oT_hi_done, 1)

        @block.vector
        def _(dve):
            dve.sem_inc(qk_ready, QK0)
            dve.sem_inc(vo_ready, VO0)
            dve.sem_inc(unit_free, FREE0)
            dve.sem_inc(oT_ready, OT0)
            dve.sem_inc(credit_given, 1)
            nc.vector.memset(as_f32(pT_hi[:, :, 0:P]), 0.0)
            nc.vector.memset(as_f32(pT_lo[:, :, 0:P]), 0.0).then_inc(zeros_done, 1)
            dve.wait_ge(zeros_done, 1)
            dve.wait_ge(mask_loaded, 16)

            def inverse(g, p):
                dve.wait_ge(exp_done, g * PAIRS + p + 1)
                nc.vector.reciprocal(inv[:, p % 2, :], total[:, p % 2, :]).then_inc(inv_done, 1)

            with dve.Fori(0, NG) as g:
                for step in GROUP:
                    if step[0] == "S":
                        p = step[1]
                        dve.wait_ge(s_done, g * PAIRS + p + 1)
                        dve.sem_inc(wait_passed, 1)
                        for r, pr, sc, ma in row_tiles(p):
                            ins = nc.vector.tensor_tensor_reduce(out=pr, in0=sc, in1=ma, scale=-QK_SCALE, scalar=3e38,
                                                                 op0=ALU.add, op1=ALU.min,
                                                                 accum_out=top[:, p % 2, r:r + 1])
                        ins.then_inc(s_top, 1)
                        if p == 0:
                            inverse(g, 0)
                    elif step[0] in "QKV":
                        hi, lo = unit_dest(step)
                        dve.wait_ge(unit_hi, g * n_split_units + split_unit(step))
                        nc.vector.tensor_tensor(lo, banks[:, G + (unit(*step) - 1) % GBANKS], as_f32(hi),
                                                ALU.subtract).then_inc(unit_free, 1)
                    elif step[0] == "W":
                        t = step[1]
                        dve.wait_ge(unit_done, g * NU + unit(*step))
                        nc.vector.tensor_tensor(acc[:, t, :], acc[:, t, :], banks[:, G + (unit(*step) - 1) % GBANKS],
                                                ALU.add).then_inc(unit_free, 1)
                    elif step[0] == "T":
                        p = step[1]
                        dve.wait_ge(pT_hi_done, g * PAIRS + p + 1)
                        nc.vector.tensor_tensor(pT_lo[:, p % 2, P:], banks[:, T, 0:3 * P],
                                                as_f32(pT_hi[:, p % 2, P:]), ALU.subtract).then_inc(pT_ready, 1)
                        if p + 1 < PAIRS:
                            inverse(g, p + 1)
                    elif step[0] == "O" and step[1] % 2:
                        h, half = step[1] // BATCH, step[1] % BATCH // 2
                        cols = slice(half * HALF, (half + 1) * HALF)
                        dve.wait_ge(oT_hi_done, g * (PAIRS // 2) + step[1] // 2 + 1)
                        nc.vector.tensor_tensor(oT_lo[:, h, cols], banks[:, O], as_f32(oT_hi[:, h, cols]),
                                                ALU.subtract).then_inc(oT_ready, 1)

        @block.tensor
        def _(pe):
            pe.wait_ge(zeros_done, 1)
            pe.wait_ge(credit_given, 1)
            with pe.Fori(0, NG) as g:
                for step in GROUP:
                    kind, n = step[0], step[1]
                    if kind in "QKVW":
                        u = unit(*step)
                        bank = banks[:, G + (u - 1) % GBANKS]
                        pe.wait_ge(unit_free, g * NU + u - GBANKS + FREE0)
                    if kind in "QK":
                        m, cols = "QK".index(kind), slice(step[2] * HALF, (step[2] + 1) * HALF)
                        pe.wait_ge(qk_ready, g * NQK + 2 * n + m + 1 + QK0)
                        for k in range(KD):
                            ins = matmul3(nc, bank, wqk_hi[:, n % RING, m, k], wqk_lo[:, n % RING, m, k],
                                          xT_hi[:, k, cols], xT_lo[:, k, cols], k == 0, k == KD - 1)
                        ins.then_inc(unit_done, 1)
                    elif kind == "V":
                        pe.wait_ge(vo_ready, g * NVO + KD + VO0)
                        for k in range(KD):
                            ins = matmul3(nc, bank, xT_hi[:, k, n * P:(n + 1) * P], xT_lo[:, k, n * P:(n + 1) * P],
                                          wv_hi[:, k], wv_lo[:, k], k == 0, k == KD - 1)
                        ins.then_inc(unit_done, 1)
                    elif kind == "W":
                        pe.wait_ge(vo_ready, g * NVO + NVO + VO0)
                        pe.wait_ge(oT_ready, g * (PAIRS // 2) + PAIRS // 2 - 1 + (n >= TH) + OT0)
                        for h in range(GH):
                            cols = slice(n * P, (n + 1) * P)
                            ins = matmul3(nc, bank, oT_hi[:, h, cols], oT_lo[:, h, cols], wo_hi[:, h], wo_lo[:, h],
                                          h == 0, h == GH - 1)
                        ins.then_inc(unit_done, 1)
                    elif kind == "S":
                        h, b = n // BATCH, n % BATCH
                        last = max(unit("Q", h, b // 2), unit("K", h, b // 2))
                        pe.wait_ge(unit_free, g * NU + last + FREE0)
                        keys = slice(b * SEQ, (b + 1) * SEQ)
                        for r in range(2):
                            rows = slice(b * SEQ + r * P, b * SEQ + (r + 1) * P)
                            ins = matmul3(nc, banks[:, S + n % 2, 2 * r * P:2 * (r + 1) * P], qT_hi[:, rows],
                                          qT_lo[:, rows], kT_hi[:, keys], kT_lo[:, keys], True, True)
                        ins.then_inc(s_done, 1)
                    elif kind == "T":
                        pe.wait_ge(norm_done, g * PAIRS + n + 1)
                        for to, at in ((0, 2), (1, 0), (2, 1)):
                            ins = nc.tensor.transpose(banks[:, T, to * P:(to + 1) * P],
                                                      prob[:, n % 2, at * P:(at + 1) * P], ident[:, :])
                        ins.then_inc(t_done, 1)
                    elif kind == "O":
                        h, b = n // BATCH, n % BATCH
                        pe.wait_ge(pT_ready, g * PAIRS + n + 1)
                        if h == 0:
                            pe.wait_ge(unit_free, g * NU + unit("V", 2 * b + 1) + FREE0)
                        if n % 2 == 0:
                            pe.wait_ge(oT_ready, g * (PAIRS // 2) + n // 2 + OT0)
                        cols = slice(b % 2 * SEQ, (b % 2 + 1) * SEQ)
                        d = slice(h * DH, (h + 1) * DH)
                        matmul3(nc, banks[:, O, cols], v_hi[:, 2 * b, d], v_lo[:, 2 * b, d],
                                pT_hi[:, n % 2, 2 * P:], pT_lo[:, n % 2, 2 * P:], True, False)
                        ins = matmul3(nc, banks[:, O, cols], v_hi[:, 2 * b + 1, d], v_lo[:, 2 * b + 1, d],
                                      pT_hi[:, n % 2, 0:2 * P], pT_lo[:, n % 2, 0:2 * P], False, True)
                        ins.then_inc(o_done, 1)


def build(nc, x, w_gu, w_down, lam, p_ri, q_ri, ct, vc, bp, d_skip, log_step, om_rows, om_cols, tables,
          w_comb, b_base, b_thr, w_expb, w_qk, w_v, w_o, identity, mask, out):
    with ExitStack() as ctx:
        acc = ctx.enter_context(nc.sbuf_tensor("acc", [P, NT, DM], F32))
        xT_hi, xT_lo = (ctx.enter_context(nc.sbuf_tensor(f"xT_{s}", [P, KD, TOK], F32R)) for s in ("hi", "lo"))
        ident = ctx.enter_context(nc.sbuf_tensor("ident", [P, P], F32))
        banks = ctx.enter_context(nc.psum_tensor("banks", [P, 8, DM], F32))
        shared = (acc, xT_hi, xT_lo, ident, identity, banks)
        layer0(nc, shared, (x, w_gu, w_down, lam, p_ri, q_ri, ct, vc, bp, d_skip, log_step, om_rows, om_cols,
                            tables, w_comb, b_base, b_thr, w_expb))
        attention(nc, shared, (w_qk, w_v, w_o, mask, out))


def constants():
    import numpy as np
    f = np.arange(DM)
    w = np.exp(-2j * np.pi * f / DM)
    om_rows = np.stack([1 - w.real, 1 + w.real, w.imag]).astype(np.float32)
    om_cols = np.stack([1 + w.real, w.imag]).astype(np.float32).reshape(2, KD, P).transpose(2, 0, 1)
    turn = 2 * np.pi * (f[:, None] * f[None, :] % DM) / DM
    tables = np.stack([np.cos(turn), np.sin(turn)]).astype(np.float32)
    tables = tables.reshape(2, KD, P, DM).transpose(2, 0, 1, 3).reshape(P, 2 * KD * DM)
    mask = np.zeros((P, 2 * P), np.float32)
    mask[:, P:][np.triu_indices(P, 1)] = NEG
    return {"om_rows": om_rows, "om_cols": om_cols, "tables": tables, "identity": np.eye(P, dtype=np.float32),
            "mask": mask}


def layout(a):
    import numpy as np

    def chunks(w, n):
        return w.reshape(KD, P, n, P).transpose(2, 1, 0, 3)

    pad = ((0, 0), (0, NF * P - FF))
    gate, up, down = (np.pad(w, pad) for w in (a["L0_ffn_W_gate"].T, a["L0_ffn_W_up"].T, a["L0_ffn_W_down"]))
    wq = a["L1_attn_wq"].reshape(DM, HEADS, 192)[:, :, :DH].reshape(DM, HEADS * DH)
    wk, wv = a["L1_attn_wkv"][:, :HEADS * DH], a["L1_attn_wkv"][:, HEADS * DH:2 * HEADS * DH]
    comb = np.concatenate([a["L1_ffn_W_base"], a["L1_ffn_A_w"].reshape(ER, DM), a["L1_ffn_W_gate"],
                           a["L1_ffn_W_thr"][None], np.zeros((1, DM), np.float32)])
    return {
        "x": a["L0_attn_u"].reshape(TOK, DM),
        "w_gu": np.stack([chunks(gate, NF), chunks(up, NF)], axis=2),
        "w_down": down.T.reshape(NF, P, DM),
        "lam": a["L0_attn_Lambda_ri"], "p_ri": a["L0_attn_p_ri"], "q_ri": a["L0_attn_q_ri"],
        "ct": a["L0_attn_Ct_ri"].reshape(NS, 2), "vc": a["L0_attn_Vc_ri"].transpose(0, 2, 1).reshape(NS, 2 * NS),
        "bp": a["L0_attn_Bp"].reshape(NS), "d_skip": a["L0_attn_D"], "log_step": a["L0_attn_log_step"],
        "w_comb": comb.T.reshape(KD, P, WC), "b_base": a["L1_ffn_b_base"], "b_thr": a["L1_ffn_b_thr"],
        "w_expb": a["L1_ffn_B_w"].transpose(0, 2, 1).reshape(ER, DM),
        "w_qk": np.stack([chunks(wq, HEADS), chunks(wk, HEADS)], axis=2),
        "w_v": wv.reshape(KD, P, NG, GH * DH).transpose(2, 0, 1, 3),
        "w_o": a["L1_attn_wo"].reshape(HEADS, DH, DM),
    }


ORDER = ["x", "w_gu", "w_down", "lam", "p_ri", "q_ri", "ct", "vc", "bp", "d_skip", "log_step", "om_rows", "om_cols",
         "tables", "w_comb", "b_base", "b_thr", "w_expb", "w_qk", "w_v", "w_o", "identity", "mask"]


def kernel(**inputs):
    import numpy as np
    import concourse.bacc as bacc
    from concourse.bass_utils import run_bass_kernel_spmd

    nc = bacc.Bacc("TRN2", target_bir_lowering=False, num_devices=1)
    data = {**layout({k: np.asarray(v) for k, v in inputs.items()}), **constants()}
    arrays, args = {}, []
    for name in ORDER:
        arrays[f"in_{name}"] = np.ascontiguousarray(data[name])
        args.append(nc.dram_tensor(f"in_{name}", arrays[f"in_{name}"].shape, F32, kind="ExternalInput").ap())
    out = nc.dram_tensor("out", (TOK, DM), F32, kind="ExternalOutput").ap()
    build(nc, *args, out)
    r = run_bass_kernel_spmd(nc, [arrays], core_ids=[0])
    return r.results[0]["out"].reshape(BATCH, SEQ, DM)
```

```python
from contextlib import ExitStack

import concourse.bass as bass
from concourse import mybir

P = 128
F32 = mybir.dt.float32
F32R = mybir.dt.float32r
ALU = mybir.AluOpType
ACT = mybir.ActivationFunctionType
AX_X = mybir.AxisListType.X

BATCH, SEQ, DM = 4, 256, 512
TOK = BATCH * SEQ
NT = TOK // P
KD = DM // P
HALF = TOK // 2
TH = NT // 2
FF = 1376
NF = (FF + P - 1) // P
NS = 64
HEADS, DH = 32, 128
QK_SCALE = float(192) ** -0.5
GH = 4
NG = HEADS // GH
PAIRS = GH * BATCH
NE, RANK = 8, 16
ER = NE * RANK
WC = DM + ER + NE + 2
CUT = 384
EPS = 1e-5
NEG = -1e30
MAX_THRESHOLD, SCALING = 0.125, 2.0

AHEAD = [("Q", 0, 0), ("K", 0, 0), ("V", 0), ("V", 1)]
START = [("S", 0), ("Q", 0, 1), ("K", 0, 1),
         ("S", 1), ("T", 0), ("V", 2), ("V", 3), ("O", 0),
         ("S", 2), ("T", 1), ("Q", 1, 0), ("K", 1, 0), ("O", 1),
         ("S", 3), ("T", 2), ("V", 4), ("V", 5), ("Q", 1, 1), ("O", 2),
         ("S", 4), ("T", 3), ("V", 6), ("V", 7), ("K", 1, 1), ("O", 3)]
for _p, _unit in enumerate([("Q", 2, 0), ("K", 2, 0), ("Q", 2, 1), ("K", 2, 1),
                            ("Q", 3, 0), ("K", 3, 0), ("Q", 3, 1), ("K", 3, 1)], 5):
    START += [("S", _p), ("T", _p - 1), _unit, ("O", _p - 1)]
GROUP = START + [
    ("S", 13), ("T", 12), ("Q", 4, 0), ("O", 12),
    ("S", 14), ("T", 13), ("K", 4, 0), ("O", 13),
    ("S", 15), ("T", 14), ("V", 8), ("O", 14), ("W", 0), ("T", 15), ("V", 9), ("O", 15)] + [("W", t) for t in range(NT)][1:]
LAST_GROUP = START + [
    ("S", 13), ("T", 12), ("A", 0), ("O", 12),
    ("S", 14), ("T", 13), ("A", 1), ("A", 2), ("O", 13),
    ("S", 15), ("T", 14), ("A", 3), ("O", 14), ("A", 4), ("T", 15), ("A", 5), ("O", 15), ("A", 6), ("A", 7)] + [
    ("B", t) for t in range(NT)]


def units(steps):
    return [s for s in steps if s[0] in "QKVWAB"]


NU = len(units(GROUP))
GBANKS = 4
SPLITS = [("q", 1), ("k", 1), ("N", 0), ("o", 0), ("N", 1), ("q", 2), ("N", 2), ("k", 2), ("N", 3), ("o", 1),
          ("N", 4), ("o", 2), ("N", 5), ("q", 3), ("N", 6), ("k", 3), ("N", 7), ("o", 3), ("N", 8), ("v", 0),
          ("N", 9), ("v", 1), ("N", 10), ("q", 4), ("N", 11), ("v", 2), ("N", 12), ("k", 4), ("N", 13), ("v", 3),
          ("N", 14), ("N", 15)]
LAST_SPLITS = [s for s in SPLITS if s[0] != "v" and s not in (("q", 4), ("k", 4))]
NQK = 2 * GH
NVO = GH + KD
RING = 2


def matmul3(nc, out, w_hi, w_lo, x_hi, x_lo, first, last):
    nc.tensor.matmul(out, w_hi, x_hi, start=first, stop=False)
    nc.tensor.matmul(out, w_hi, x_lo, start=False, stop=False)
    return nc.tensor.matmul(out, w_lo, x_hi, start=False, stop=last)


def as_f32(ap):
    return ap.bitcast(F32)


def layer0(nc, sem, shared, ins, ffn_sb, expert_sb, small_sb):
    acc, xT_hi, xT_lo, ident, ident_dram, banks, y_done = shared
    (x, w_gu, w_down, lam, p_ri, q_ri, ct, vc, bp, d_skip, log_step, om_rows, om_cols, tables,
     w_comb, b_base, b_thr, w_expb) = ins
    G, D = 0, 4

    (hT_hi, hT_lo, gu_stage, gu_hi, gu_lo, wd_stage, wd_hi, wd_lo, work, toep_hi, toep_lo, tab) = ffn_sb
    wc_hi, wc_lo, wb_hi, wb_lo, s4, hwT_hi, hwT_lo, uv_place = expert_sb
    uv = uv_place[:, 0:2 * KD * P].rearrange("p (a t j) -> p a t j", a=2, t=KD)
    vcs, bps, sm, ex, exi, bb, vv, omc, cs, A, dsk, st, mv, ln, gt = small_sb
    cos_t = tab[:, 0:KD * DM].rearrange("p (t l) -> p t l", t=KD)
    sin_t = tab[:, KD * DM:].rearrange("p (t l) -> p t l", t=KD)
    wc_stage = tab[:, 0:KD * WC].rearrange("p (k n) -> p k n", k=KD)
    wb_stage = tab[:, KD * WC:KD * WC + DM]
    bias = s4[:, 7, :]
    om = s4[0:NS, 0:3, :]
    hg = s4[:, 0:2, :].rearrange("p a b -> p (a b)")[:, 0:TH * (WC - DM)].rearrange("p (t n) -> p t n", t=TH)
    hw = s4[:, 2, :].rearrange("p (t n) -> p t n", t=TH)
    ge = s4[:, 3, 0:TH * NE].rearrange("p (t e) -> p t e", t=TH)
    gw = s4[:, 4, 0:TH * NE].rearrange("p (t e) -> p t e", t=TH)

    x_loaded = [sem(f"x_loaded{t}") for t in range(NT)]
    ident_loaded = sem("ident_loaded")
    gu_loaded = [sem(f"gu_loaded{i}") for i in range(2)]
    wd_loaded = [sem(f"wd_loaded{i}") for i in range(2)]
    s4_loaded = sem("s4_loaded")
    tab_loaded = sem("tab_loaded")
    wc_loaded = sem("wc_loaded")
    bias_loaded = sem("bias_loaded")
    gu_hi_done = sem("gu_hi_done")
    gu_ready = sem("gu_ready")
    gu_used = sem("gu_used")
    wait_passed = sem("wait_passed")
    silu_done = sem("silu_done")
    h_done = sem("h_done")
    h_hi_done = sem("h_hi_done")
    h_lo_done = sem("h_lo_done")
    wd_hi_done = sem("wd_hi_done")
    wd_ready = sem("wd_ready")
    wd_used = sem("wd_used")
    var_done = sem("var_done")
    sd_done = sem("sd_done")
    xn_done = sem("xn_done")
    xT_done = sem("xT_done")
    xT_hi_done = sem("xT_hi_done")
    xT_lo_done = sem("xT_lo_done")
    ones_set = sem("ones_set")
    cauchy_in = sem("cauchy_in")
    cauchy_done = sem("cauchy_done")
    cauchy_read = sem("cauchy_read")
    uv_done = sem("uv_done")
    toep_done = sem("toep_done")
    toep_copied = sem("toep_copied")
    toep_masked = sem("toep_masked")
    toep_ready = sem("toep_ready")
    x1_done = sem("x1_done")
    comb_hi_done = sem("comb_hi_done")
    comb_ready = sem("comb_ready")
    base_done = sem("base_done")
    hg_done = sem("hg_done")
    base_added = sem("base_added")
    bias_added = sem("bias_added")
    ge_in = sem("ge_in")
    ge_done = sem("ge_done")
    hw_done = sem("hw_done")
    hwT_done = sem("hwT_done")
    hwT_hi_done = sem("hwT_hi_done")
    hwT_lo_done = sem("hwT_lo_done")
    moe_done = sem("moe_done")
    moe_added = sem("moe_added")
    dve_chain = sem("dve_chain")

    def ffn_tiles(eng, half, body, first=0, end=NF // 2 + 1):
        if first < min(end, NF // 2):
            with eng.Fori(first, min(end, NF // 2)) as it:
                for j in range(2):
                    n = half * NF + j
                    body(it * 2 + j, n % 2, it + n // 2)
        if end > NF // 2:
            n = half * NF + NF - 1
            body(NF - 1, n % 2, n // 2)

    def sync_program(sp):
        def load_x(t):
            sp.dma_start(acc[:, t, :], x[t * P:(t + 1) * P, :]).then_inc(x_loaded[t], 16)

        def load_gu(f, i, seen):
            sp.wait_ge(gu_ready, seen * 2 + i + 1)
            sp.dma_start(gu_stage[:, i], w_gu[f]).then_inc(gu_loaded[i], 16)

        for t in range(TH):
            load_x(t)
        sp.dma_start(ident[:, :], ident_dram).then_inc(ident_loaded, 16)
        ffn_tiles(sp, 0, load_gu, 0, 1)
        for t in range(TH, NT):
            load_x(t)
        for c, a in ((0, lam), (2, p_ri), (4, q_ri), (6, ct)):
            sp.dma_start(sm[:, c:c + 2], a).then_inc(s4_loaded, 16)
        sp.dma_start(sm[:, 8:9], log_step.partition_broadcast(NS)).then_inc(s4_loaded, 16)
        sp.dma_start(vcs[:, :], vc).then_inc(s4_loaded, 16)
        sp.dma_start(bps[:, :], bp.partition_broadcast(NS)).then_inc(s4_loaded, 16)
        sp.dma_start(om, om_rows.partition_broadcast(NS)).then_inc(s4_loaded, 16)
        sp.dma_start(omc[:, :, :], om_cols).then_inc(s4_loaded, 16)
        sp.dma_start(dsk[:, 0:1], d_skip.partition_broadcast(P)).then_inc(s4_loaded, 16)
        sp.dma_start(bias, b_base.partition_broadcast(P)).then_inc(bias_loaded, 16)
        sp.dma_start(dsk[:, 1:2], b_thr.partition_broadcast(P)).then_inc(bias_loaded, 16)
        ffn_tiles(sp, 0, load_gu, 1, 2)
        sp.dma_start(tab[:, :], tables).then_inc(tab_loaded, 16)
        for half in range(2):
            ffn_tiles(sp, half, load_gu, 0 if half else 2)
            for c in range(NF):
                n = half * NF + c
                if n >= 2:
                    sp.wait_ge(wd_ready, n - 1)
                sp.dma_start(wd_stage[:, n % 2], w_down[c]).then_inc(wd_loaded[n % 2], 16)
        sp.wait_ge(toep_done, 1)
        sp.dma_start(wc_stage, w_comb.rearrange("k p n -> p k n")).then_inc(wc_loaded, 16)
        sp.dma_start(wb_stage, w_expb).then_inc(wc_loaded, 16)
        sp.wait_ge(comb_ready, KD + 1)
        sp.wait_ge(xT_done, 2 * NT)

    def gpsimd_program(pool):
        for half in range(2):
            def split_gu(f, i, seen):
                n = seen * 2 + i
                pool.wait_ge(gu_loaded[i], seen * 16 + 16)
                pool.wait_ge(gu_used, n + 1)
                pool.sem_inc(wait_passed, 1)
                nc.gpsimd.tensor_scalar(gu_hi[:, i], gu_stage[:, i], 1.0, 1.0, ALU.mult, ALU.mult).then_inc(gu_hi_done, 1)
                pool.wait_ge(gu_hi_done, n + 1)
                nc.gpsimd.tensor_tensor(gu_lo[:, i], gu_stage[:, i], as_f32(gu_hi[:, i]),
                                        ALU.subtract).then_inc(gu_ready, 1)
            ffn_tiles(pool, half, split_gu)
            for c in range(NF):
                n = half * NF + c
                i = n % 2
                pool.wait_ge(wd_loaded[i], 16 * (n // 2 + 1))
                if n >= 2:
                    pool.wait_ge(wd_used, n - 1)
                nc.gpsimd.tensor_scalar(wd_hi[:, i], wd_stage[:, i], 1.0, 1.0, ALU.mult, ALU.mult).then_inc(wd_hi_done, 1)
                pool.wait_ge(wd_hi_done, n + 1)
                nc.gpsimd.tensor_tensor(wd_lo[:, i], wd_stage[:, i], as_f32(wd_hi[:, i]),
                                        ALU.subtract).then_inc(wd_ready, 1)
                if n == 7:
                    pool.wait_ge(toep_copied, 1)
                    nc.gpsimd.affine_select(out=s4[:, 5, 0:P], in_=s4[:, 5, 0:P], compare_op=ALU.is_ge, fill=0.0,
                                            base=0, pattern=[[1, P]], channel_multiplier=-1).then_inc(toep_masked, 1)
        pool.wait_ge(wc_loaded, 32)
        for k in range(KD):
            nc.gpsimd.tensor_scalar(wc_hi[:, k], wc_stage[:, k], 1.0, 1.0, ALU.mult, ALU.mult).then_inc(comb_hi_done, 1)
            pool.wait_ge(comb_hi_done, k + 1)
            nc.gpsimd.tensor_tensor(wc_lo[:, k], wc_stage[:, k], as_f32(wc_hi[:, k]),
                                    ALU.subtract).then_inc(comb_ready, 1)
        nc.gpsimd.tensor_scalar(wb_hi[:, :], wb_stage, 1.0, 1.0, ALU.mult, ALU.mult).then_inc(comb_hi_done, 1)
        pool.wait_ge(comb_hi_done, KD + 1)
        nc.gpsimd.tensor_tensor(wb_lo[:, :], wb_stage, as_f32(wb_hi[:, :]), ALU.subtract).then_inc(comb_ready, 1)
        pool.wait_ge(bias_loaded, 32)
        for t in range(NT):
            pool.wait_ge(xn_done, NT + t + 1)
            nc.gpsimd.tensor_tensor(acc[:, t, :], acc[:, t, :], bias, ALU.add).then_inc(bias_added, 1)

    def scalar_program(act, ahead):
        act.wait_ge(ones_set, 1)
        nc.scalar.activation(gt[:, 9, :], gt[:, 8, :], ACT.Sqrt)

        def sqrt_var(n):
            act.wait_ge(var_done, n + 1)
            nc.scalar.activation(ln[:, 1, :], ln[:, 0, :], ACT.Sqrt).then_inc(sd_done, 1)

        def xT_evac(n, bank):
            act.wait_ge(xT_done, n + 1)
            t = n % NT
            nc.scalar.activation(xT_hi[:, :, t * P:(t + 1) * P],
                                 banks[:, bank, :].rearrange("p (k n) -> p k n", k=KD),
                                 ACT.Copy).then_inc(xT_hi_done, 1)

        def ffn(half):
            def silu_tile(f, i, seen):
                n = seen * 2 + i
                act.wait_ge(gu_used, n + 3)
                nc.scalar.activation(work[:, i], banks[:, G + 2 * i], ACT.Silu).then_inc(silu_done, 1)
                act.wait_ge(h_done, n + 3)
                nc.scalar.activation(hT_hi[:, f], work[:, 2 + i], ACT.Copy).then_inc(h_hi_done, 1)
            ffn_tiles(act, half, silu_tile)

        def hg_copy(tiles):
            for n in tiles:
                half, t = n // TH, n % TH
                act.wait_ge(base_done, n + 1)
                if half:
                    act.wait_ge(hw_done, 1)
                nc.scalar.activation(hg[:, t, :], banks[:, G + 2 * (n % 2) + 1, DM - CUT:WC - CUT],
                                     ACT.Copy).then_inc(hg_done, 1)

        def gate_exps(half):
            act.wait_ge(ge_in, 2 * half + 2)
            nc.scalar.activation(ge, ge, ACT.Exp).then_inc(ge_done, 1)
            nc.scalar.activation(gt[:, 1, :], gt[:, 0, :], ACT.Exp, scale=-1.0).then_inc(ge_done, 1)

        def hwT_evac(half):
            for t in range(TH):
                n = half * TH + t
                act.wait_ge(hwT_done, n + 1)
                if n >= 2:
                    act.wait_ge(moe_done, n - 1)
                nc.scalar.activation(hwT_hi[:, t % 2], banks[:, D + t % 2, 0:P], ACT.Copy).then_inc(hwT_hi_done, 1)

        sqrt_var(0)
        for t in range(TH):
            xT_evac(t, D + t)
        ffn(0)
        sqrt_var(1)
        for t in range(TH, NT):
            xT_evac(t, G + t - TH)
        act.wait_ge(toep_ready, 1)
        nc.scalar.activation(toep_hi[:, P:], s4[:, 6, :], ACT.Copy).then_inc(toep_ready, 1)
        ffn(1)
        sqrt_var(2)
        for t in range(TH):
            xT_evac(NT + t, G + t)
        sqrt_var(3)
        hg_copy(range(0, 2))
        for t in range(TH, NT):
            xT_evac(NT + t, D + t - TH)
        hg_copy(range(2, TH))
        gate_exps(0)
        hg_copy(range(TH, NT))
        hwT_evac(0)
        gate_exps(1)
        ahead()
        hwT_evac(1)

    def vector_program(dve, ahead):
        chained = [0]

        def link(ins):
            chained[0] += 1
            ins.then_inc(dve_chain, 1)
            dve.wait_ge(dve_chain, chained[0])

        nc.vector.memset(gt[:, 8, :], 1.0).then_inc(ones_set, 1)
        dve.sem_inc(h_done, 2)
        dve.sem_inc(gu_ready, 2)
        dve.sem_inc(gu_used, 2)
        nc.vector.memset(as_f32(toep_hi[:, 0:P]), 0.0)
        link(nc.vector.memset(as_f32(toep_lo[:, 0:P]), 0.0))

        def norm(n, half):
            tiles = range(half * TH, half * TH + TH)
            for j, t in enumerate(tiles):
                if n < 2:
                    dve.wait_ge(x_loaded[t], 16)
                ins = nc.vector.bn_stats(st[:, j, :], acc[:, t, :])
            link(ins)
            for j in range(TH):
                ins = nc.vector.bn_aggr(mv[:, j, :], st[:, j, :])
            link(ins)
            nc.vector.tensor_scalar(ln[:, 0, :], mv[:, :, 1], EPS, None, ALU.add).then_inc(var_done, 1)
            dve.wait_ge(sd_done, n + 1)
            link(nc.vector.reciprocal(ln[:, 2, :], ln[:, 1, :]))
            link(nc.vector.tensor_tensor(ln[:, 3, :], ln[:, 2, :], ln[:, 2, :], ALU.mult))
            link(nc.vector.tensor_tensor(ln[:, 3, :], ln[:, 3, :], ln[:, 0, :], ALU.mult))
            link(nc.vector.tensor_scalar(ln[:, 3, :], ln[:, 3, :], -0.5, 1.5, ALU.mult, ALU.add))
            link(nc.vector.tensor_tensor(ln[:, 2, :], ln[:, 2, :], ln[:, 3, :], ALU.mult))
            for j, t in enumerate(tiles):
                nc.vector.tensor_scalar(work[:, j], acc[:, t, :], mv[:, j, 0:1], ln[:, 2, j:j + 1],
                                        ALU.subtract, ALU.mult).then_inc(xn_done, 1)

        def xT_evac(n, bank):
            dve.wait_ge(xT_hi_done, n + 1)
            cols = slice((n % NT) * P, (n % NT + 1) * P)
            nc.vector.tensor_tensor(xT_lo[:, :, cols], banks[:, bank, :].rearrange("p (k n) -> p k n", k=KD),
                                    as_f32(xT_hi[:, :, cols]), ALU.subtract).then_inc(xT_lo_done, 1)

        def ffn(half, between):
            def h_tile(f, i, seen):
                n = seen * 2 + i
                dve.wait_ge(silu_done, n + 1)
                nc.vector.tensor_tensor(work[:, 2 + i], banks[:, G + 2 * i + 1], work[:, i],
                                        ALU.mult).then_inc(h_done, 1)
                dve.wait_ge(h_hi_done, n + 1)
                nc.vector.tensor_tensor(hT_lo[:, f], work[:, 2 + i], as_f32(hT_hi[:, f]),
                                        ALU.subtract).then_inc(h_lo_done, 1)
            cuts = [0, *sorted(between), NF // 2 + 1]
            for first, end in zip(cuts, cuts[1:]):
                if first in between:
                    between[first]()
                ffn_tiles(dve, half, h_tile, first, end)

        one_m, one_p, w_im, dr, di, sq = (s4[0:NS, i, :] for i in range(6))

        def step_size():
            dve.wait_ge(s4_loaded, 160)
            xx, n, r, poly = (ex[:, i:i + 1] for i in range(4))
            link(nc.vector.tensor_scalar(xx, sm[:, 8:9], -1.0, None, ALU.mult))
            link(nc.vector.tensor_scalar(n, xx, 1.4426950408889634, 1.5 * 2 ** 23, ALU.mult, ALU.add))
            link(nc.vector.tensor_scalar(n, n, -1.5 * 2 ** 23, None, ALU.add))
            link(nc.vector.scalar_tensor_tensor(r, n, -0.693359375, xx, ALU.mult, ALU.add))
            link(nc.vector.scalar_tensor_tensor(r, n, 2.12194440e-4, r, ALU.mult, ALU.add))
            nc.vector.tensor_scalar(exi[:, :], n, 127.0, 2.0 ** 23, ALU.add, ALU.mult)
            link(nc.vector.tensor_scalar(poly, r, 1 / 5040, 1 / 720, ALU.mult, ALU.add))
            for coef in (1 / 120, 1 / 24, 1 / 6, 1 / 2, 1.0, 1.0):
                link(nc.vector.tensor_scalar(poly, poly, r, coef, ALU.mult, ALU.add))
            link(nc.vector.tensor_scalar(sm[:, 9:10], poly, as_f32(exi[:, :]), 2.0, ALU.mult, ALU.mult))

        def cauchy_d():
            link(nc.vector.tensor_scalar(sm[:, 11:12], sm[:, 0:1], -1.0, None, ALU.mult))
            nc.vector.tensor_scalar(bb[:, 4:5], sm[:, 1:2], -1.0, None, ALU.mult)
            link(nc.vector.tensor_tensor(sm[:, 10:11], sm[:, 11:12], sm[:, 9:10], ALU.subtract))
            link(nc.vector.tensor_scalar(dr, one_m, sm[:, 9:10], None, ALU.mult))
            link(nc.vector.scalar_tensor_tensor(dr, one_p, sm[:, 11:12], dr, ALU.mult, ALU.add))
            link(nc.vector.scalar_tensor_tensor(dr, w_im, sm[:, 1:2], dr, ALU.mult, ALU.add))
            link(nc.vector.tensor_scalar(di, w_im, sm[:, 10:11], None, ALU.mult))
            link(nc.vector.scalar_tensor_tensor(di, one_p, bb[:, 4:5], di, ALU.mult, ALU.add))

        def cauchy_inverse():
            link(nc.vector.tensor_tensor(sq, dr, dr, ALU.mult))
            link(nc.vector.tensor_tensor(one_m, di, di, ALU.mult))
            link(nc.vector.tensor_tensor(sq, sq, one_m, ALU.add))
            link(nc.vector.reciprocal(sq, sq))
            nc.vector.tensor_tensor(dr, dr, sq, ALU.mult)
            link(nc.vector.scalar_tensor_tensor(di, di, -1.0, sq, ALU.mult, ALU.mult))

        def cauchy_numerators():
            for c in range(2):
                link(nc.vector.tensor_tensor(sq[:, 0:NS], vcs[:, c * NS:(c + 1) * NS], bps[:, :], ALU.mult))
                link(nc.vector.tensor_reduce(bb[:, 2 * c:2 * c + 1], sq[:, 0:NS], AX_X, ALU.add))
            nc.vector.tensor_copy(bb[:, 1:2], sm[:, 2:3])
            link(nc.vector.tensor_copy(bb[:, 3:4], sm[:, 3:4]))
            for n, a in enumerate((6, 4)):
                re, im = sm[:, a:a + 1], sm[:, a + 1:a + 2]
                link(nc.vector.tensor_scalar(bb[:, 5:7], bb[:, 0:2], re, None, ALU.mult))
                link(nc.vector.scalar_tensor_tensor(vv[:, 2 * n:2 * n + 2], bb[:, 2:4], im, bb[:, 5:7],
                                                    ALU.mult, ALU.add))
                link(nc.vector.tensor_scalar(bb[:, 5:7], bb[:, 0:2], im, None, ALU.mult))
                link(nc.vector.scalar_tensor_tensor(vv[:, 4 + 2 * n:6 + 2 * n], bb[:, 2:4], re, bb[:, 5:7],
                                                    ALU.mult, ALU.subtract))
            nc.vector.tensor_scalar(vv[:, 8:12], vv[:, 4:8], -1.0, None, ALU.mult)
            link(nc.vector.tensor_copy(vv[:, 12:16], vv[:, 0:4]))
            dve.sem_inc(cauchy_in, 1)

        def roots():
            dve.wait_ge(cauchy_done, 1)
            nc.vector.tensor_copy(A[:, :, :], banks[:, D, 0:KD * 8].rearrange("p (t c) -> p t c",
                                                                               t=KD)).then_inc(cauchy_read, 1)
            dve.wait_ge(cauchy_read, 1)
            wr, wi = omc[:, 0, :], omc[:, 1, :]

            def c(i):
                return cs[:, i, :]

            def a(i):
                return A[:, :, i], A[:, :, 4 + i]

            def cmul(o, u, v, t):
                nc.vector.tensor_tensor(c(t), u[0], v[0], ALU.mult)
                nc.vector.tensor_tensor(c(t + 1), u[1], v[1], ALU.mult)
                nc.vector.tensor_tensor(c(t + 2), u[0], v[1], ALU.mult)
                link(nc.vector.tensor_tensor(c(t + 3), u[1], v[0], ALU.mult))
                nc.vector.tensor_tensor(c(o), c(t), c(t + 1), ALU.subtract)
                link(nc.vector.tensor_tensor(c(o + 1), c(t + 2), c(t + 3), ALU.add))
                return c(o), c(o + 1)

            den = cmul(0, (wr, wi), a(3), 8)
            link(nc.vector.tensor_scalar(c(0), c(0), 1.0, None, ALU.add))
            num = cmul(2, a(1), a(2), 8)
            num = cmul(4, num, (wr, wi), 8)
            nc.vector.tensor_tensor(c(8), den[0], den[0], ALU.mult)
            link(nc.vector.tensor_tensor(c(9), den[1], den[1], ALU.mult))
            link(nc.vector.tensor_tensor(c(8), c(8), c(9), ALU.add))
            link(nc.vector.reciprocal(c(8), c(8)))
            nc.vector.tensor_tensor(c(0), den[0], c(8), ALU.mult)
            link(nc.vector.scalar_tensor_tensor(c(1), den[1], -1.0, c(8), ALU.mult, ALU.mult))
            quo = cmul(6, num, den, 8)
            nc.vector.tensor_tensor(c(8), a(0)[0], quo[0], ALU.subtract)
            link(nc.vector.tensor_tensor(c(9), a(0)[1], quo[1], ALU.subtract))
            link(nc.vector.tensor_scalar(cs[:, 8:10, :], cs[:, 8:10, :], 2.0 / DM, None, ALU.mult))

        def phases():
            dve.wait_ge(tab_loaded, 16)
            for t in range(KD):
                re, im = cs[:, 8, t:t + 1], cs[:, 9, t:t + 1]
                nc.vector.tensor_scalar(s4[:, 6, 0:P], cos_t[:, t, 0:P], re, None, ALU.mult)
                link(nc.vector.tensor_scalar(s4[:, 6, P:2 * P], cos_t[:, t, 0:P], im, None, ALU.mult))
                nc.vector.scalar_tensor_tensor(uv[:, 0, t], sin_t[:, t, 0:P], im, s4[:, 6, 0:P], ALU.mult, ALU.add)
                link(nc.vector.scalar_tensor_tensor(uv[:, 1, t], sin_t[:, t, 0:P], re, s4[:, 6, P:2 * P],
                                                    ALU.mult, ALU.subtract))
            dve.sem_inc(uv_done, 1)

        def toeplitz():
            dve.wait_ge(toep_done, 1)
            nc.vector.tensor_copy(s4[:, 5, :], banks[:, G + 1, :]).then_inc(toep_copied, 1)
            dve.wait_ge(toep_masked, 1)
            nc.vector.tensor_copy(s4[:, 6, P:], s4[:, 5, P:])
            nc.vector.scalar_tensor_tensor(s4[:, 6, 0:P], ident[:, :], dsk[:, 0:1], s4[:, 5, 0:P],
                                           ALU.mult, ALU.add).then_inc(toep_ready, 1)
            dve.wait_ge(toep_ready, 2)
            nc.vector.tensor_tensor(toep_lo[:, P:], s4[:, 6, :], as_f32(toep_hi[:, P:]),
                                    ALU.subtract).then_inc(toep_ready, 1)

        def residual(half):
            for t in range(half * TH, half * TH + TH):
                dve.wait_ge(y_done, t + 1)
                ins = nc.vector.tensor_tensor(acc[:, t, :], acc[:, t, :], banks[:, D + t % TH, :], ALU.add)
                ins.then_inc(x1_done, 1)
            dve.wait_ge(x1_done, half * TH + TH)

        def linear_add(n):
            t, bank = n, G + 2 * (n % 2)
            dve.wait_ge(hg_done, n + 1)
            dve.wait_ge(bias_added, n + 1)
            nc.vector.tensor_tensor(acc[:, t, 0:CUT], acc[:, t, 0:CUT], banks[:, bank, 0:CUT], ALU.add)
            nc.vector.tensor_tensor(acc[:, t, CUT:DM], acc[:, t, CUT:DM], banks[:, bank + 1, 0:DM - CUT],
                                    ALU.add).then_inc(base_added, 1)

        def gates(half):
            dve.wait_ge(hg_done, half * TH + TH)
            logits = hg[:, :, ER:ER + NE]

            def wide(i):
                return gt[:, i, :].unsqueeze(2).broadcast_to([P, TH, NE])
            link(nc.vector.tensor_reduce(gt[:, 2, :], logits, AX_X, ALU.max))
            nc.vector.tensor_tensor(ge, logits, wide(2), ALU.subtract).then_inc(ge_in, 1)
            nc.vector.tensor_scalar(gt[:, 0, :], hg[:, :, ER + NE], dsk[:, 1:2], None, ALU.add).then_inc(ge_in, 1)
            dve.wait_ge(ge_done, 2 * half + 2)
            nc.vector.tensor_reduce(gt[:, 3, :], ge, AX_X, ALU.add)
            link(nc.vector.tensor_scalar(gt[:, 4, :], gt[:, 1, :], 1.0, None, ALU.add))
            nc.vector.reciprocal(gt[:, 5, :], gt[:, 3, :])
            link(nc.vector.reciprocal(gt[:, 6, :], gt[:, 4, :]))
            nc.vector.tensor_tensor(gw, ge, wide(5), ALU.mult)
            link(nc.vector.tensor_scalar(gt[:, 6, :], gt[:, 6, :], MAX_THRESHOLD, None, ALU.mult))
            link(nc.vector.tensor_tensor(gw, gw, wide(6), ALU.subtract))
            link(nc.vector.tensor_scalar(gw, gw, 0.0, None, ALU.max))
            link(nc.vector.tensor_reduce(gt[:, 7, :], gw, AX_X, ALU.add))
            link(nc.vector.tensor_scalar(gt[:, 8, :], gt[:, 7, :], 0.0, None, ALU.is_equal))
            link(nc.vector.tensor_tensor(gt[:, 7, :], gt[:, 7, :], gt[:, 8, :], ALU.add))
            link(nc.vector.reciprocal(gt[:, 9, :], gt[:, 7, :]))
            link(nc.vector.tensor_scalar(gt[:, 9, :], gt[:, 9, :], SCALING, None, ALU.mult))
            link(nc.vector.tensor_tensor(gw, gw, wide(9), ALU.mult))
            if half:
                dve.wait_ge(hwT_done, TH)
            for t in range(TH):
                ins = nc.vector.tensor_tensor(hw[:, t, :].rearrange("p (e r) -> p e r", e=NE),
                                              hg[:, t, 0:ER].rearrange("p (e r) -> p e r", e=NE),
                                              gw[:, t, :].unsqueeze(2).broadcast_to([P, NE, RANK]), ALU.mult)
            ins.then_inc(hw_done, 1)

        def experts_add(half):
            for t in range(TH):
                n = half * TH + t
                dve.wait_ge(hwT_hi_done, n + 1)
                nc.vector.tensor_tensor(hwT_lo[:, t % 2], banks[:, D + t % 2, 0:P],
                                        as_f32(hwT_hi[:, t % 2]), ALU.subtract).then_inc(hwT_lo_done, 1)
                if t:
                    expert_out(n - 1)
            expert_out(half * TH + TH - 1)

        def expert_out(n):
            dve.wait_ge(moe_done, n + 1)
            nc.vector.tensor_tensor(acc[:, n, :], acc[:, n, :], banks[:, D + 2 + n % 2, :],
                                    ALU.add).then_inc(moe_added, 1)

        norm(0, 0)
        for t in range(TH):
            xT_evac(t, D + t)
        ffn(0, {1: step_size, 2: cauchy_d, 3: cauchy_inverse, 4: cauchy_numerators, 5: roots})
        phases()
        norm(1, 1)
        for t in range(TH, NT):
            xT_evac(t, G + t - TH)
        toeplitz()
        residual(0)
        ffn(1, {})
        norm(2, 0)
        for t in range(TH):
            xT_evac(NT + t, G + t)
        residual(1)
        norm(3, 1)
        for n in range(2):
            linear_add(n)
        for t in range(TH, NT):
            xT_evac(NT + t, D + t - TH)
        for n in range(2, TH):
            linear_add(n)
        gates(0)
        for n in range(TH, NT):
            linear_add(n)
        experts_add(0)
        gates(1)
        ahead()
        experts_add(1)

    def tensor_program(pe, ahead):
        def transposes(n, bank):
            pe.wait_ge(xn_done, n + 1)
            for k in range(KD):
                ins = nc.tensor.transpose(banks[:, bank, k * P:(k + 1) * P],
                                          work[:, n % TH, k * P:(k + 1) * P], ident[:, :])
            ins.then_inc(xT_done, 1)

        def gate_up(half):
            def tile(f, i, seen):
                n = seen * 2 + i
                pe.wait_ge(gu_ready, n + 3)
                pe.wait_ge(h_done, n + 1)
                for m in range(2):
                    for k in range(KD):
                        cols = slice(half * HALF, (half + 1) * HALF)
                        ins = matmul3(nc, banks[:, G + 2 * i + m], gu_hi[:, i, m, k], gu_lo[:, i, m, k],
                                      xT_hi[:, k, cols], xT_lo[:, k, cols], k == 0, k == KD - 1)
                ins.then_inc(gu_used, 1)
            return tile

        def down(half, chunks):
            for c in chunks:
                n = half * NF + c
                pe.wait_ge(wd_ready, n + 1)
                pe.wait_ge(h_lo_done, n + 1)
                for t in range(TH):
                    cols = slice(t * P, (t + 1) * P)
                    ins = matmul3(nc, banks[:, D + t], hT_hi[:, c, cols], hT_lo[:, c, cols],
                                  wd_hi[:, n % 2], wd_lo[:, n % 2], c == 0, False)
                ins.then_inc(wd_used, 1)

        def convolve(half):
            pe.wait_ge(toep_ready, 3)
            for t in range(half * TH, half * TH + TH):
                cols = slice(t * P, (t + 1) * P)
                for j in range(KD):
                    lo = min(j * P, DM - 2 * P)
                    src = slice(P + lo - j * P, P + DM - j * P)
                    ins = matmul3(nc, banks[:, D + t % TH, lo:DM], xT_hi[:, j, cols], xT_lo[:, j, cols],
                                  toep_hi[:, src], toep_lo[:, src], False, j == KD - 1)
                ins.then_inc(y_done, 1)

        def linear(n):
            cols = slice(n * P, (n + 1) * P)
            bank = G + 2 * (n % 2)
            pe.wait_ge(comb_ready, KD)
            pe.wait_ge(xT_lo_done, NT + max(n + 1, TH))
            if n >= 2:
                pe.wait_ge(base_added, n - 1)
            for b, part in ((bank, slice(0, CUT)), (bank + 1, slice(CUT, WC))):
                for k in range(KD):
                    ins = matmul3(nc, banks[:, b, 0:part.stop - part.start], xT_hi[:, k, cols], xT_lo[:, k, cols],
                                  wc_hi[:, k, part], wc_lo[:, k, part], k == 0, k == KD - 1)
            ins.then_inc(base_done, 1)

        def experts(half):
            for t in range(TH + 1):
                n = half * TH + t
                if t < TH:
                    pe.wait_ge(hw_done, half + 1)
                    if n >= 2:
                        pe.wait_ge(hwT_lo_done, n - 1)
                    nc.tensor.transpose(banks[:, D + t % 2, 0:P], hw[:, t, :], ident[:, :]).then_inc(hwT_done, 1)
                if t:
                    expert_product(n - 1)

        def expert_product(n):
            i = n % 2
            pe.wait_ge(hwT_lo_done, n + 1)
            pe.wait_ge(comb_ready, KD + 1)
            if n >= 2:
                pe.wait_ge(moe_added, n - 1)
            matmul3(nc, banks[:, D + 2 + i], hwT_hi[:, i], hwT_lo[:, i], wb_hi[:, :], wb_lo[:, :],
                    True, True).then_inc(moe_done, 1)

        pe.wait_ge(ident_loaded, 16)
        for t in range(TH):
            transposes(t, D + t)
        pe.wait_ge(xT_lo_done, TH)
        ffn_tiles(pe, 0, gate_up(0), 0, 5)
        pe.wait_ge(cauchy_in, 1)
        for t in range(KD):
            out = banks[:, D, 8 * t:8 * t + 8]
            nc.tensor.matmul(out, s4[0:NS, 3, t * P:(t + 1) * P], vv[:, 0:8], start=True, stop=False)
            ins = nc.tensor.matmul(out, s4[0:NS, 4, t * P:(t + 1) * P], vv[:, 8:16], start=False, stop=True)
        ins.then_inc(cauchy_done, 1)
        ffn_tiles(pe, 0, gate_up(0), 5, 6)
        pe.wait_ge(cauchy_read, 1)
        down(0, range(0, 4))
        for t in range(TH, NT):
            transposes(t, G + t - TH)
        pe.wait_ge(xT_lo_done, NT)
        pe.wait_ge(uv_done, 1)
        for i, table in enumerate((cos_t, sin_t)):
            for t in range(KD):
                ins = nc.tensor.matmul(banks[:, G + 1, :], uv[:, i, t], table[:, t, :],
                                       start=i + t == 0, stop=i * KD + t == 2 * KD - 1)
        ins.then_inc(toep_done, 1)
        down(0, range(4, NF))
        convolve(0)
        ffn_tiles(pe, 1, gate_up(1), 0, 6)
        pe.wait_ge(x1_done, TH)
        down(1, range(0, 6))
        for t in range(TH):
            transposes(NT + t, G + t)
        down(1, range(6, NF))
        convolve(1)
        for n in range(2):
            linear(n)
        pe.wait_ge(x1_done, NT)
        for t in range(TH, NT):
            transposes(NT + t, D + t - TH)
        for n in range(2, NT):
            linear(n)
        experts(0)
        pe.wait_ge(base_added, NT)
        ahead()
        experts(1)

    return sync_program, gpsimd_program, scalar_program, vector_program, tensor_program


def attention(nc, sem, shared, ins, late_sb, attention_sb):
    acc, xT_hi, xT_lo, ident, ident_dram, banks, y_done = shared
    w_qk, w_v, w_o, mask_dram, out = ins
    oT_hi, oT_lo, wo_hi, wo_lo = late_sb
    (qT_hi, qT_lo, kT_hi, kT_lo, v_hi, v_lo, q_full, k_full, v_full, p_full, wqk_stage, wvo_stage, wqk_hi, wqk_lo,
     wv_hi, wv_lo, prob, pT_hi, pT_lo, mask, top, total, inv) = attention_sb
    G, S, T, O = 0, 4, 6, 7

    mask_loaded = sem("mask_loaded")
    qk_loaded = [sem(f"qk_loaded{i}") for i in range(RING)]
    vo_loaded = [sem(f"vo_loaded{i}") for i in range(RING)]
    qk_ready = sem("qk_ready")
    vo_ready = sem("vo_ready")
    unit_free = sem("unit_free")
    oT_ready = sem("oT_ready")
    QK0, VO0, FREE0, OT0 = 2 * RING, RING, GBANKS, 1
    credit_given = sem("credit_given")
    split_hi = sem("split_hi")
    unit_done = sem("unit_done")
    unit_hi = sem("unit_hi")
    s_done = sem("s_done")
    s_top = sem("s_top")
    exp_done = sem("exp_done")
    inv_done = sem("inv_done")
    norm_done = sem("norm_done")
    t_done = sem("t_done")
    pT_hi_done = sem("pT_hi_done")
    pT_ready = sem("pT_ready")
    o_done = sem("o_done")
    oT_hi_done = sem("oT_hi_done")
    out_done = sem("out_done")
    wait_passed = sem("wait_passed_2")

    NA = len(AHEAD)
    JV = KD

    def is_split(step):
        return step[0] in "QK" or step[0] == "V" and step[1] % 2 == 0

    n_split_units = sum(map(is_split, units(GROUP)))

    def unit(steps, step):
        return NA + units(steps).index(step) + 1

    def split_unit(steps, step):
        return len(list(filter(is_split, AHEAD))) + list(filter(is_split, units(steps))).index(step) + 1

    def vo_piece(kind, n):
        return JV + n + GH * (kind == "v")

    def unit_bank(n):
        return banks[:, G + (n - 1) % GBANKS]

    def groups(eng, body, steps, last):
        with eng.Fori(0, NG - 1) as g:
            body(g, steps)
        body(NG - 1, last)

    def unit_parts(step, bank):
        if step[0] == "V":
            b = step[1] // 2 % BATCH
            return (bank, v_hi[:, b], v_lo[:, b]), None
        two = slice(2 * step[2], 2 * step[2] + 2)
        tiles = bank.rearrange("p (b r n) -> p b r n", b=2, r=2)
        if step[0] == "Q":
            return (tiles[:, :, 1], qT_hi[:, two], qT_lo[:, two]), (tiles[:, :, 0], q_full[:, two])
        cols = slice(step[2] * HALF, (step[2] + 1) * HALF)
        return (bank, kT_hi[:, cols], kT_lo[:, cols]), (tiles[:, :, 0], k_full[:, two])

    def row_tiles(p):
        yield 0, prob[:, p % 2, 0:P], banks[:, S + p % 2, 0:P], mask[:, P:2 * P]
        yield 1, prob[:, p % 2, P:3 * P], banks[:, S + p % 2, 2 * P:4 * P], mask[:, :]

    def sync_program(sp):
        sp.wait_ge(credit_given, 1)
        sp.wait_ge(y_done, NT)
        sp.dma_start(wqk_stage[:, 0], w_qk[0]).then_inc(qk_loaded[0], 16)
        sp.dma_start(mask[:, :], mask_dram).then_inc(mask_loaded, 16)

        def load_vo(g, j, src):
            sp.wait_ge(vo_ready, g * NVO + j - RING + 1 + VO0)
            sp.dma_start(wvo_stage[:, j % RING], src).then_inc(vo_loaded[j % RING], 16)

        for k in range(KD):
            load_vo(0, k, w_v[0, k])

        def load(g, splits):
            for kind, n in splits:
                if kind == "q":
                    sp.wait_ge(qk_ready, g * NQK + 2 * (n - RING) + 2 + QK0)
                    sp.dma_start(wqk_stage[:, n % RING], w_qk[g * GH + n]).then_inc(qk_loaded[n % RING], 16)
                elif kind in "vo":
                    load_vo(g, vo_piece(kind, n), w_v[g + 1, n] if kind == "v" else w_o[g * GH + n])

        groups(sp, load, SPLITS, LAST_SPLITS)
        for t in range(NT):
            sp.wait_ge(unit_free, (NG - 1) * NU + unit(LAST_GROUP, ("B", t)) + FREE0)
            sp.dma_start(out[t * P:(t + 1) * P, :], acc[:, t, :]).then_inc(out_done, 16)
        sp.wait_ge(out_done, 16 * NT)

    def gpsimd_program(pool):
        def split(src, hi, lo, count, ready):
            nc.gpsimd.tensor_scalar(hi, src, 1.0, 1.0, ALU.mult, ALU.mult).then_inc(split_hi, 1)
            pool.wait_ge(split_hi, count)
            nc.gpsimd.tensor_tensor(lo, src, as_f32(hi), ALU.subtract).then_inc(ready, 1)

        pool.wait_ge(qk_loaded[0], 16)
        for m in range(2):
            split(wqk_stage[:, 0, m], wqk_hi[:, 0, m], wqk_lo[:, 0, m], m + 1, qk_ready)
        for k in range(KD):
            pool.wait_ge(vo_loaded[k % RING], 16 * (k // RING + 1))
            split(wvo_stage[:, k % RING], wv_hi[:, k], wv_lo[:, k], 2 + k + 1, vo_ready)

        def group(g, splits):
            pieces = 2 + KD
            for kind, n in splits:
                if kind == "N":
                    i = n % 2
                    pool.wait_ge(inv_done, g * PAIRS + n + 1)
                    pool.sem_inc(wait_passed, 1)
                    nc.gpsimd.tensor_scalar(prob[:, i, 0:P], prob[:, i, 0:P], inv[:, i, 0:1], 1.0,
                                            ALU.mult, ALU.mult)
                    nc.gpsimd.tensor_scalar(prob[:, i, P:3 * P], prob[:, i, P:3 * P], inv[:, i, 1:2], 1.0,
                                            ALU.mult, ALU.mult).then_inc(norm_done, 1)
                    continue
                if kind in "qk":
                    i, m = n % RING, "qk".index(kind)
                    pool.wait_ge(qk_loaded[i], g * (16 * GH // RING) + 16 * (n // RING + 1))
                    src, hi, lo, ready = wqk_stage[:, i, m], wqk_hi[:, i, m], wqk_lo[:, i, m], qk_ready
                else:
                    j = vo_piece(kind, n)
                    pool.wait_ge(vo_loaded[j % RING], g * (16 * NVO // RING) + 16 * (j // RING + 1))
                    hi, lo = (wv_hi, wv_lo) if kind == "v" else (wo_hi, wo_lo)
                    src, hi, lo, ready = wvo_stage[:, j % RING], hi[:, n], lo[:, n], vo_ready
                pool.sem_inc(wait_passed, 1)
                pieces += 1
                split(src, hi, lo, g * (NQK + NVO) + pieces, ready)

        groups(pool, group, SPLITS, LAST_SPLITS)

    def unit_evac_hi(act, n, g, step):
        (src, hi, _), whole = unit_parts(step, unit_bank(n))
        act.wait_ge(unit_done, g * NU + n)
        if whole:
            nc.scalar.activation(whole[1], whole[0], ACT.Copy)
        nc.scalar.activation(hi, src, ACT.Copy).then_inc(unit_hi, 1)

    def unit_evac_lo(dve, n, split_n, g, step):
        (src, hi, lo), _ = unit_parts(step, unit_bank(n))
        dve.wait_ge(unit_hi, g * n_split_units + split_n)
        nc.vector.tensor_tensor(lo, src, as_f32(hi), ALU.subtract).then_inc(unit_free, 1)

    def v_evac(dve, n, g, step):
        dve.wait_ge(unit_done, g * NU + n)
        nc.vector.tensor_copy(v_full[:, step[1] // 2 % BATCH], unit_bank(n)).then_inc(unit_free, 1)

    def scalar_ahead(act):
        for n, step in enumerate(AHEAD, 1):
            if is_split(step):
                unit_evac_hi(act, n, 0, step)

    def vector_ahead(dve):
        for n, step in enumerate(AHEAD, 1):
            if is_split(step):
                unit_evac_lo(dve, n, n, 0, step)
            else:
                v_evac(dve, n, 0, step)

    def tensor_ahead(pe):
        for n, step in enumerate(AHEAD, 1):
            if step[0] == "V":
                values_or_output(pe, n, 0, step)
            else:
                project(pe, n, 0, step)

    def scalar_program(act):
        def exps(g, p):
            act.wait_ge(s_top, g * PAIRS + p + 1)
            for r, pr, _, _ in row_tiles(p):
                ins = nc.scalar.activation(pr, pr, ACT.Exp, bias=top[:, p % 2, r:r + 1], scale=-1.0,
                                           accum_out=total[:, p % 2, r:r + 1])
            ins.then_inc(exp_done, 1)

        def group(g, steps):
            for step in steps:
                if step == ("S", 0):
                    exps(g, 0)
                elif is_split(step):
                    unit_evac_hi(act, unit(steps, step), g, step)
                elif step[0] == "T":
                    p = step[1]
                    act.wait_ge(t_done, g * PAIRS + p + 1)
                    nc.scalar.activation(p_full[:, p % 2], banks[:, T, 2 * P:3 * P], ACT.Copy)
                    nc.scalar.activation(pT_hi[:, p % 2], banks[:, T, 0:2 * P], ACT.Copy).then_inc(pT_hi_done, 1)
                    if p + 1 < PAIRS:
                        exps(g, p + 1)
                elif step[0] == "O" and step[1] % 2:
                    h, half = step[1] // BATCH, step[1] % BATCH // 2
                    act.wait_ge(o_done, g * PAIRS + step[1] + 1)
                    nc.scalar.activation(oT_hi[:, h, half * HALF:(half + 1) * HALF], banks[:, O],
                                         ACT.Copy).then_inc(oT_hi_done, 1)

        groups(act, group, GROUP, LAST_GROUP)

    def vector_program(dve):
        def inverse(g, p):
            dve.wait_ge(exp_done, g * PAIRS + p + 1)
            nc.vector.reciprocal(inv[:, p % 2, :], total[:, p % 2, :]).then_inc(inv_done, 1)

        def group(g, steps):
            for step in steps:
                if step[0] == "S":
                    p = step[1]
                    dve.wait_ge(s_done, g * PAIRS + p + 1)
                    dve.sem_inc(wait_passed, 1)
                    for r, pr, sc, ma in row_tiles(p):
                        ins = nc.vector.tensor_tensor_reduce(out=pr, in0=sc, in1=ma, scale=-QK_SCALE, scalar=3e38,
                                                             op0=ALU.add, op1=ALU.min,
                                                             accum_out=top[:, p % 2, r:r + 1])
                    ins.then_inc(s_top, 1)
                    if p == 0:
                        inverse(g, 0)
                elif is_split(step):
                    unit_evac_lo(dve, unit(steps, step), split_unit(steps, step), g, step)
                elif step[0] == "V":
                    v_evac(dve, unit(steps, step), g, step)
                elif step[0] in "WAB":
                    t, n = step[1], unit(steps, step)
                    dve.wait_ge(unit_done, g * NU + n)
                    nc.vector.tensor_tensor(acc[:, t, :], acc[:, t, :], unit_bank(n), ALU.add).then_inc(unit_free, 1)
                elif step[0] == "T":
                    p = step[1]
                    dve.wait_ge(pT_hi_done, g * PAIRS + p + 1)
                    nc.vector.tensor_tensor(pT_lo[:, p % 2], banks[:, T, 0:2 * P],
                                            as_f32(pT_hi[:, p % 2]), ALU.subtract).then_inc(pT_ready, 1)
                    if p + 1 < PAIRS:
                        inverse(g, p + 1)
                elif step[0] == "O" and step[1] % 2:
                    h, half = step[1] // BATCH, step[1] % BATCH // 2
                    cols = slice(half * HALF, (half + 1) * HALF)
                    dve.wait_ge(oT_hi_done, g * (PAIRS // 2) + step[1] // 2 + 1)
                    nc.vector.tensor_tensor(oT_lo[:, h, cols], banks[:, O], as_f32(oT_hi[:, h, cols]),
                                            ALU.subtract).then_inc(oT_ready, 1)

        dve.wait_ge(mask_loaded, 16)
        groups(dve, group, GROUP, LAST_GROUP)

    def project(pe, n, g, step):
        kind, h, half = step
        m, cols = "QK".index(kind), slice(half * HALF, (half + 1) * HALF)
        pe.wait_ge(unit_free, g * NU + n - GBANKS + FREE0)
        pe.wait_ge(qk_ready, g * NQK + 2 * h + m + 1 + QK0)
        for k in range(KD):
            ins = matmul3(nc, unit_bank(n), wqk_hi[:, h % RING, m, k], wqk_lo[:, h % RING, m, k],
                          xT_hi[:, k, cols], xT_lo[:, k, cols], k == 0, k == KD - 1)
        ins.then_inc(unit_done, 1)

    def values_or_output(pe, u, g, step):
        kind, n = step
        cols = slice(n % NT * P, (n % NT + 1) * P)
        pe.wait_ge(unit_free, g * NU + u - GBANKS + FREE0)
        heads = range(GH)
        if kind == "V":
            if n in (0, 1, NT, NT + 1):
                pe.wait_ge(vo_ready, g * NVO + (vo_piece("v", KD - 1) + 1 if n >= NT else KD) + VO0)
            left, right = (xT_hi, xT_lo), (wv_hi, wv_lo)
        else:
            pe.wait_ge(vo_ready, g * NVO + vo_piece("o", GH - 1) + 1 + VO0)
            heads = {"W": range(GH), "A": range(GH - 1), "B": range(GH - 1, GH)}[kind]
            pe.wait_ge(oT_ready, g * (PAIRS // 2) + (heads.stop - 1) * (BATCH // 2) + 1 + (n >= TH) + OT0)
            left, right = (oT_hi, oT_lo), (wo_hi, wo_lo)
        for k in heads:
            ins = matmul3(nc, unit_bank(u), left[0][:, k, cols], left[1][:, k, cols],
                          right[0][:, k], right[1][:, k], k == heads.start, k == heads.stop - 1)
        ins.then_inc(unit_done, 1)

    def tensor_program(pe):
        def group(g, steps):
            for step in steps:
                kind, n = step[0], step[1]
                if kind in "QK":
                    project(pe, unit(steps, step), g, step)
                elif kind in "VWAB":
                    values_or_output(pe, unit(steps, step), g, step)
                elif kind == "S":
                    h, b = n // BATCH, n % BATCH
                    if n and b % 2 == 0:
                        last = max(unit(steps, ("Q", h, b // 2)), unit(steps, ("K", h, b // 2)))
                        pe.wait_ge(unit_free, g * NU + last + FREE0)
                    keys = slice(b * SEQ, (b + 1) * SEQ)
                    nc.tensor.matmul(banks[:, S + n % 2, 0:P], q_full[:, b], k_full[:, b], start=True, stop=True)
                    ins = matmul3(nc, banks[:, S + n % 2, 2 * P:4 * P], qT_hi[:, b], qT_lo[:, b],
                                  kT_hi[:, keys], kT_lo[:, keys], True, True)
                    ins.then_inc(s_done, 1)
                elif kind == "T":
                    pe.wait_ge(norm_done, g * PAIRS + n + 1)
                    for block in range(3):
                        part = slice(block * P, (block + 1) * P)
                        ins = nc.tensor.transpose(banks[:, T, part], prob[:, n % 2, part], ident[:, :])
                    ins.then_inc(t_done, 1)
                elif kind == "O":
                    h, b = n // BATCH, n % BATCH
                    pe.wait_ge(pT_ready, g * PAIRS + n + 1)
                    if h == 0:
                        pe.wait_ge(unit_free, g * NU + (unit(steps, ("V", 2 * b + 1)) if b else NA) + FREE0)
                    if n % 2 == 0:
                        pe.wait_ge(oT_ready, g * (PAIRS // 2) + n // 2 + OT0)
                    cols = slice(b % 2 * SEQ, (b % 2 + 1) * SEQ)
                    d = slice(h * DH, (h + 1) * DH)
                    matmul3(nc, banks[:, O, cols], v_hi[:, b, d], v_lo[:, b, d], pT_hi[:, n % 2], pT_lo[:, n % 2],
                            True, False)
                    ins = nc.tensor.matmul(banks[:, O, cols.start + P:cols.stop], v_full[:, b, d], p_full[:, n % 2],
                                           start=False, stop=True)
                    ins.then_inc(o_done, 1)

        pe.wait_ge(unit_free, 2 + FREE0)
        groups(pe, group, GROUP, LAST_GROUP)

    def credits(dve):
        dve.sem_inc(qk_ready, QK0)
        dve.sem_inc(vo_ready, VO0)
        dve.sem_inc(unit_free, FREE0)
        dve.sem_inc(oT_ready, OT0)
        dve.sem_inc(credit_given, 1)

    return (sync_program, gpsimd_program, scalar_program, vector_program, tensor_program,
            scalar_ahead, vector_ahead, tensor_ahead, credits)


def build(nc, x, w_gu, w_down, lam, p_ri, q_ri, ct, vc, bp, d_skip, log_step, om_rows, om_cols, tables,
          w_comb, b_base, b_thr, w_expb, w_qk, w_v, w_o, identity, mask, out):
    with ExitStack() as ctx:
        def place(stack, *tensors):
            return [stack.enter_context(nc.sbuf_tensor(name, shape, dt)) for name, shape, dt in tensors]

        def split(name, shape):
            return (f"{name}_hi", shape, F32R), (f"{name}_lo", shape, F32R)

        def sem(name):
            return ctx.enter_context(nc.semaphore(name))

        acc, xT_hi, xT_lo, ident = place(ctx, ("acc", [P, NT, DM], F32), *split("xT", [P, KD, TOK]),
                                         ("ident", [P, P], F32))
        small_sb = place(ctx, ("vcs", [NS, 2 * NS], F32), ("bps", [NS, NS], F32), ("sm", [NS, 12], F32),
                         ("ex", [NS, 4], F32), ("exi", [NS, 1], mybir.dt.int32), ("bb", [NS, 8], F32),
                         ("vv", [NS, 16], F32), ("omc", [P, 2, KD], F32), ("cs", [P, 12, KD], F32),
                         ("A", [P, KD, 8], F32), ("dsk", [P, 2], F32), ("st", [P, TH, 6], F32),
                         ("mv", [P, TH, 2], F32), ("ln", [P, 4, TH], F32), ("gt", [P, 10, TH], F32))
        with ExitStack() as late:
            late_sb = place(late, *split("oT", [P, GH, TOK]), *split("wo", [P, GH, DM]))
        shared_bytes = 4 * 2 * (GH * TOK + GH * DM)
        expert_bytes = 4 * (2 * KD * WC + 2 * DM + 8 * DM + 2 * 2 * P)
        expert_sb = place(ctx, *split("wc", [P, KD, WC]), *split("wb", [P, DM]), ("s4", [P, 8, DM], F32),
                          *split("hwT", [P, 2, P]), ("uv", [P, (shared_bytes - expert_bytes) // 4], F32))
        with ExitStack() as early:
            ffn_sb = place(early, *split("hT", [P, NF, HALF]), ("gu_stage", [P, 2, 2, KD, P], F32),
                           *split("gu", [P, 2, 2, KD, P]), ("wd_stage", [P, 2, DM], F32), *split("wd", [P, 2, DM]),
                           ("work", [P, 4, DM], F32), *split("toep", [P, P + DM]),
                           ("tab", [P, 2 * KD * DM], F32))
        attention_sb = place(ctx, *split("qT", [P, BATCH, P]), *split("kT", [P, TOK]),
                             *split("v", [P, BATCH, GH * DH]), ("q_full", [P, BATCH, P], F32),
                             ("k_full", [P, BATCH, P], F32), ("v_full", [P, BATCH, GH * DH], F32),
                             ("p_full", [P, 2, P], F32),
                             ("wqk_stage", [P, RING, 2, KD, DH], F32), ("wvo_stage", [P, RING, DM], F32),
                             *split("wqk", [P, RING, 2, KD, DH]), *split("wv", [P, KD, GH * DH]),
                             ("prob", [P, 2, 3 * P], F32),
                             *split("pT", [P, 2, 2 * P]), ("mask", [P, 2 * P], F32),
                             ("top", [P, 2, 2], F32), ("total", [P, 2, 2], F32), ("inv", [P, 2, 2], F32))
        banks = ctx.enter_context(nc.psum_tensor("banks", [P, 8, DM], F32))
        shared = (acc, xT_hi, xT_lo, ident, identity, banks, sem("y_done"))

        (sync_0, gpsimd_0, scalar_0, vector_0, tensor_0) = layer0(
            nc, sem, shared, (x, w_gu, w_down, lam, p_ri, q_ri, ct, vc, bp, d_skip, log_step, om_rows, om_cols,
                              tables, w_comb, b_base, b_thr, w_expb), ffn_sb, expert_sb, small_sb)
        (sync_1, gpsimd_1, scalar_1, vector_1, tensor_1, scalar_ahead, vector_ahead, tensor_ahead,
         credits) = attention(nc, sem, shared, (w_qk, w_v, w_o, mask, out), late_sb, attention_sb)

        block = ctx.enter_context(nc.Block())

        @block.sync
        def _(sp):
            sync_0(sp)
            sync_1(sp)

        @block.gpsimd
        def _(pool):
            gpsimd_0(pool)
            gpsimd_1(pool)

        @block.scalar
        def _(act):
            scalar_0(act, lambda: scalar_ahead(act))
            scalar_1(act)

        @block.vector
        def _(dve):
            credits(dve)
            vector_0(dve, lambda: vector_ahead(dve))
            vector_1(dve)

        @block.tensor
        def _(pe):
            tensor_0(pe, lambda: tensor_ahead(pe))
            tensor_1(pe)


def constants():
    import numpy as np
    f = np.arange(DM)
    w = np.exp(-2j * np.pi * f / DM)
    om_rows = np.stack([1 - w.real, 1 + w.real, w.imag]).astype(np.float32)
    om_cols = np.stack([1 + w.real, w.imag]).astype(np.float32).reshape(2, KD, P).transpose(2, 0, 1)
    turn = 2 * np.pi * (f[:, None] * f[None, :] % DM) / DM
    tables = np.stack([np.cos(turn), np.sin(turn)]).astype(np.float32)
    tables = tables.reshape(2, KD, P, DM).transpose(2, 0, 1, 3).reshape(P, 2 * KD * DM)
    mask = np.zeros((P, 2 * P), np.float32)
    mask[:, P:][np.triu_indices(P, 1)] = NEG
    return {"om_rows": om_rows, "om_cols": om_cols, "tables": tables, "identity": np.eye(P, dtype=np.float32),
            "mask": mask}


def layout(a):
    import numpy as np

    def chunks(w, n):
        return w.reshape(KD, P, n, P).transpose(2, 1, 0, 3)

    pad = ((0, 0), (0, NF * P - FF))
    gate, up, down = (np.pad(w, pad) for w in (a["L0_ffn_W_gate"].T, a["L0_ffn_W_up"].T, a["L0_ffn_W_down"]))
    wq = a["L1_attn_wq"].reshape(DM, HEADS, 192)[:, :, :DH].reshape(DM, HEADS * DH)
    wk, wv = a["L1_attn_wkv"][:, :HEADS * DH], a["L1_attn_wkv"][:, HEADS * DH:2 * HEADS * DH]
    comb = np.concatenate([a["L1_ffn_W_base"], a["L1_ffn_A_w"].reshape(ER, DM), a["L1_ffn_W_gate"],
                           a["L1_ffn_W_thr"][None], np.zeros((1, DM), np.float32)])
    return {
        "x": a["L0_attn_u"].reshape(TOK, DM),
        "w_gu": np.stack([chunks(gate, NF), chunks(up, NF)], axis=2),
        "w_down": down.T.reshape(NF, P, DM),
        "lam": a["L0_attn_Lambda_ri"], "p_ri": a["L0_attn_p_ri"], "q_ri": a["L0_attn_q_ri"],
        "ct": a["L0_attn_Ct_ri"].reshape(NS, 2), "vc": a["L0_attn_Vc_ri"].transpose(0, 2, 1).reshape(NS, 2 * NS),
        "bp": a["L0_attn_Bp"].reshape(NS), "d_skip": a["L0_attn_D"], "log_step": a["L0_attn_log_step"],
        "w_comb": comb.T.reshape(KD, P, WC), "b_base": a["L1_ffn_b_base"], "b_thr": a["L1_ffn_b_thr"],
        "w_expb": a["L1_ffn_B_w"].transpose(0, 2, 1).reshape(ER, DM),
        "w_qk": np.stack([chunks(wq, HEADS), chunks(wk, HEADS)], axis=2),
        "w_v": wv.reshape(KD, P, NG, GH * DH).transpose(2, 0, 1, 3),
        "w_o": a["L1_attn_wo"].reshape(HEADS, DH, DM),
    }


ORDER = ["x", "w_gu", "w_down", "lam", "p_ri", "q_ri", "ct", "vc", "bp", "d_skip", "log_step", "om_rows", "om_cols",
         "tables", "w_comb", "b_base", "b_thr", "w_expb", "w_qk", "w_v", "w_o", "identity", "mask"]


def kernel(**inputs):
    import numpy as np
    import concourse.bacc as bacc
    from concourse.bass_utils import run_bass_kernel_spmd

    nc = bacc.Bacc("TRN2", target_bir_lowering=False, num_devices=1)
    data = {**layout({k: np.asarray(v) for k, v in inputs.items()}), **constants()}
    arrays, args = {}, []
    for name in ORDER:
        arrays[f"in_{name}"] = np.ascontiguousarray(data[name])
        args.append(nc.dram_tensor(f"in_{name}", arrays[f"in_{name}"].shape, F32, kind="ExternalInput").ap())
    out = nc.dram_tensor("out", (TOK, DM), F32, kind="ExternalOutput").ap()
    build(nc, *args, out)
    r = run_bass_kernel_spmd(nc, [arrays], core_ids=[0])
    return r.results[0]["out"].reshape(BATCH, SEQ, DM)
```

```python
from contextlib import ExitStack

import concourse.bass as bass
from concourse import mybir

P = 128
F32 = mybir.dt.float32
F32R = mybir.dt.float32r
ALU = mybir.AluOpType
ACT = mybir.ActivationFunctionType
AX_X = mybir.AxisListType.X

BATCH, SEQ, DM = 4, 256, 512
TOK = BATCH * SEQ
NT = TOK // P
KD = DM // P
HALF = TOK // 2
TH = NT // 2
FF = 1376
NF = (FF + P - 1) // P
NS = 64
FT = KD // 2
HEADS, DH = 32, 128
QK_SCALE = float(192) ** -0.5
GH = 4
NG = HEADS // GH
PAIRS = GH * BATCH
NE, RANK = 8, 16
ER = NE * RANK
WC = DM + ER + NE + 2
CUT = 384
EPS = 1e-5
NEG = -1e30
MAX_THRESHOLD, SCALING = 0.125, 2.0

AHEAD = [("Q", 0, 0), ("K", 0, 0), ("V", 0), ("V", 1)]
START = [("S", 0), ("Q", 0, 1), ("K", 0, 1),
         ("S", 1), ("T", 0), ("V", 2), ("V", 3), ("O", 0),
         ("S", 2), ("T", 1), ("Q", 1, 0), ("K", 1, 0), ("O", 1),
         ("S", 3), ("T", 2), ("V", 4), ("V", 5), ("Q", 1, 1), ("O", 2),
         ("S", 4), ("T", 3), ("V", 6), ("V", 7), ("K", 1, 1), ("O", 3)]
for _p, _unit in enumerate([("Q", 2, 0), ("K", 2, 0), ("Q", 2, 1), ("K", 2, 1),
                            ("Q", 3, 0), ("K", 3, 0), ("Q", 3, 1), ("K", 3, 1)], 5):
    START += [("S", _p), ("T", _p - 1), _unit, ("O", _p - 1)]
GROUP = START + [
    ("S", 13), ("T", 12), ("Q", 4, 0), ("O", 12),
    ("S", 14), ("T", 13), ("K", 4, 0), ("O", 13),
    ("S", 15), ("T", 14), ("V", 8), ("O", 14), ("W", 0), ("T", 15), ("V", 9), ("O", 15)] + [
    ("W", t) for t in range(1, NT)]
LAST_GROUP = START + [
    ("S", 13), ("T", 12), ("A", 0), ("O", 12),
    ("S", 14), ("T", 13), ("A", 1), ("A", 2), ("O", 13),
    ("S", 15), ("T", 14), ("A", 3), ("O", 14), ("A", 4), ("T", 15), ("A", 5), ("O", 15),
    ("A", 6), ("A", 7)] + [
    ("B", t) for t in range(NT)]


def units(steps):
    return [s for s in steps if s[0] in "QKVWAB"]


NU = len(units(GROUP))
GBANKS = 4
WARM_UP = 17, 10
SPLITS = [("q", 1), ("k", 1), ("N", 0), ("o", 0), ("N", 1), ("q", 2), ("N", 2), ("k", 2), ("N", 3), ("o", 1),
          ("N", 4), ("o", 2), ("N", 5), ("q", 3), ("N", 6), ("k", 3), ("N", 7), ("o", 3), ("N", 8), ("v", 0),
          ("N", 9), ("v", 1), ("N", 10), ("q", 4), ("N", 11), ("v", 2), ("N", 12), ("k", 4), ("N", 13), ("v", 3),
          ("N", 14), ("N", 15)]
LAST_SPLITS = [s for s in SPLITS if s[0] != "v" and s not in (("q", 4), ("k", 4))]
NQK = 2 * GH
NVO = GH + KD
RING = 2


def matmul3(nc, out, w_hi, w_lo, x_hi, x_lo, first, last):
    nc.tensor.matmul(out, w_hi, x_hi, start=first, stop=False)
    nc.tensor.matmul(out, w_hi, x_lo, start=False, stop=False)
    return nc.tensor.matmul(out, w_lo, x_hi, start=False, stop=last)


def as_f32(ap):
    return ap.bitcast(F32)


def layer0(nc, sem, shared, ins, ffn_sb, expert_sb, small_sb):
    acc, xT_hi, xT_lo, ident, ident_dram, banks, y_done = shared
    (x, w_gu, w_down, lam, p_ri, q_ri, ct, vc, bp, d_skip, log_step, om_rows, om_cols, tables,
     w_comb, b_base, b_thr, w_expb) = ins
    G, D = 0, 4

    (hT_hi, hT_lo, gu_stage, gu_hi, gu_lo, wd_stage, wd_hi, wd_lo, work, toep_hi, toep_lo, tab) = ffn_sb
    wc_hi, wc_lo, wb_hi, wb_lo, s4, hwT_hi, hwT_lo, _ = expert_sb
    vcs, bps, sm, ex, exi, bb, vv, omc, cs, A, dsk, st, mv, ln, gt = small_sb
    cos_t = tab[:, 0:FT * DM].rearrange("p (t l) -> p t l", t=FT)
    sin_t = tab[:, FT * DM:2 * FT * DM].rearrange("p (t l) -> p t l", t=FT)
    wc_stage = tab[:, 0:KD * WC].rearrange("p (k n) -> p k n", k=KD)
    wb_stage = tab[:, KD * WC:KD * WC + DM]
    bias = s4[:, 7, :]
    om = s4[0:NS, 0:3, :]
    uv = s4[:, 0, :].rearrange("p (a t j) -> p a t j", a=2, t=FT)
    hg = s4[:, 0:2, :].rearrange("p a b -> p (a b)")[:, 0:TH * (WC - DM)].rearrange("p (t n) -> p t n", t=TH)
    hw = s4[:, 2, :].rearrange("p (t n) -> p t n", t=TH)
    ge = s4[:, 3, 0:TH * NE].rearrange("p (t e) -> p t e", t=TH)
    gw = s4[:, 4, 0:TH * NE].rearrange("p (t e) -> p t e", t=TH)

    x_loaded = [sem(f"x_loaded{t}") for t in range(NT)]
    ident_loaded = sem("ident_loaded")
    gu_loaded = [sem(f"gu_loaded{i}") for i in range(2)]
    wd_loaded = [sem(f"wd_loaded{i}") for i in range(2)]
    s4_loaded = sem("s4_loaded")
    tab_loaded = sem("tab_loaded")
    wc_loaded = sem("wc_loaded")
    bias_loaded = sem("bias_loaded")
    gu_hi_done = sem("gu_hi_done")
    gu_ready = sem("gu_ready")
    gu_used = sem("gu_used")
    wait_passed = sem("wait_passed")
    silu_done = sem("silu_done")
    h_done = sem("h_done")
    h_hi_done = sem("h_hi_done")
    h_lo_done = sem("h_lo_done")
    wd_hi_done = sem("wd_hi_done")
    wd_ready = sem("wd_ready")
    wd_used = sem("wd_used")
    var_done = sem("var_done")
    sd_done = sem("sd_done")
    xn_done = sem("xn_done")
    xT_done = sem("xT_done")
    xT_hi_done = sem("xT_hi_done")
    xT_lo_done = sem("xT_lo_done")
    ones_set = sem("ones_set")
    zeros_set = sem("zeros_set")
    cauchy_in = sem("cauchy_in")
    cauchy_done = sem("cauchy_done")
    cauchy_read = sem("cauchy_read")
    uv_done = sem("uv_done")
    toep_done = sem("toep_done")
    toep_copied = sem("toep_copied")
    toep_masked = sem("toep_masked")
    toep_ready = sem("toep_ready")
    x1_done = sem("x1_done")
    comb_hi_done = sem("comb_hi_done")
    comb_ready = sem("comb_ready")
    base_done = sem("base_done")
    hg_done = sem("hg_done")
    base_added = sem("base_added")
    bias_added = sem("bias_added")
    ge_in = sem("ge_in")
    ge_done = sem("ge_done")
    hw_done = sem("hw_done")
    hwT_done = sem("hwT_done")
    hwT_hi_done = sem("hwT_hi_done")
    hwT_lo_done = sem("hwT_lo_done")
    moe_done = sem("moe_done")
    moe_added = sem("moe_added")
    dve_chain = sem("dve_chain")

    def linear_bank(n):
        return G + 2 * (n % 2) if n < NT - 2 else D + 2 * (n % 2)

    def expert_bank(n):
        return D + 1 + n % 3

    def ffn_tiles(eng, half, body, first=0, end=NF // 2 + 1):
        if first < min(end, NF // 2):
            with eng.Fori(first, min(end, NF // 2)) as it:
                for j in range(2):
                    n = half * NF + j
                    body(it * 2 + j, n % 2, it + n // 2)
        if end > NF // 2:
            n = half * NF + NF - 1
            body(NF - 1, n % 2, n // 2)

    def sync_program(sp):
        def load_x(t):
            sp.dma_start(acc[:, t, :], x[t * P:(t + 1) * P, :]).then_inc(x_loaded[t], 16)

        def load_gu(f, i, seen):
            sp.wait_ge(gu_ready, seen * 2 + i + 1)
            sp.dma_start(gu_stage[:, i], w_gu[f]).then_inc(gu_loaded[i], 16)

        for t in range(TH):
            load_x(t)
        sp.dma_start(ident[:, :], ident_dram).then_inc(ident_loaded, 16)
        ffn_tiles(sp, 0, load_gu, 0, 1)
        for t in range(TH, NT):
            load_x(t)
        for c, a in ((0, lam), (2, p_ri), (4, q_ri), (6, ct)):
            sp.dma_start(sm[:, c:c + 2], a).then_inc(s4_loaded, 16)
        sp.dma_start(sm[:, 8:9], log_step.partition_broadcast(NS)).then_inc(s4_loaded, 16)
        sp.dma_start(vcs[:, :], vc).then_inc(s4_loaded, 16)
        sp.dma_start(bps[:, :], bp.partition_broadcast(NS)).then_inc(s4_loaded, 16)
        sp.dma_start(om, om_rows.partition_broadcast(NS)).then_inc(s4_loaded, 16)
        sp.dma_start(omc[:, :, :], om_cols).then_inc(s4_loaded, 16)
        sp.dma_start(dsk[:, 0:1], d_skip.partition_broadcast(P)).then_inc(s4_loaded, 16)
        sp.dma_start(bias, b_base.partition_broadcast(P)).then_inc(bias_loaded, 16)
        sp.dma_start(dsk[:, 1:2], b_thr.partition_broadcast(P)).then_inc(bias_loaded, 16)
        ffn_tiles(sp, 0, load_gu, 1, 2)
        sp.dma_start(tab[:, 0:2 * FT * DM], tables).then_inc(tab_loaded, 16)
        for half in range(2):
            if half:
                ffn_tiles(sp, half, load_gu, 0, 2)
                sp.wait_ge(toep_done, 1)
                sp.dma_start(wc_stage, w_comb.rearrange("k p n -> p k n")).then_inc(wc_loaded, 16)
                sp.dma_start(wb_stage, w_expb).then_inc(wc_loaded, 16)
            ffn_tiles(sp, half, load_gu, 2)
            for c in range(NF):
                n = half * NF + c
                if n >= 2:
                    sp.wait_ge(wd_ready, n - 1)
                sp.dma_start(wd_stage[:, n % 2], w_down[c]).then_inc(wd_loaded[n % 2], 16)
        sp.wait_ge(comb_ready, KD + 1)
        sp.wait_ge(xT_done, 2 * NT)

    def gpsimd_program(pool):
        for half in range(2):
            def split_gu(f, i, seen):
                n = seen * 2 + i
                pool.wait_ge(gu_loaded[i], seen * 16 + 16)
                pool.wait_ge(gu_used, n + 1)
                pool.sem_inc(wait_passed, 1)
                nc.gpsimd.tensor_scalar(gu_hi[:, i], gu_stage[:, i], 1.0, 1.0,
                                        ALU.mult, ALU.mult).then_inc(gu_hi_done, 1)
                pool.wait_ge(gu_hi_done, n + 1)
                nc.gpsimd.tensor_tensor(gu_lo[:, i], gu_stage[:, i], as_f32(gu_hi[:, i]),
                                        ALU.subtract).then_inc(gu_ready, 1)
            if half:
                ffn_tiles(pool, half, split_gu, 0, 2)
                pool.wait_ge(wc_loaded, 32)
                for k in range(KD):
                    nc.gpsimd.tensor_scalar(wc_hi[:, k], wc_stage[:, k], 1.0, 1.0,
                                            ALU.mult, ALU.mult).then_inc(comb_hi_done, 1)
                    pool.wait_ge(comb_hi_done, k + 1)
                    nc.gpsimd.tensor_tensor(wc_lo[:, k], wc_stage[:, k], as_f32(wc_hi[:, k]),
                                            ALU.subtract).then_inc(comb_ready, 1)
                    ffn_tiles(pool, half, split_gu, 2 + k, 3 + k)
            else:
                ffn_tiles(pool, half, split_gu)
            for c in range(NF):
                n = half * NF + c
                i = n % 2
                pool.wait_ge(wd_loaded[i], 16 * (n // 2 + 1))
                if n >= 2:
                    pool.wait_ge(wd_used, n - 1)
                nc.gpsimd.tensor_scalar(wd_hi[:, i], wd_stage[:, i], 1.0, 1.0,
                                        ALU.mult, ALU.mult).then_inc(wd_hi_done, 1)
                pool.wait_ge(wd_hi_done, n + 1)
                nc.gpsimd.tensor_tensor(wd_lo[:, i], wd_stage[:, i], as_f32(wd_hi[:, i]),
                                        ALU.subtract).then_inc(wd_ready, 1)
                if n == 9:
                    pool.wait_ge(toep_copied, 1)
                    nc.gpsimd.affine_select(out=s4[:, 5, 0:P], in_=s4[:, 5, 0:P], compare_op=ALU.is_ge, fill=0.0,
                                            base=0, pattern=[[1, P]], channel_multiplier=-1).then_inc(toep_masked, 1)
        nc.gpsimd.tensor_scalar(wb_hi[:, :], wb_stage, 1.0, 1.0, ALU.mult, ALU.mult).then_inc(comb_hi_done, 1)
        pool.wait_ge(comb_hi_done, KD + 1)
        nc.gpsimd.tensor_tensor(wb_lo[:, :], wb_stage, as_f32(wb_hi[:, :]), ALU.subtract).then_inc(comb_ready, 1)
        pool.wait_ge(bias_loaded, 32)
        for t in range(NT):
            pool.wait_ge(xn_done, NT + t + 1)
            nc.gpsimd.tensor_tensor(acc[:, t, :], acc[:, t, :], bias, ALU.add).then_inc(bias_added, 1)

    def scalar_program(act, ahead):
        act.wait_ge(ones_set, 1)
        nc.scalar.activation(gt[:, 9, :], gt[:, 8, :], ACT.Sqrt)

        def sqrt_var(n, js=slice(0, TH)):
            act.wait_ge(var_done, n + 1)
            nc.scalar.activation(ln[:, 1, js], ln[:, 0, js], ACT.Sqrt).then_inc(sd_done, 1)

        def xT_evac(n, bank):
            act.wait_ge(xT_done, n + 1)
            t = n % NT
            nc.scalar.activation(xT_hi[:, :, t * P:(t + 1) * P],
                                 banks[:, bank, :].rearrange("p (k n) -> p k n", k=KD),
                                 ACT.Copy).then_inc(xT_hi_done, 1)

        def ffn(half):
            def silu_tile(f, i, seen):
                n = seen * 2 + i
                act.wait_ge(gu_used, n + 3)
                nc.scalar.activation(work[:, i], banks[:, G + 2 * i], ACT.Silu).then_inc(silu_done, 1)
                act.wait_ge(h_done, n + 3)
                nc.scalar.activation(hT_hi[:, f], work[:, 2 + i], ACT.Copy).then_inc(h_hi_done, 1)
            ffn_tiles(act, half, silu_tile)

        def hg_copy(tiles):
            for n in tiles:
                half, t = n // TH, n % TH
                act.wait_ge(base_done, n + 1)
                if half:
                    act.wait_ge(hw_done, 1)
                nc.scalar.activation(hg[:, t, :], banks[:, linear_bank(n) + 1, DM - CUT:WC - CUT],
                                     ACT.Copy).then_inc(hg_done, 1)

        def gate_exps(half):
            act.wait_ge(ge_in, 2 * half + 2)
            nc.scalar.activation(ge, ge, ACT.Exp).then_inc(ge_done, 1)
            nc.scalar.activation(gt[:, 1, :], gt[:, 0, :], ACT.Exp, scale=-1.0).then_inc(ge_done, 1)

        def hwT_evac(half):
            act.wait_ge(hwT_done, half + 1)
            if half:
                act.wait_ge(moe_done, TH)
            nc.scalar.activation(hwT_hi[:, :], banks[:, D, :].rearrange("p (t n) -> p t n", t=TH),
                                 ACT.Copy).then_inc(hwT_hi_done, 1)

        sqrt_var(0, slice(0, 2))
        sqrt_var(1, slice(2, TH))
        for t in range(TH):
            xT_evac(t, D + t)
        ffn(0)
        sqrt_var(2)
        for t in range(TH, NT):
            xT_evac(t, G + t - TH)
        act.wait_ge(toep_ready, 1)
        nc.scalar.activation(toep_hi[:, P:], s4[:, 6, :], ACT.Copy).then_inc(toep_ready, 1)
        ffn(1)
        sqrt_var(3)
        for t in range(TH):
            xT_evac(NT + t, G + t)
        sqrt_var(4)
        hg_copy(range(0, 2))
        for t in range(TH, NT):
            xT_evac(NT + t, D + t - TH)
        hg_copy(range(2, TH))
        gate_exps(0)
        hg_copy(range(TH, NT))
        gate_exps(1)
        ahead(0, 1)
        hwT_evac(0)
        ahead(1, 2)
        hwT_evac(1)
        ahead(2, 4)

    def vector_program(dve, ahead):
        chained = [0]

        def link(ins):
            chained[0] += 1
            ins.then_inc(dve_chain, 1)
            dve.wait_ge(dve_chain, chained[0])

        nc.vector.memset(gt[:, 8, :], 1.0).then_inc(ones_set, 1)
        dve.sem_inc(h_done, 2)
        dve.sem_inc(gu_ready, 2)
        dve.sem_inc(gu_used, 2)
        nc.vector.memset(as_f32(toep_lo[:, 0:P]), 0.0).then_inc(zeros_set, 1)
        nc.vector.memset(as_f32(toep_hi[:, 0:P]), 0.0)

        def stats(t):
            return nc.vector.bn_stats(st[:, t % TH, :], acc[:, t, :])

        def variance(tiles):
            for t in tiles:
                ins = nc.vector.bn_aggr(mv[:, t % TH, :], st[:, t % TH, :])
            link(ins)
            js = slice(tiles[0] % TH, tiles[-1] % TH + 1)
            nc.vector.tensor_scalar(ln[:, 0, js], mv[:, js, 1], EPS, None, ALU.add).then_inc(var_done, 1)

        def inverse_deviation(n, tiles):
            dve.wait_ge(sd_done, n + 1)
            v, sd, inv, y = (ln[:, i, tiles[0] % TH:tiles[-1] % TH + 1] for i in range(4))
            link(nc.vector.reciprocal(inv, sd))
            link(nc.vector.tensor_tensor(y, inv, inv, ALU.mult))
            link(nc.vector.tensor_tensor(y, y, v, ALU.mult))
            link(nc.vector.tensor_scalar(y, y, -0.5, 1.5, ALU.mult, ALU.add))
            link(nc.vector.tensor_tensor(inv, inv, y, ALU.mult))

        def normalise(tiles):
            for t in tiles:
                j = t % TH
                nc.vector.tensor_scalar(work[:, j], acc[:, t, :], mv[:, j, 0:1], ln[:, 2, j:j + 1],
                                        ALU.subtract, ALU.mult).then_inc(xn_done, 1)

        def norm(n, tiles):
            variance(tiles)
            inverse_deviation(n, tiles)
            normalise(tiles)

        def load_stats(tiles):
            for t in tiles:
                dve.wait_ge(x_loaded[t], 16)
                ins = stats(t)
            link(ins)

        def xT_evac(n, bank):
            dve.wait_ge(xT_hi_done, n + 1)
            cols = slice((n % NT) * P, (n % NT + 1) * P)
            nc.vector.tensor_tensor(xT_lo[:, :, cols], banks[:, bank, :].rearrange("p (k n) -> p k n", k=KD),
                                    as_f32(xT_hi[:, :, cols]), ALU.subtract).then_inc(xT_lo_done, 1)

        def ffn(half, between):
            def h_tile(f, i, seen):
                n = seen * 2 + i
                dve.wait_ge(silu_done, n + 1)
                nc.vector.tensor_tensor(work[:, 2 + i], banks[:, G + 2 * i + 1], work[:, i],
                                        ALU.mult).then_inc(h_done, 1)
                dve.wait_ge(h_hi_done, n + 1)
                nc.vector.tensor_tensor(hT_lo[:, f], work[:, 2 + i], as_f32(hT_hi[:, f]),
                                        ALU.subtract).then_inc(h_lo_done, 1)
            cuts = [0, *sorted(between), NF // 2 + 1]
            for first, end in zip(cuts, cuts[1:]):
                if first in between:
                    between[first]()
                ffn_tiles(dve, half, h_tile, first, end)

        one_m, one_p, w_im, dr, di, sq = (s4[0:NS, i, :] for i in range(6))

        def step_size():
            dve.wait_ge(s4_loaded, 160)
            xx, n, r, poly = (ex[:, i:i + 1] for i in range(4))
            link(nc.vector.tensor_scalar(xx, sm[:, 8:9], -1.0, None, ALU.mult))
            link(nc.vector.tensor_scalar(n, xx, 1.4426950408889634, 1.5 * 2 ** 23, ALU.mult, ALU.add))
            link(nc.vector.tensor_scalar(n, n, -1.5 * 2 ** 23, None, ALU.add))
            link(nc.vector.scalar_tensor_tensor(r, n, -0.693359375, xx, ALU.mult, ALU.add))
            link(nc.vector.scalar_tensor_tensor(r, n, 2.12194440e-4, r, ALU.mult, ALU.add))
            nc.vector.tensor_scalar(exi[:, :], n, 127.0, 2.0 ** 23, ALU.add, ALU.mult)
            link(nc.vector.tensor_scalar(poly, r, 1 / 5040, 1 / 720, ALU.mult, ALU.add))
            for coef in (1 / 120, 1 / 24, 1 / 6, 1 / 2, 1.0, 1.0):
                link(nc.vector.tensor_scalar(poly, poly, r, coef, ALU.mult, ALU.add))
            link(nc.vector.tensor_scalar(sm[:, 9:10], poly, as_f32(exi[:, :]), 2.0, ALU.mult, ALU.mult))

        def cauchy_d():
            link(nc.vector.tensor_scalar(sm[:, 11:12], sm[:, 0:1], -1.0, None, ALU.mult))
            nc.vector.tensor_scalar(bb[:, 4:5], sm[:, 1:2], -1.0, None, ALU.mult)
            link(nc.vector.tensor_tensor(sm[:, 10:11], sm[:, 11:12], sm[:, 9:10], ALU.subtract))
            link(nc.vector.tensor_scalar(dr, one_m, sm[:, 9:10], None, ALU.mult))
            link(nc.vector.scalar_tensor_tensor(dr, one_p, sm[:, 11:12], dr, ALU.mult, ALU.add))
            link(nc.vector.scalar_tensor_tensor(dr, w_im, sm[:, 1:2], dr, ALU.mult, ALU.add))
            link(nc.vector.tensor_scalar(di, w_im, sm[:, 10:11], None, ALU.mult))
            link(nc.vector.scalar_tensor_tensor(di, one_p, bb[:, 4:5], di, ALU.mult, ALU.add))

        def cauchy_inverse():
            link(nc.vector.tensor_tensor(sq, dr, dr, ALU.mult))
            link(nc.vector.tensor_tensor(one_m, di, di, ALU.mult))
            link(nc.vector.tensor_tensor(sq, sq, one_m, ALU.add))
            link(nc.vector.reciprocal(sq, sq))
            nc.vector.tensor_tensor(dr, dr, sq, ALU.mult)
            link(nc.vector.scalar_tensor_tensor(di, di, -1.0, sq, ALU.mult, ALU.mult))

        def cauchy_numerators():
            for c in range(2):
                link(nc.vector.tensor_tensor(sq[:, 0:NS], vcs[:, c * NS:(c + 1) * NS], bps[:, :], ALU.mult))
                link(nc.vector.tensor_reduce(bb[:, 2 * c:2 * c + 1], sq[:, 0:NS], AX_X, ALU.add))
            nc.vector.tensor_copy(bb[:, 1:2], sm[:, 2:3])
            link(nc.vector.tensor_copy(bb[:, 3:4], sm[:, 3:4]))
            for n, a in enumerate((6, 4)):
                re, im = sm[:, a:a + 1], sm[:, a + 1:a + 2]
                link(nc.vector.tensor_scalar(bb[:, 5:7], bb[:, 0:2], re, None, ALU.mult))
                link(nc.vector.scalar_tensor_tensor(vv[:, 2 * n:2 * n + 2], bb[:, 2:4], im, bb[:, 5:7],
                                                    ALU.mult, ALU.add))
                link(nc.vector.tensor_scalar(bb[:, 5:7], bb[:, 0:2], im, None, ALU.mult))
                link(nc.vector.scalar_tensor_tensor(vv[:, 4 + 2 * n:6 + 2 * n], bb[:, 2:4], re, bb[:, 5:7],
                                                    ALU.mult, ALU.subtract))
            nc.vector.tensor_scalar(vv[:, 8:12], vv[:, 4:8], -1.0, None, ALU.mult)
            link(nc.vector.tensor_copy(vv[:, 12:16], vv[:, 0:4]))
            dve.sem_inc(cauchy_in, 1)

        def roots():
            dve.wait_ge(cauchy_done, 1)
            nc.vector.tensor_copy(A[:, :, :], banks[:, D, 0:KD * 8].rearrange("p (t c) -> p t c",
                                                                               t=KD)).then_inc(cauchy_read, 1)
            dve.wait_ge(cauchy_read, 1)
            wr, wi = omc[:, 0, :], omc[:, 1, :]

            def c(i):
                return cs[:, i, :]

            def a(i):
                return A[:, :, i], A[:, :, 4 + i]

            def cmul(o, u, v, t):
                nc.vector.tensor_tensor(c(t), u[0], v[0], ALU.mult)
                nc.vector.tensor_tensor(c(t + 1), u[1], v[1], ALU.mult)
                nc.vector.tensor_tensor(c(t + 2), u[0], v[1], ALU.mult)
                link(nc.vector.tensor_tensor(c(t + 3), u[1], v[0], ALU.mult))
                nc.vector.tensor_tensor(c(o), c(t), c(t + 1), ALU.subtract)
                link(nc.vector.tensor_tensor(c(o + 1), c(t + 2), c(t + 3), ALU.add))
                return c(o), c(o + 1)

            den = cmul(0, (wr, wi), a(3), 8)
            link(nc.vector.tensor_scalar(c(0), c(0), 1.0, None, ALU.add))
            num = cmul(2, a(1), a(2), 8)
            num = cmul(4, num, (wr, wi), 8)
            nc.vector.tensor_tensor(c(8), den[0], den[0], ALU.mult)
            link(nc.vector.tensor_tensor(c(9), den[1], den[1], ALU.mult))
            link(nc.vector.tensor_tensor(c(8), c(8), c(9), ALU.add))
            link(nc.vector.reciprocal(c(8), c(8)))
            nc.vector.tensor_tensor(c(0), den[0], c(8), ALU.mult)
            link(nc.vector.scalar_tensor_tensor(c(1), den[1], -1.0, c(8), ALU.mult, ALU.mult))
            quo = cmul(6, num, den, 8)
            nc.vector.tensor_tensor(c(8), a(0)[0], quo[0], ALU.subtract)
            link(nc.vector.tensor_tensor(c(9), a(0)[1], quo[1], ALU.subtract))
            link(nc.vector.tensor_scalar(cs[:, 8:10, :], cs[:, 8:10, :], 2.0 / DM, None, ALU.mult))
            nc.vector.tensor_tensor(c(10)[:, 0:FT], c(8)[:, 0:FT], c(8)[:, FT:KD], ALU.add)
            link(nc.vector.tensor_tensor(c(11)[:, 0:FT], c(9)[:, 0:FT], c(9)[:, FT:KD], ALU.subtract))
            nc.vector.tensor_copy(c(10)[0:1, 0:1], c(8)[0:1, 0:1])
            link(nc.vector.memset(c(11)[0:1, 0:1], 0.0))

        def phases():
            dve.wait_ge(tab_loaded, 16)
            for t in range(FT):
                re, im = cs[:, 10, t:t + 1], cs[:, 11, t:t + 1]
                nc.vector.tensor_scalar(s4[:, 6, 0:P], cos_t[:, t, 0:P], re, None, ALU.mult)
                link(nc.vector.tensor_scalar(s4[:, 6, P:2 * P], cos_t[:, t, 0:P], im, None, ALU.mult))
                nc.vector.scalar_tensor_tensor(uv[:, 0, t], sin_t[:, t, 0:P], im, s4[:, 6, 0:P], ALU.mult, ALU.add)
                link(nc.vector.scalar_tensor_tensor(uv[:, 1, t], sin_t[:, t, 0:P], re, s4[:, 6, P:2 * P],
                                                    ALU.mult, ALU.subtract))
            link(nc.vector.tensor_scalar(uv[0:1, 1, 0], sin_t[0:1, 0, 0:P], cs[0:1, 8, FT:FT + 1], None, ALU.mult))
            dve.sem_inc(uv_done, 1)

        def toeplitz():
            dve.wait_ge(toep_done, 1)
            nc.vector.tensor_copy(s4[:, 5, :], banks[:, G + 1, :]).then_inc(toep_copied, 1)
            dve.wait_ge(toep_masked, 1)
            nc.vector.tensor_copy(s4[:, 6, P:], s4[:, 5, P:])
            nc.vector.scalar_tensor_tensor(s4[:, 6, 0:P], ident[:, :], dsk[:, 0:1], s4[:, 5, 0:P],
                                           ALU.mult, ALU.add).then_inc(toep_ready, 1)
            dve.wait_ge(toep_ready, 2)
            nc.vector.tensor_tensor(toep_lo[:, P:], s4[:, 6, :], as_f32(toep_hi[:, P:]),
                                    ALU.subtract).then_inc(toep_ready, 1)

        def residual(half):
            for t in range(half * TH, half * TH + TH + half):
                if t < half * TH + TH:
                    dve.wait_ge(y_done, t + 1)
                    nc.vector.tensor_tensor(acc[:, t, :], acc[:, t, :], banks[:, D + t % TH, :],
                                            ALU.add).then_inc(x1_done, 1)
                if half and t > TH:
                    dve.wait_ge(x1_done, t)
                    ins = stats(t - 1)
            if half:
                link(ins)
            else:
                dve.wait_ge(x1_done, TH)

        def linear_add(n):
            t, bank = n, linear_bank(n)
            dve.wait_ge(hg_done, n + 1)
            dve.wait_ge(bias_added, n + 1)
            nc.vector.tensor_tensor(acc[:, t, 0:CUT], acc[:, t, 0:CUT], banks[:, bank, 0:CUT], ALU.add)
            nc.vector.tensor_tensor(acc[:, t, CUT:DM], acc[:, t, CUT:DM], banks[:, bank + 1, 0:DM - CUT],
                                    ALU.add).then_inc(base_added, 1)

        def gates(half):
            dve.wait_ge(hg_done, half * TH + TH)
            logits = hg[:, :, ER:ER + NE]

            def wide(i):
                return gt[:, i, :].unsqueeze(2).broadcast_to([P, TH, NE])
            link(nc.vector.tensor_reduce(gt[:, 2, :], logits, AX_X, ALU.max))
            nc.vector.tensor_tensor(ge, logits, wide(2), ALU.subtract).then_inc(ge_in, 1)
            nc.vector.tensor_scalar(gt[:, 0, :], hg[:, :, ER + NE], dsk[:, 1:2], None, ALU.add).then_inc(ge_in, 1)
            dve.wait_ge(ge_done, 2 * half + 2)
            nc.vector.tensor_reduce(gt[:, 3, :], ge, AX_X, ALU.add)
            link(nc.vector.tensor_scalar(gt[:, 4, :], gt[:, 1, :], 1.0, None, ALU.add))
            nc.vector.reciprocal(gt[:, 5, :], gt[:, 3, :])
            link(nc.vector.reciprocal(gt[:, 6, :], gt[:, 4, :]))
            nc.vector.tensor_tensor(gw, ge, wide(5), ALU.mult)
            link(nc.vector.tensor_scalar(gt[:, 6, :], gt[:, 6, :], MAX_THRESHOLD, None, ALU.mult))
            link(nc.vector.tensor_tensor(gw, gw, wide(6), ALU.subtract))
            link(nc.vector.tensor_scalar(gw, gw, 0.0, None, ALU.max))
            link(nc.vector.tensor_reduce(gt[:, 7, :], gw, AX_X, ALU.add))
            link(nc.vector.tensor_scalar(gt[:, 8, :], gt[:, 7, :], 0.0, None, ALU.is_equal))
            link(nc.vector.tensor_tensor(gt[:, 7, :], gt[:, 7, :], gt[:, 8, :], ALU.add))
            link(nc.vector.reciprocal(gt[:, 9, :], gt[:, 7, :]))
            link(nc.vector.tensor_scalar(gt[:, 9, :], gt[:, 9, :], SCALING, None, ALU.mult))
            link(nc.vector.tensor_tensor(gw, gw, wide(9), ALU.mult))
            if half:
                dve.wait_ge(hwT_done, 1)
            for t in range(TH):
                ins = nc.vector.tensor_tensor(hw[:, t, :].rearrange("p (e r) -> p e r", e=NE),
                                              hg[:, t, 0:ER].rearrange("p (e r) -> p e r", e=NE),
                                              gw[:, t, :].unsqueeze(2).broadcast_to([P, NE, RANK]), ALU.mult)
            ins.then_inc(hw_done, 1)

        def hwT_evac(half):
            dve.wait_ge(hwT_hi_done, half + 1)
            nc.vector.tensor_tensor(hwT_lo[:, :], banks[:, D, :].rearrange("p (t n) -> p t n", t=TH),
                                    as_f32(hwT_hi[:, :]), ALU.subtract).then_inc(hwT_lo_done, 1)

        def experts_add(half):
            for n in range(half * TH, half * TH + TH):
                dve.wait_ge(moe_done, n + 1)
                nc.vector.tensor_tensor(acc[:, n, :], acc[:, n, :], banks[:, expert_bank(n), :],
                                        ALU.add).then_inc(moe_added, 1)

        first, second = range(0, 2), range(2, TH)
        load_stats(first)
        variance(first)
        load_stats(second)
        inverse_deviation(0, first)
        normalise(first)
        variance(second)
        inverse_deviation(1, second)
        for t in first:
            xT_evac(t, D + t)
        normalise(second)
        for t in second:
            xT_evac(t, D + t)
        ffn(0, {1: step_size, 2: cauchy_d, 3: cauchy_inverse, 4: cauchy_numerators, 5: roots})
        phases()
        load_stats(range(TH, NT))
        norm(2, range(TH, NT))
        for t in range(TH, NT):
            xT_evac(t, G + t - TH)
        toeplitz()
        residual(0)
        ffn(1, {})
        for t in range(TH):
            ins = stats(t)
        link(ins)
        norm(3, range(TH))
        for t in range(TH):
            xT_evac(NT + t, G + t)
        residual(1)
        norm(4, range(TH, NT))
        for n in range(2):
            linear_add(n)
        for t in range(TH, NT):
            xT_evac(NT + t, D + t - TH)
        for n in range(2, TH):
            linear_add(n)
        gates(0)
        for n in range(TH, NT):
            linear_add(n)
        gates(1)
        hwT_evac(0)
        ahead(0, 2)
        experts_add(0)
        hwT_evac(1)
        ahead(2, 3)
        experts_add(1)
        ahead(3, 4)

    def tensor_program(pe, ahead):
        def transposes(n, bank):
            pe.wait_ge(xn_done, n + 1)
            for k in range(KD):
                ins = nc.tensor.transpose(banks[:, bank, k * P:(k + 1) * P],
                                          work[:, n % TH, k * P:(k + 1) * P], ident[:, :])
            ins.then_inc(xT_done, 1)

        def gate_up(half):
            def tile(f, i, seen):
                n = seen * 2 + i
                pe.wait_ge(gu_ready, n + 3)
                pe.wait_ge(h_done, n + 1)
                for m in range(2):
                    for k in range(KD):
                        cols = slice(half * HALF, (half + 1) * HALF)
                        ins = matmul3(nc, banks[:, G + 2 * i + m], gu_hi[:, i, m, k], gu_lo[:, i, m, k],
                                      xT_hi[:, k, cols], xT_lo[:, k, cols], k == 0, k == KD - 1)
                ins.then_inc(gu_used, 1)
            return tile

        def down(half, chunks):
            for c in chunks:
                n = half * NF + c
                pe.wait_ge(wd_ready, n + 1)
                pe.wait_ge(h_lo_done, n + 1)
                for t in range(TH):
                    cols = slice(t * P, (t + 1) * P)
                    ins = matmul3(nc, banks[:, D + t], hT_hi[:, c, cols], hT_lo[:, c, cols],
                                  wd_hi[:, n % 2], wd_lo[:, n % 2], c == 0, False)
                ins.then_inc(wd_used, 1)

        def convolve(half):
            pe.wait_ge(toep_ready, 3)
            for t in range(half * TH, half * TH + TH):
                cols = slice(t * P, (t + 1) * P)
                for j in range(KD):
                    lo = min(j * P, DM - 2 * P)
                    src = slice(P + lo - j * P, P + DM - j * P)
                    ins = matmul3(nc, banks[:, D + t % TH, lo:DM], xT_hi[:, j, cols], xT_lo[:, j, cols],
                                  toep_hi[:, src], toep_lo[:, src], False, j == KD - 1)
                ins.then_inc(y_done, 1)

        def linear(n):
            cols = slice(n * P, (n + 1) * P)
            bank = linear_bank(n)
            pe.wait_ge(comb_ready, KD)
            pe.wait_ge(xT_lo_done, NT + max(n + 1, TH))
            if 2 <= n < NT - 2:
                pe.wait_ge(base_added, n - 1)
            for b, part in ((bank, slice(0, CUT)), (bank + 1, slice(CUT, WC))):
                for k in range(KD):
                    ins = matmul3(nc, banks[:, b, 0:part.stop - part.start], xT_hi[:, k, cols], xT_lo[:, k, cols],
                                  wc_hi[:, k, part], wc_lo[:, k, part], k == 0, k == KD - 1)
            ins.then_inc(base_done, 1)

        def gated_transposes(half):
            pe.wait_ge(hw_done, half + 1)
            pe.wait_ge(*((hwT_lo_done, 1) if half else (base_added, NT - 1)))
            for t in range(TH):
                ins = nc.tensor.transpose(banks[:, D, t * P:(t + 1) * P], hw[:, t, :], ident[:, :])
            ins.then_inc(hwT_done, 1)

        def experts(half):
            pe.wait_ge(hwT_lo_done, half + 1)
            pe.wait_ge(comb_ready, KD + 1)
            pe.wait_ge(base_added, NT)
            for t in range(TH):
                n = half * TH + t
                if n >= 3:
                    pe.wait_ge(moe_added, n - 2)
                matmul3(nc, banks[:, expert_bank(n), :], hwT_hi[:, t], hwT_lo[:, t], wb_hi[:, :], wb_lo[:, :],
                        True, True).then_inc(moe_done, 1)

        def warm_up(count):
            for _ in range(count):
                nc.tensor.matmul(banks[:, G + 3, 0:P], as_f32(toep_lo[:, 0:P]), as_f32(toep_lo[:, 0:P]),
                                 start=True, stop=True)

        def first_tile(m, part):
            cols = slice(part * (HALF // 2), (part + 1) * (HALF // 2))
            pe.wait_ge(xT_lo_done, (part + 1) * TH // 2)
            for k in range(KD):
                ins = matmul3(nc, banks[:, G + m, cols], gu_hi[:, 0, m, k], gu_lo[:, 0, m, k],
                              xT_hi[:, k, cols], xT_lo[:, k, cols], k == 0, k == KD - 1)
            return ins

        pe.wait_ge(zeros_set, 1)
        warm_up(WARM_UP[0])
        pe.wait_ge(ident_loaded, 16)
        for t in range(2):
            transposes(t, D + t)
        warm_up(WARM_UP[1])
        pe.wait_ge(gu_ready, 3)
        first_tile(0, 0)
        for t in range(2, TH):
            transposes(t, D + t)
        first_tile(1, 0)
        first_tile(0, 1)
        first_tile(1, 1).then_inc(gu_used, 1)
        gate_up(0)(1, 1, 0)
        ffn_tiles(pe, 0, gate_up(0), 1, 5)
        pe.wait_ge(cauchy_in, 1)
        for t in range(KD):
            out = banks[:, D, 8 * t:8 * t + 8]
            nc.tensor.matmul(out, s4[0:NS, 3, t * P:(t + 1) * P], vv[:, 0:8], start=True, stop=False)
            ins = nc.tensor.matmul(out, s4[0:NS, 4, t * P:(t + 1) * P], vv[:, 8:16], start=False, stop=True)
        ins.then_inc(cauchy_done, 1)
        ffn_tiles(pe, 0, gate_up(0), 5, 6)
        pe.wait_ge(cauchy_read, 1)
        down(0, range(0, 6))
        for t in range(TH, NT):
            transposes(t, G + t - TH)
        down(0, range(6, 8))
        pe.wait_ge(xT_lo_done, NT)
        pe.wait_ge(uv_done, 1)
        for i, table in enumerate((cos_t, sin_t)):
            for t in range(FT):
                ins = nc.tensor.matmul(banks[:, G + 1, :], uv[:, i, t], table[:, t, :],
                                       start=i + t == 0, stop=i * FT + t == 2 * FT - 1)
        ins.then_inc(toep_done, 1)
        down(0, range(8, NF))
        convolve(0)
        ffn_tiles(pe, 1, gate_up(1), 0, 6)
        pe.wait_ge(x1_done, TH)
        down(1, range(0, 6))
        for t in range(TH):
            transposes(NT + t, G + t)
        down(1, range(6, NF))
        convolve(1)
        for n in range(2):
            linear(n)
        pe.wait_ge(x1_done, NT)
        for t in range(TH, NT):
            transposes(NT + t, D + t - TH)
        for n in range(2, NT):
            linear(n)
        pe.wait_ge(base_added, NT - 2)
        ahead(0, 1)
        gated_transposes(0)
        ahead(1, 2)
        experts(0)
        gated_transposes(1)
        ahead(2, 3)
        experts(1)
        ahead(3, 4)
        pe.wait_ge(moe_added, NT)

    return sync_program, gpsimd_program, scalar_program, vector_program, tensor_program


def attention(nc, sem, shared, ins, late_sb, attention_sb):
    acc, xT_hi, xT_lo, ident, _, banks, y_done = shared
    w_qk, w_v, w_o, mask_dram, out = ins
    oT_hi, oT_lo, wo_hi, wo_lo = late_sb
    (qT_hi, qT_lo, kT_hi, kT_lo, v_hi, v_lo, q_full, k_full, v_full, p_full, wqk_stage, wvo_stage, wqk_hi, wqk_lo,
     wv_hi, wv_lo, prob, pT_hi, pT_lo, mask, top, total, inv) = attention_sb
    G, S, T, O = 0, 4, 6, 7

    mask_loaded = sem("mask_loaded")
    qk_loaded = [sem(f"qk_loaded{i}") for i in range(RING)]
    vo_loaded = [sem(f"vo_loaded{i}") for i in range(RING)]
    qk_ready = sem("qk_ready")
    vo_ready = sem("vo_ready")
    unit_free = sem("unit_free")
    oT_ready = sem("oT_ready")
    QK0, VO0, FREE0, OT0 = 2 * RING, RING, GBANKS, 1
    credit_given = sem("credit_given")
    split_hi = sem("split_hi")
    unit_done = sem("unit_done")
    unit_hi = sem("unit_hi")
    s_done = sem("s_done")
    s_top = sem("s_top")
    exp_done = sem("exp_done")
    inv_done = sem("inv_done")
    norm_done = sem("norm_done")
    t_done = sem("t_done")
    pT_hi_done = sem("pT_hi_done")
    pT_ready = sem("pT_ready")
    o_done = sem("o_done")
    oT_hi_done = sem("oT_hi_done")
    out_done = sem("out_done")
    wait_passed = sem("wait_passed_2")

    NA = len(AHEAD)
    JV = KD

    def is_split(step):
        return step[0] in "QK" or step[0] == "V" and step[1] % 2 == 0

    n_split_units = sum(map(is_split, units(GROUP)))

    def unit(steps, step):
        return NA + units(steps).index(step) + 1

    def split_unit(steps, step):
        return len(list(filter(is_split, AHEAD))) + list(filter(is_split, units(steps))).index(step) + 1

    def vo_piece(kind, n):
        return JV + n + GH * (kind == "v")

    def unit_bank(n):
        return banks[:, G + (n - 1) % GBANKS]

    def groups(eng, body, steps, last):
        with eng.Fori(0, NG - 1) as g:
            body(g, steps)
        body(NG - 1, last)

    def unit_parts(step, bank):
        if step[0] == "V":
            b = step[1] // 2 % BATCH
            return (bank, v_hi[:, b], v_lo[:, b]), None
        two = slice(2 * step[2], 2 * step[2] + 2)
        tiles = bank.rearrange("p (b r n) -> p b r n", b=2, r=2)
        if step[0] == "Q":
            return (tiles[:, :, 1], qT_hi[:, two], qT_lo[:, two]), (tiles[:, :, 0], q_full[:, two])
        cols = slice(step[2] * HALF, (step[2] + 1) * HALF)
        return (bank, kT_hi[:, cols], kT_lo[:, cols]), (tiles[:, :, 0], k_full[:, two])

    def row_tiles(p):
        yield 0, prob[:, p % 2, 0:P], banks[:, S + p % 2, 0:P], mask[:, P:2 * P]
        yield 1, prob[:, p % 2, P:3 * P], banks[:, S + p % 2, 2 * P:4 * P], mask[:, :]

    def sync_program(sp):
        sp.wait_ge(credit_given, 1)
        sp.wait_ge(y_done, NT)
        sp.dma_start(wqk_stage[:, 0], w_qk[0]).then_inc(qk_loaded[0], 16)
        sp.dma_start(mask[:, :], mask_dram).then_inc(mask_loaded, 16)

        def load_vo(g, j, src):
            sp.wait_ge(vo_ready, g * NVO + j - RING + 1 + VO0)
            sp.dma_start(wvo_stage[:, j % RING], src).then_inc(vo_loaded[j % RING], 16)

        for k in range(KD):
            load_vo(0, k, w_v[0, k])

        def load(g, splits):
            for kind, n in splits:
                if kind == "q":
                    sp.wait_ge(qk_ready, g * NQK + 2 * (n - RING) + 2 + QK0)
                    sp.dma_start(wqk_stage[:, n % RING], w_qk[g * GH + n]).then_inc(qk_loaded[n % RING], 16)
                elif kind in "vo":
                    load_vo(g, vo_piece(kind, n), w_v[g + 1, n] if kind == "v" else w_o[g * GH + n])

        groups(sp, load, SPLITS, LAST_SPLITS)
        for t in range(NT):
            sp.wait_ge(unit_free, (NG - 1) * NU + unit(LAST_GROUP, ("B", t)) + FREE0)
            sp.dma_start(out[t * P:(t + 1) * P, :], acc[:, t, :]).then_inc(out_done, 16)
        sp.wait_ge(out_done, 16 * NT)

    def gpsimd_program(pool):
        def split(src, hi, lo, count, ready):
            nc.gpsimd.tensor_scalar(hi, src, 1.0, 1.0, ALU.mult, ALU.mult).then_inc(split_hi, 1)
            pool.wait_ge(split_hi, count)
            nc.gpsimd.tensor_tensor(lo, src, as_f32(hi), ALU.subtract).then_inc(ready, 1)

        pool.wait_ge(qk_loaded[0], 16)
        for m in range(2):
            split(wqk_stage[:, 0, m], wqk_hi[:, 0, m], wqk_lo[:, 0, m], m + 1, qk_ready)
        for k in range(KD):
            pool.wait_ge(vo_loaded[k % RING], 16 * (k // RING + 1))
            split(wvo_stage[:, k % RING], wv_hi[:, k], wv_lo[:, k], 2 + k + 1, vo_ready)

        def group(g, splits):
            pieces = 2 + KD
            for kind, n in splits:
                if kind == "N":
                    i = n % 2
                    pool.wait_ge(inv_done, g * PAIRS + n + 1)
                    pool.sem_inc(wait_passed, 1)
                    nc.gpsimd.tensor_scalar(prob[:, i, 0:P], prob[:, i, 0:P], inv[:, i, 0:1], 1.0,
                                            ALU.mult, ALU.mult)
                    nc.gpsimd.tensor_scalar(prob[:, i, P:3 * P], prob[:, i, P:3 * P], inv[:, i, 1:2], 1.0,
                                            ALU.mult, ALU.mult).then_inc(norm_done, 1)
                    continue
                if kind in "qk":
                    i, m = n % RING, "qk".index(kind)
                    pool.wait_ge(qk_loaded[i], g * (16 * GH // RING) + 16 * (n // RING + 1))
                    src, hi, lo, ready = wqk_stage[:, i, m], wqk_hi[:, i, m], wqk_lo[:, i, m], qk_ready
                else:
                    j = vo_piece(kind, n)
                    pool.wait_ge(vo_loaded[j % RING], g * (16 * NVO // RING) + 16 * (j // RING + 1))
                    hi, lo = (wv_hi, wv_lo) if kind == "v" else (wo_hi, wo_lo)
                    src, hi, lo, ready = wvo_stage[:, j % RING], hi[:, n], lo[:, n], vo_ready
                pool.sem_inc(wait_passed, 1)
                pieces += 1
                split(src, hi, lo, g * (NQK + NVO) + pieces, ready)

        groups(pool, group, SPLITS, LAST_SPLITS)

    def unit_evac_hi(act, n, g, step):
        (src, hi, _), whole = unit_parts(step, unit_bank(n))
        act.wait_ge(unit_done, g * NU + n)
        if whole:
            nc.scalar.activation(whole[1], whole[0], ACT.Copy)
        nc.scalar.activation(hi, src, ACT.Copy).then_inc(unit_hi, 1)

    def unit_evac_lo(dve, n, split_n, g, step):
        (src, hi, lo), _ = unit_parts(step, unit_bank(n))
        dve.wait_ge(unit_hi, g * n_split_units + split_n)
        nc.vector.tensor_tensor(lo, src, as_f32(hi), ALU.subtract).then_inc(unit_free, 1)

    def v_evac(dve, n, g, step):
        dve.wait_ge(unit_done, g * NU + n)
        nc.vector.tensor_copy(v_full[:, step[1] // 2 % BATCH], unit_bank(n)).then_inc(unit_free, 1)

    def scalar_ahead(act, start, stop):
        for n, step in enumerate(AHEAD[start:stop], start + 1):
            if is_split(step):
                unit_evac_hi(act, n, 0, step)

    def vector_ahead(dve, start, stop):
        for n, step in enumerate(AHEAD[start:stop], start + 1):
            if is_split(step):
                unit_evac_lo(dve, n, n, 0, step)
            else:
                v_evac(dve, n, 0, step)

    def tensor_ahead(pe, start, stop):
        for n, step in enumerate(AHEAD[start:stop], start + 1):
            if step[0] == "V":
                values_or_output(pe, n, 0, step)
            else:
                project(pe, n, 0, step)

    def scalar_program(act):
        def exps(g, p):
            act.wait_ge(s_top, g * PAIRS + p + 1)
            for r, pr, _, _ in row_tiles(p):
                ins = nc.scalar.activation(pr, pr, ACT.Exp, bias=top[:, p % 2, r:r + 1], scale=-1.0,
                                           accum_out=total[:, p % 2, r:r + 1])
            ins.then_inc(exp_done, 1)

        def group(g, steps):
            for step in steps:
                if step == ("S", 0):
                    exps(g, 0)
                elif is_split(step):
                    unit_evac_hi(act, unit(steps, step), g, step)
                elif step[0] == "T":
                    p = step[1]
                    act.wait_ge(t_done, g * PAIRS + p + 1)
                    nc.scalar.activation(p_full[:, p % 2], banks[:, T, 2 * P:3 * P], ACT.Copy)
                    nc.scalar.activation(pT_hi[:, p % 2], banks[:, T, 0:2 * P], ACT.Copy).then_inc(pT_hi_done, 1)
                    if p + 1 < PAIRS:
                        exps(g, p + 1)
                elif step[0] == "O" and step[1] % 2:
                    h, half = step[1] // BATCH, step[1] % BATCH // 2
                    act.wait_ge(o_done, g * PAIRS + step[1] + 1)
                    nc.scalar.activation(oT_hi[:, h, half * HALF:(half + 1) * HALF], banks[:, O],
                                         ACT.Copy).then_inc(oT_hi_done, 1)

        groups(act, group, GROUP, LAST_GROUP)

    def vector_program(dve):
        def inverse(g, p):
            dve.wait_ge(exp_done, g * PAIRS + p + 1)
            nc.vector.reciprocal(inv[:, p % 2, :], total[:, p % 2, :]).then_inc(inv_done, 1)

        def group(g, steps):
            for step in steps:
                if step[0] == "S":
                    p = step[1]
                    dve.wait_ge(s_done, g * PAIRS + p + 1)
                    dve.sem_inc(wait_passed, 1)
                    for r, pr, sc, ma in row_tiles(p):
                        ins = nc.vector.tensor_tensor_reduce(out=pr, in0=sc, in1=ma, scale=-QK_SCALE, scalar=3e38,
                                                             op0=ALU.add, op1=ALU.min,
                                                             accum_out=top[:, p % 2, r:r + 1])
                    ins.then_inc(s_top, 1)
                    if p == 0:
                        inverse(g, 0)
                elif is_split(step):
                    unit_evac_lo(dve, unit(steps, step), split_unit(steps, step), g, step)
                elif step[0] == "V":
                    v_evac(dve, unit(steps, step), g, step)
                elif step[0] in "WAB":
                    t, n = step[1], unit(steps, step)
                    dve.wait_ge(unit_done, g * NU + n)
                    nc.vector.tensor_tensor(acc[:, t, :], acc[:, t, :], unit_bank(n), ALU.add).then_inc(unit_free, 1)
                elif step[0] == "T":
                    p = step[1]
                    dve.wait_ge(pT_hi_done, g * PAIRS + p + 1)
                    nc.vector.tensor_tensor(pT_lo[:, p % 2], banks[:, T, 0:2 * P],
                                            as_f32(pT_hi[:, p % 2]), ALU.subtract).then_inc(pT_ready, 1)
                    if p + 1 < PAIRS:
                        inverse(g, p + 1)
                elif step[0] == "O" and step[1] % 2:
                    h, half = step[1] // BATCH, step[1] % BATCH // 2
                    cols = slice(half * HALF, (half + 1) * HALF)
                    dve.wait_ge(oT_hi_done, g * (PAIRS // 2) + step[1] // 2 + 1)
                    nc.vector.tensor_tensor(oT_lo[:, h, cols], banks[:, O], as_f32(oT_hi[:, h, cols]),
                                            ALU.subtract).then_inc(oT_ready, 1)

        dve.wait_ge(mask_loaded, 16)
        groups(dve, group, GROUP, LAST_GROUP)

    def project(pe, n, g, step):
        kind, h, half = step
        m, cols = "QK".index(kind), slice(half * HALF, (half + 1) * HALF)
        pe.wait_ge(unit_free, g * NU + n - GBANKS + FREE0)
        pe.wait_ge(qk_ready, g * NQK + 2 * h + m + 1 + QK0)
        for k in range(KD):
            ins = matmul3(nc, unit_bank(n), wqk_hi[:, h % RING, m, k], wqk_lo[:, h % RING, m, k],
                          xT_hi[:, k, cols], xT_lo[:, k, cols], k == 0, k == KD - 1)
        ins.then_inc(unit_done, 1)

    def values_or_output(pe, u, g, step):
        kind, n = step
        cols = slice(n % NT * P, (n % NT + 1) * P)
        pe.wait_ge(unit_free, g * NU + u - GBANKS + FREE0)
        heads = range(GH)
        if kind == "V":
            if n in (0, 1, NT, NT + 1):
                pe.wait_ge(vo_ready, g * NVO + (vo_piece("v", KD - 1) + 1 if n >= NT else KD) + VO0)
            left, right = (xT_hi, xT_lo), (wv_hi, wv_lo)
        else:
            pe.wait_ge(vo_ready, g * NVO + vo_piece("o", GH - 1) + 1 + VO0)
            heads = {"W": range(GH), "A": range(GH - 1), "B": range(GH - 1, GH)}[kind]
            pe.wait_ge(oT_ready, g * (PAIRS // 2) + (heads.stop - 1) * (BATCH // 2) + 1 + (n >= TH) + OT0)
            left, right = (oT_hi, oT_lo), (wo_hi, wo_lo)
        for k in heads:
            ins = matmul3(nc, unit_bank(u), left[0][:, k, cols], left[1][:, k, cols],
                          right[0][:, k], right[1][:, k], k == heads.start, k == heads.stop - 1)
        ins.then_inc(unit_done, 1)

    def tensor_program(pe):
        def group(g, steps):
            for step in steps:
                kind, n = step[0], step[1]
                if kind in "QK":
                    project(pe, unit(steps, step), g, step)
                elif kind in "VWAB":
                    values_or_output(pe, unit(steps, step), g, step)
                elif kind == "S":
                    h, b = n // BATCH, n % BATCH
                    if n and b % 2 == 0:
                        last = max(unit(steps, ("Q", h, b // 2)), unit(steps, ("K", h, b // 2)))
                        pe.wait_ge(unit_free, g * NU + last + FREE0)
                    keys = slice(b * SEQ, (b + 1) * SEQ)
                    nc.tensor.matmul(banks[:, S + n % 2, 0:P], q_full[:, b], k_full[:, b], start=True, stop=True)
                    ins = matmul3(nc, banks[:, S + n % 2, 2 * P:4 * P], qT_hi[:, b], qT_lo[:, b],
                                  kT_hi[:, keys], kT_lo[:, keys], True, True)
                    ins.then_inc(s_done, 1)
                elif kind == "T":
                    pe.wait_ge(norm_done, g * PAIRS + n + 1)
                    for block in range(3):
                        part = slice(block * P, (block + 1) * P)
                        ins = nc.tensor.transpose(banks[:, T, part], prob[:, n % 2, part], ident[:, :])
                    ins.then_inc(t_done, 1)
                elif kind == "O":
                    h, b = n // BATCH, n % BATCH
                    pe.wait_ge(pT_ready, g * PAIRS + n + 1)
                    if h == 0:
                        pe.wait_ge(unit_free, g * NU + (unit(steps, ("V", 2 * b + 1)) if b else NA) + FREE0)
                    if n % 2 == 0:
                        pe.wait_ge(oT_ready, g * (PAIRS // 2) + n // 2 + OT0)
                    cols = slice(b % 2 * SEQ, (b % 2 + 1) * SEQ)
                    d = slice(h * DH, (h + 1) * DH)
                    matmul3(nc, banks[:, O, cols], v_hi[:, b, d], v_lo[:, b, d], pT_hi[:, n % 2], pT_lo[:, n % 2],
                            True, False)
                    ins = nc.tensor.matmul(banks[:, O, cols.start + P:cols.stop], v_full[:, b, d], p_full[:, n % 2],
                                           start=False, stop=True)
                    ins.then_inc(o_done, 1)

        pe.wait_ge(unit_free, 2 + FREE0)
        groups(pe, group, GROUP, LAST_GROUP)

    def credits(dve):
        dve.sem_inc(qk_ready, QK0)
        dve.sem_inc(vo_ready, VO0)
        dve.sem_inc(unit_free, FREE0)
        dve.sem_inc(oT_ready, OT0)
        dve.sem_inc(credit_given, 1)

    return (sync_program, gpsimd_program, scalar_program, vector_program, tensor_program,
            scalar_ahead, vector_ahead, tensor_ahead, credits)


def build(nc, x, w_gu, w_down, lam, p_ri, q_ri, ct, vc, bp, d_skip, log_step, om_rows, om_cols, tables,
          w_comb, b_base, b_thr, w_expb, w_qk, w_v, w_o, identity, mask, out):
    with ExitStack() as ctx:
        def place(stack, *tensors):
            return [stack.enter_context(nc.sbuf_tensor(name, shape, dt)) for name, shape, dt in tensors]

        def split(name, shape):
            return (f"{name}_hi", shape, F32R), (f"{name}_lo", shape, F32R)

        def sem(name):
            return ctx.enter_context(nc.semaphore(name))

        acc, xT_hi, xT_lo, ident = place(ctx, ("acc", [P, NT, DM], F32), *split("xT", [P, KD, TOK]),
                                         ("ident", [P, P], F32))
        small_sb = place(ctx, ("vcs", [NS, 2 * NS], F32), ("bps", [NS, NS], F32), ("sm", [NS, 12], F32),
                         ("ex", [NS, 4], F32), ("exi", [NS, 1], mybir.dt.int32), ("bb", [NS, 8], F32),
                         ("vv", [NS, 16], F32), ("omc", [P, 2, KD], F32), ("cs", [P, 12, KD], F32),
                         ("A", [P, KD, 8], F32), ("dsk", [P, 2], F32), ("st", [P, TH, 6], F32),
                         ("mv", [P, TH, 2], F32), ("ln", [P, 4, TH], F32), ("gt", [P, 10, TH], F32))
        with ExitStack() as late:
            late_sb = place(late, *split("oT", [P, GH, TOK]), *split("wo", [P, GH, DM]))
        shared_bytes = 4 * 2 * (GH * TOK + GH * DM)
        expert_bytes = 4 * (2 * KD * WC + 2 * DM + 8 * DM + 2 * TH * P)
        expert_sb = place(ctx, *split("wc", [P, KD, WC]), *split("wb", [P, DM]), ("s4", [P, 8, DM], F32),
                          *split("hwT", [P, TH, P]), ("rest", [P, (shared_bytes - expert_bytes) // 4], F32))
        with ExitStack() as early:
            ffn_sb = place(early, *split("hT", [P, NF, HALF]), ("gu_stage", [P, 2, 2, KD, P], F32),
                           *split("gu", [P, 2, 2, KD, P]), ("wd_stage", [P, 2, DM], F32), *split("wd", [P, 2, DM]),
                           ("work", [P, 4, DM], F32), *split("toep", [P, P + DM]),
                           ("tab", [P, KD * WC + DM], F32))
        attention_sb = place(ctx, *split("qT", [P, BATCH, P]), *split("kT", [P, TOK]),
                             *split("v", [P, BATCH, GH * DH]), ("q_full", [P, BATCH, P], F32),
                             ("k_full", [P, BATCH, P], F32), ("v_full", [P, BATCH, GH * DH], F32),
                             ("p_full", [P, 2, P], F32),
                             ("wqk_stage", [P, RING, 2, KD, DH], F32), ("wvo_stage", [P, RING, DM], F32),
                             *split("wqk", [P, RING, 2, KD, DH]), *split("wv", [P, KD, GH * DH]),
                             ("prob", [P, 2, 3 * P], F32),
                             *split("pT", [P, 2, 2 * P]), ("mask", [P, 2 * P], F32),
                             ("top", [P, 2, 2], F32), ("total", [P, 2, 2], F32), ("inv", [P, 2, 2], F32))
        banks = ctx.enter_context(nc.psum_tensor("banks", [P, 8, DM], F32))
        shared = (acc, xT_hi, xT_lo, ident, identity, banks, sem("y_done"))

        (sync_0, gpsimd_0, scalar_0, vector_0, tensor_0) = layer0(
            nc, sem, shared, (x, w_gu, w_down, lam, p_ri, q_ri, ct, vc, bp, d_skip, log_step, om_rows, om_cols,
                              tables, w_comb, b_base, b_thr, w_expb), ffn_sb, expert_sb, small_sb)
        (sync_1, gpsimd_1, scalar_1, vector_1, tensor_1, scalar_ahead, vector_ahead, tensor_ahead,
         credits) = attention(nc, sem, shared, (w_qk, w_v, w_o, mask, out), late_sb, attention_sb)

        block = ctx.enter_context(nc.Block())

        @block.sync
        def _(sp):
            sync_0(sp)
            sync_1(sp)

        @block.gpsimd
        def _(pool):
            gpsimd_0(pool)
            gpsimd_1(pool)

        @block.scalar
        def _(act):
            scalar_0(act, lambda *part: scalar_ahead(act, *part))
            scalar_1(act)

        @block.vector
        def _(dve):
            credits(dve)
            vector_0(dve, lambda *part: vector_ahead(dve, *part))
            vector_1(dve)

        @block.tensor
        def _(pe):
            tensor_0(pe, lambda *part: tensor_ahead(pe, *part))
            tensor_1(pe)


def constants():
    import numpy as np
    half = np.arange(DM // 2)
    f = np.concatenate([half, DM - half])
    f[DM // 2] = DM // 2
    w = np.exp(-2j * np.pi * f / DM)
    om_rows = np.stack([1 - w.real, 1 + w.real, w.imag]).astype(np.float32)
    om_cols = np.stack([1 + w.real, w.imag]).astype(np.float32).reshape(2, KD, P).transpose(2, 0, 1)
    turn = 2 * np.pi * (half[:, None] * np.arange(DM)[None, :] % DM) / DM
    cos, sin = np.cos(turn), np.sin(turn)
    sin[0] = np.cos(np.pi * np.arange(DM))
    tables = np.stack([cos, sin]).astype(np.float32)
    tables = tables.reshape(2, FT, P, DM).transpose(2, 0, 1, 3).reshape(P, 2 * FT * DM)
    mask = np.zeros((P, 2 * P), np.float32)
    mask[:, P:][np.triu_indices(P, 1)] = NEG
    return {"om_rows": om_rows, "om_cols": om_cols, "tables": tables, "identity": np.eye(P, dtype=np.float32),
            "mask": mask}


def layout(a):
    import numpy as np

    def chunks(w, n):
        return w.reshape(KD, P, n, P).transpose(2, 1, 0, 3)

    pad = ((0, 0), (0, NF * P - FF))
    gate, up, down = (np.pad(w, pad) for w in (a["L0_ffn_W_gate"].T, a["L0_ffn_W_up"].T, a["L0_ffn_W_down"]))
    wq = a["L1_attn_wq"].reshape(DM, HEADS, 192)[:, :, :DH].reshape(DM, HEADS * DH)
    wk, wv = a["L1_attn_wkv"][:, :HEADS * DH], a["L1_attn_wkv"][:, HEADS * DH:2 * HEADS * DH]
    comb = np.concatenate([a["L1_ffn_W_base"], a["L1_ffn_A_w"].reshape(ER, DM), a["L1_ffn_W_gate"],
                           a["L1_ffn_W_thr"][None], np.zeros((1, DM), np.float32)])
    return {
        "x": a["L0_attn_u"].reshape(TOK, DM),
        "w_gu": np.stack([chunks(gate, NF), chunks(up, NF)], axis=2),
        "w_down": down.T.reshape(NF, P, DM),
        "lam": a["L0_attn_Lambda_ri"], "p_ri": a["L0_attn_p_ri"], "q_ri": a["L0_attn_q_ri"],
        "ct": a["L0_attn_Ct_ri"].reshape(NS, 2), "vc": a["L0_attn_Vc_ri"].transpose(0, 2, 1).reshape(NS, 2 * NS),
        "bp": a["L0_attn_Bp"].reshape(NS), "d_skip": a["L0_attn_D"], "log_step": a["L0_attn_log_step"],
        "w_comb": comb.T.reshape(KD, P, WC), "b_base": a["L1_ffn_b_base"], "b_thr": a["L1_ffn_b_thr"],
        "w_expb": a["L1_ffn_B_w"].transpose(0, 2, 1).reshape(ER, DM),
        "w_qk": np.stack([chunks(wq, HEADS), chunks(wk, HEADS)], axis=2),
        "w_v": wv.reshape(KD, P, NG, GH * DH).transpose(2, 0, 1, 3),
        "w_o": a["L1_attn_wo"].reshape(HEADS, DH, DM),
    }


ORDER = ["x", "w_gu", "w_down", "lam", "p_ri", "q_ri", "ct", "vc", "bp", "d_skip", "log_step", "om_rows", "om_cols",
         "tables", "w_comb", "b_base", "b_thr", "w_expb", "w_qk", "w_v", "w_o", "identity", "mask"]


def kernel(**inputs):
    import numpy as np
    import concourse.bacc as bacc
    from concourse.bass_utils import run_bass_kernel_spmd

    nc = bacc.Bacc("TRN2", target_bir_lowering=False, num_devices=1)
    data = {**layout({k: np.asarray(v) for k, v in inputs.items()}), **constants()}
    arrays, args = {}, []
    for name in ORDER:
        arrays[f"in_{name}"] = np.ascontiguousarray(data[name])
        args.append(nc.dram_tensor(f"in_{name}", arrays[f"in_{name}"].shape, F32, kind="ExternalInput").ap())
    out = nc.dram_tensor("out", (TOK, DM), F32, kind="ExternalOutput").ap()
    build(nc, *args, out)
    r = run_bass_kernel_spmd(nc, [arrays], core_ids=[0])
    return r.results[0]["out"].reshape(BATCH, SEQ, DM)
```
